# Optimizing a Trainium2 kernel written in Bass

```python
import numpy as np
import jax
import jax.numpy as jnp

def _softmax(x, axis=-1):
    return jax.nn.softmax(x, axis=axis)

def _gelu(x):
    return jax.nn.gelu(x, approximate=True)

def _silu(x):
    return jax.nn.silu(x)

def _sigmoid(x):
    return jax.nn.sigmoid(x)

def _layernorm(x, axis=-1, eps=1e-05):
    m = jnp.mean(x, axis=axis, keepdims=True)
    v = jnp.var(x, axis=axis, keepdims=True)
    return (x - m) / jnp.sqrt(v + eps)

def _scatter_add(tgt, idx, src, axis=0):
    return tgt.at[idx].add(src)

def _segment_sum(src, seg, n):
    return jax.ops.segment_sum(src, seg, n)
kernel_name = 'mk_vit_tower_postln_d2_tok_img768_r4_66b065'

def setup_inputs(seed: int=0):
    np.random.seed(seed)
    _w = jnp.asarray

    def _rec_inputs():
        import jax
        import jax.numpy as jnp
        _rk = jax.random.key(seed)
        x = -0.000222058 + 0.999998 * jax.random.normal(jax.random.fold_in(_rk, 1), (32, 3, 84, 84), jnp.float32)
        return x
    x = _rec_inputs()

    def _L0_tok_setup():
        import jax, jax.numpy as jnp
        import numpy as np
        from jax import lax
        HIDDEN = 192
        C_IN = 3
        PATCH = 16
        SIDE = 32
        NUM_PATCHES = SIDE * SIDE

        def _position_ids(nb_h, nb_w):
            boundaries = np.arange(1.0 / SIDE, 1.0, 1.0 / SIDE, dtype=np.float32)
            frac_h = np.arange(0.0, 1.0 - 1e-06, 1.0 / nb_h, dtype=np.float32)
            frac_w = np.arange(0.0, 1.0 - 1e-06, 1.0 / nb_w, dtype=np.float32)
            bh = np.searchsorted(boundaries, frac_h, side='right')
            bw = np.searchsorted(boundaries, frac_w, side='right')
            return jnp.asarray((bh[:, None] * SIDE + bw).reshape(-1), dtype=jnp.int32)
        key = jax.random.key(seed)
        k1, k2, k3 = jax.random.split(key, 3)
        pixel_values = jax.random.normal(k1, (32, C_IN, 128, 128), dtype=jnp.float32)
        conv_w = jax.random.normal(k2, (HIDDEN, C_IN, PATCH, PATCH), dtype=jnp.float32) * 0.02
        conv_b = jnp.zeros((HIDDEN,), dtype=jnp.float32)
        pos_table = jax.random.normal(k3, (NUM_PATCHES, HIDDEN), dtype=jnp.float32) * 0.02
        return {'pixel_values': pixel_values, 'conv_w': conv_w, 'conv_b': conv_b, 'pos_table': pos_table}
    _L0_tok_all = _L0_tok_setup()
    _L0_tok_in = {k: v for k, v in _L0_tok_all.items() if k in ('conv_w', 'conv_b', 'pos_table')}
    del _L0_tok_all

    def _L0_attn_setup():
        import jax, jax.numpy as jnp
        import numpy as np
        B, N, C = (8, 1024, 192)
        H = 8
        G = 2
        HD = C // H
        HG = H // G
        SCALE = HD ** (-0.5)
        key = jax.random.key(seed)
        k0, k1, k2, k3 = jax.random.split(key, 4)
        std = 0.02
        return {'x': jax.random.normal(k0, (B, N, C), dtype=jnp.float32), 'Wq': jax.random.normal(k1, (C, HD * G), dtype=jnp.float32) * std, 'Wkv': jax.random.normal(k2, (C, 2 * C), dtype=jnp.float32) * std, 'Wproj': jax.random.normal(k3, (C, C), dtype=jnp.float32) * std, 'bproj': jnp.zeros((C,), dtype=jnp.float32)}
    _L0_attn_all = _L0_attn_setup()
    _L0_attn_in = {k: v for k, v in _L0_attn_all.items() if k in ('Wq', 'Wkv', 'Wproj', 'bproj')}
    del _L0_attn_all

    def _L0_ffn_setup():
        import jax, jax.numpy as jnp
        import numpy as np
        TOP_K = 2
        key = jax.random.key(seed)
        ks = jax.random.split(key, 5)
        B, T, C, H, E = (4, 256, 192, 768, 8)
        x = jax.random.normal(ks[0], (B, T, C), dtype=jnp.float32)
        Wg = jax.random.normal(ks[1], (C, E), dtype=jnp.float32) * 0.02
        W1 = jax.random.normal(ks[2], (E, C, H), dtype=jnp.float32) * (1.0 / np.sqrt(C))
        b1 = jnp.zeros((E, H), dtype=jnp.float32)
        W2 = jax.random.normal(ks[3], (E, H, C), dtype=jnp.float32) * (1.0 / np.sqrt(H))
        b2 = jnp.zeros((E, C), dtype=jnp.float32)
        return {'x': x, 'Wg': Wg, 'W1': W1, 'b1': b1, 'W2': W2, 'b2': b2}
    _L0_ffn_all = _L0_ffn_setup()
    _L0_ffn_in = {k: v for k, v in _L0_ffn_all.items() if k in ('Wg', 'W1', 'b1', 'W2', 'b2')}
    del _L0_ffn_all

    def _L1_attn_setup():
        import jax, jax.numpy as jnp
        import numpy as np
        H = 12

        def _attn(q, k, v):
            D = q.shape[-1]
            scores = jnp.einsum('bhnd,bhmd->bhnm', q, k) / jnp.sqrt(jnp.asarray(D, q.dtype))
            p = jax.nn.softmax(scores, axis=-1)
            return jnp.einsum('bhnm,bhmd->bhnd', p, v)
        key = jax.random.key(seed)
        ks = jax.random.split(key, 5)
        B, N, C = (2, 512, 192)
        s = 0.02
        return {'x': jax.random.normal(ks[0], (B, N, C), jnp.float32), 'Wq': jax.random.normal(ks[1], (C, 2 * C), jnp.float32) * s, 'Wk': jax.random.normal(ks[2], (C, 2 * C), jnp.float32) * s, 'Wv': jax.random.normal(ks[3], (C, C), jnp.float32) * s, 'lambda_p': jnp.zeros((H, 1, 1), jnp.float32), 'Wo': jax.random.normal(ks[4], (C, C), jnp.float32) * s, 'bo': jnp.zeros((C,), jnp.float32)}
    _L1_attn_all = _L1_attn_setup()
    _L1_attn_in = {k: v for k, v in _L1_attn_all.items() if k in ('Wq', 'Wk', 'Wv', 'lambda_p', 'Wo', 'bo')}
    del _L1_attn_all

    def _L1_ffn_setup():
        import jax, jax.numpy as jnp
        import numpy as np
        DIM = 192
        NUM_HEADS = 12
        HEAD_DIM = DIM // NUM_HEADS
        SCALE = HEAD_DIM ** (-0.5)
        NUM_EXPERTS = 8
        RANK = 16
        ALPHA = 32
        TOPK = 2
        SCALING = ALPHA / RANK
        B, S = (8, 256)
        key = jax.random.key(seed)
        ks = jax.random.split(key, 12)
        d, e, r = (DIM, NUM_EXPERTS, RANK)
        inp = {'x': jax.random.normal(ks[0], (B, S, d), jnp.float32), 'Wg': jax.random.normal(ks[1], (e, d), jnp.float32) * 0.02, 'bg': jax.random.normal(ks[2], (e,), jnp.float32) * 0.02, 'Wqkv': jax.random.normal(ks[3], (3 * d, d), jnp.float32) * 0.02, 'bqkv': jax.random.normal(ks[4], (3 * d,), jnp.float32) * 0.02, 'Wproj': jax.random.normal(ks[5], (d, d), jnp.float32) * 0.02, 'bproj': jax.random.normal(ks[6], (d,), jnp.float32) * 0.02, 'A': jax.random.normal(ks[7], (e, r, d), jnp.float32) * 0.05, 'ba': jax.random.normal(ks[8], (e, r), jnp.float32) * 0.02, 'Bm': jax.random.normal(ks[9], (e, 3 * d, r), jnp.float32) * 0.05, 'bb': jax.random.normal(ks[10], (e, 3 * d), jnp.float32) * 0.02}
        return inp
    _L1_ffn_all = _L1_ffn_setup()
    _L1_ffn_in = {k: v for k, v in _L1_ffn_all.items() if k in ('Wg', 'bg', 'Wqkv', 'bqkv', 'Wproj', 'bproj', 'A', 'ba', 'Bm', 'bb')}
    del _L1_ffn_all
    return {'x': x, 'L0_tok_conv_w': _L0_tok_in['conv_w'], 'L0_tok_conv_b': _L0_tok_in['conv_b'], 'L0_tok_pos_table': _L0_tok_in['pos_table'], 'L0_attn_Wq': _L0_attn_in['Wq'], 'L0_attn_Wkv': _L0_attn_in['Wkv'], 'L0_attn_Wproj': _L0_attn_in['Wproj'], 'L0_attn_bproj': _L0_attn_in['bproj'], 'L0_ffn_Wg': _L0_ffn_in['Wg'], 'L0_ffn_W1': _L0_ffn_in['W1'], 'L0_ffn_b1': _L0_ffn_in['b1'], 'L0_ffn_W2': _L0_ffn_in['W2'], 'L0_ffn_b2': _L0_ffn_in['b2'], 'L1_attn_Wq': _L1_attn_in['Wq'], 'L1_attn_Wk': _L1_attn_in['Wk'], 'L1_attn_Wv': _L1_attn_in['Wv'], 'L1_attn_lambda_p': _L1_attn_in['lambda_p'], 'L1_attn_Wo': _L1_attn_in['Wo'], 'L1_attn_bo': _L1_attn_in['bo'], 'L1_ffn_Wg': _L1_ffn_in['Wg'], 'L1_ffn_bg': _L1_ffn_in['bg'], 'L1_ffn_Wqkv': _L1_ffn_in['Wqkv'], 'L1_ffn_bqkv': _L1_ffn_in['bqkv'], 'L1_ffn_Wproj': _L1_ffn_in['Wproj'], 'L1_ffn_bproj': _L1_ffn_in['bproj'], 'L1_ffn_A': _L1_ffn_in['A'], 'L1_ffn_ba': _L1_ffn_in['ba'], 'L1_ffn_Bm': _L1_ffn_in['Bm'], 'L1_ffn_bb': _L1_ffn_in['bb']}

def reference(x, L0_tok_conv_w, L0_tok_conv_b, L0_tok_pos_table, L0_attn_Wq, L0_attn_Wkv, L0_attn_Wproj, L0_attn_bproj, L0_ffn_Wg, L0_ffn_W1, L0_ffn_b1, L0_ffn_W2, L0_ffn_b2, L1_attn_Wq, L1_attn_Wk, L1_attn_Wv, L1_attn_lambda_p, L1_attn_Wo, L1_attn_bo, L1_ffn_Wg, L1_ffn_bg, L1_ffn_Wqkv, L1_ffn_bqkv, L1_ffn_Wproj, L1_ffn_bproj, L1_ffn_A, L1_ffn_ba, L1_ffn_Bm, L1_ffn_bb):
    import jax
    import jax.numpy as jnp

    def _L0_tok_ref(pixel_values, conv_w, conv_b, pos_table):
        import jax, jax.numpy as jnp
        import numpy as np
        from jax import lax
        HIDDEN = 192
        C_IN = 3
        PATCH = 16
        SIDE = 32
        NUM_PATCHES = SIDE * SIDE

        def _position_ids(nb_h, nb_w):
            boundaries = np.arange(1.0 / SIDE, 1.0, 1.0 / SIDE, dtype=np.float32)
            frac_h = np.arange(0.0, 1.0 - 1e-06, 1.0 / nb_h, dtype=np.float32)
            frac_w = np.arange(0.0, 1.0 - 1e-06, 1.0 / nb_w, dtype=np.float32)
            bh = np.searchsorted(boundaries, frac_h, side='right')
            bw = np.searchsorted(boundaries, frac_w, side='right')
            return jnp.asarray((bh[:, None] * SIDE + bw).reshape(-1), dtype=jnp.int32)
        B, _, H, W = pixel_values.shape
        nb_h, nb_w = (H // PATCH, W // PATCH)
        patches = lax.conv_general_dilated(pixel_values, conv_w, window_strides=(PATCH, PATCH), padding='VALID', dimension_numbers=('NCHW', 'OIHW', 'NCHW'))
        patches = patches + conv_b[None, :, None, None]
        embeddings = patches.reshape(B, HIDDEN, nb_h * nb_w).transpose(0, 2, 1)
        pos_ids = _position_ids(nb_h, nb_w)
        pos_emb = pos_table[pos_ids]
        return embeddings + pos_emb[None, :, :]

    def _L0_attn_ref(x, Wq, Wkv, Wproj, bproj):
        import jax, jax.numpy as jnp
        import numpy as np
        B, N, C = (8, 1024, 192)
        H = 8
        G = 2
        HD = C // H
        HG = H // G
        SCALE = HD ** (-0.5)
        b, n, c = x.shape
        q = (x @ Wq).reshape(b, 1, n, G, HD).transpose(0, 3, 1, 2, 4)
        kv = (x @ Wkv).reshape(b, n, 2, G, HG, HD).transpose(2, 0, 3, 4, 1, 5)
        k = kv[0] * SCALE
        v = kv[1]
        attn = jnp.einsum('bghnd,bghne->bghde', k.astype(jnp.float32), v.astype(jnp.float32))
        attn = jax.nn.softmax(attn, axis=-1).astype(x.dtype)
        qs = q[:, :, 0]
        out = jnp.einsum('bghde,bgne->bghnd', attn, qs)
        out = out.transpose(0, 2, 1, 3, 4).reshape(b, n, c)
        return out @ Wproj + bproj

    def _L0_ffn_ref(x, Wg, W1, b1, W2, b2):
        import jax, jax.numpy as jnp
        import numpy as np
        TOP_K = 2
        E = Wg.shape[-1]
        logits = jnp.einsum('btc,ce->bte', x, Wg)
        probs = jax.nn.softmax(logits, axis=-1)
        top_vals, top_idx = jax.lax.top_k(probs, TOP_K)
        gates = (jax.nn.one_hot(top_idx, E, dtype=probs.dtype) * top_vals[..., None]).sum(-2)
        h = jax.nn.relu(jnp.einsum('btc,ech->bteh', x, W1) + b1)
        y = jnp.einsum('bteh,ehc->btec', h, W2) + b2
        out = jnp.einsum('bte,btec->btc', gates, y)
        return out

    def _L1_attn_ref(x, Wq, Wk, Wv, lambda_p, Wo, bo):
        import jax, jax.numpy as jnp
        import numpy as np
        H = 12

        def _attn(q, k, v):
            D = q.shape[-1]
            scores = jnp.einsum('bhnd,bhmd->bhnm', q, k) / jnp.sqrt(jnp.asarray(D, q.dtype))
            p = jax.nn.softmax(scores, axis=-1)
            return jnp.einsum('bhnm,bhmd->bhnd', p, v)
        B, N, C = x.shape
        D = C // H
        q = (x @ Wq).reshape(B, N, 2, H, D).transpose(2, 0, 3, 1, 4)
        k = (x @ Wk).reshape(B, N, 2, H, D).transpose(2, 0, 3, 1, 4)
        v = (x @ Wv).reshape(B, N, H, D).transpose(0, 2, 1, 3)
        out1 = _attn(q[0], k[0], v)
        out2 = _attn(q[1], k[1], v)
        lam = jnp.exp(lambda_p)
        out = out1 - lam * out2
        out = out.transpose(0, 2, 1, 3).reshape(B, N, C)
        return out @ Wo + bo

    def _L1_ffn_ref(x, Wg, bg, Wqkv, bqkv, Wproj, bproj, A, ba, Bm, bb):
        import jax, jax.numpy as jnp
        import numpy as np
        DIM = 192
        NUM_HEADS = 12
        HEAD_DIM = DIM // NUM_HEADS
        SCALE = HEAD_DIM ** (-0.5)
        NUM_EXPERTS = 8
        RANK = 16
        ALPHA = 32
        TOPK = 2
        SCALING = ALPHA / RANK
        B, S = (8, 256)
        b, s, d = x.shape
        t = b * s
        xf = x.reshape(t, d)
        probs = jax.nn.softmax(xf @ Wg.T + bg, axis=-1)
        top_w, top_idx = jax.lax.top_k(probs, TOPK)
        combine = jnp.zeros((t, NUM_EXPERTS), x.dtype).at[jnp.arange(t)[:, None], top_idx].add(top_w)
        h = jnp.einsum('td,erd->ter', xf, A) + ba
        hw = h * combine[:, :, None]
        delta = jnp.einsum('ter,eor->to', hw, Bm) + combine @ bb
        delta = delta * SCALING
        qkv = xf @ Wqkv.T + bqkv + delta
        qkv = qkv.reshape(b, s, 3, NUM_HEADS, HEAD_DIM)
        qkv = jnp.transpose(qkv, (2, 0, 3, 1, 4))
        q, k, v = (qkv[0], qkv[1], qkv[2])
        attn = jax.nn.softmax(jnp.einsum('bhsd,bhtd->bhst', q, k) * SCALE, axis=-1)
        out = jnp.einsum('bhst,bhtd->bhsd', attn, v)
        out = jnp.transpose(out, (0, 2, 1, 3)).reshape(b, s, d)
        return out @ Wproj.T + bproj
    h = _L0_tok_ref(x, L0_tok_conv_w, L0_tok_conv_b, L0_tok_pos_table)
    h = _layernorm(h + _L0_attn_ref(h, L0_attn_Wq, L0_attn_Wkv, L0_attn_Wproj, L0_attn_bproj), axis=-1)
    h = _layernorm(h + _L0_ffn_ref(h, L0_ffn_Wg, L0_ffn_W1, L0_ffn_b1, L0_ffn_W2, L0_ffn_b2), axis=-1)
    h = _layernorm(h + _L1_attn_ref(h, L1_attn_Wq, L1_attn_Wk, L1_attn_Wv, L1_attn_lambda_p, L1_attn_Wo, L1_attn_bo), axis=-1)
    h = _layernorm(h + _L1_ffn_ref(h, L1_ffn_Wg, L1_ffn_bg, L1_ffn_Wqkv, L1_ffn_bqkv, L1_ffn_Wproj, L1_ffn_bproj, L1_ffn_A, L1_ffn_ba, L1_ffn_Bm, L1_ffn_bb), axis=-1)
    return h

_drawn_inputs = setup_inputs


def setup_inputs(seed=0):
    import zlib

    import numpy as np

    out = dict(_drawn_inputs(seed))
    spreads = {'L0_tok_conv_b': (0.0, 0.1),
     'L0_attn_bproj': (0.0, 0.1),
     'L0_ffn_b1': (0.0, 0.473),
     'L0_ffn_b2': (0.0, 0.332),
     'L1_attn_lambda_p': (0.0, 0.8),
     'L1_attn_bo': (0.0, 0.1)}
    factors = {'L0_attn_Wq': 2.749,
     'L0_attn_Wkv': 8.0,
     'L0_attn_Wproj': 2.845,
     'L1_attn_Wq': 8.0,
     'L1_attn_Wk': 8.0,
     'L1_attn_Wv': 8.0,
     'L1_attn_Wo': 8.0,
     'L1_ffn_Wg': 8.0,
     'L1_ffn_bg': 8.0,
     'L1_ffn_bqkv': 8.0,
     'L1_ffn_bproj': 10.82,
     'L1_ffn_A': 8.0,
     'L1_ffn_ba': 8.0,
     'L1_ffn_Bm': 8.0,
     'L1_ffn_bb': 8.0}
    for name, (base, spread) in spreads.items():
        noise = np.random.default_rng([zlib.crc32(name.encode()), seed]).standard_normal(out[name].shape)
        drawn = base * np.exp(spread * noise) if base else spread * noise
        out[name] = jnp.asarray(drawn.astype(out[name].dtype))
    for name, factor in factors.items():
        out[name] = (out[name] * factor).astype(out[name].dtype)
    return out
```

```python
from contextlib import ExitStack

import concourse.bass as bass
from concourse import mybir

F32 = mybir.dt.float32
F32R = mybir.dt.float32r
ALU = mybir.AluOpType
ACT = mybir.ActivationFunctionType
AX = mybir.AxisListType

B, CIN, IMG, PATCH = 32, 3, 84, 16
SIDE = 32
NB = IMG // PATCH
N = NB * NB
T = B * N
C = 192
CA, CB = 128, C - 128
KP = CIN * PATCH * PATCH
KCH = KP // 128
TT = (T + 127) // 128
TP = TT * 128
IG = 4
G = B // IG
GT = IG * N
HALF = T // 2
EPS = 1e-5
E, HID = 8, 768
HC = HID // 128
NCH = E * HC
H0, D0 = 8, 24
HG0 = H0 // 2
CH = HG0 * D0
H1, D1 = 12, 16
HQ = 4
R = 16
ADAPT = 2.0
HBUF = 3


def rows(t):
    return min(128, T - 128 * t)


def view(ap, dims):
    return bass.AP(tensor=ap.tensor, offset=ap.offset, ap=[list(ap.ap[0])] + [list(d) for d in dims])


def build(nc, io):
    with ExitStack() as ctx:
        def sb(name, shape, dt=F32, scope=ctx):
            return scope.enter_context(nc.sbuf_tensor(name, shape, dt))

        def sem(name):
            return ctx.enter_context(nc.semaphore(name))

        ps = ctx.enter_context(nc.psum_tensor("ps", [128, 8, 512], F32))

        ident = sb("ident", [128, 128])
        head_mask0 = sb("head_mask0", [CH, CH])
        head_mask1 = sb("head_mask1", [128, HQ])
        expert_rows = sb("expert_rows", [104, 128])
        iota8 = sb("iota8", [128, E])
        posb = sb("posb", [N + 1, C])
        wq0a, wq0b = sb("wq0a", [CA, 256]), sb("wq0b", [CB, 256])
        wkv0a, wkv0b = sb("wkv0a", [CA, 2 * C]), sb("wkv0b", [CB, 2 * C])
        wp0 = sb("wp0", [128, 2, C])
        bp0 = sb("bp0", [CB + 1, C])
        wg0a, wg0b = sb("wg0a", [CA, E]), sb("wg0b", [CB, E])
        b1c = sb("b1c", [128, NCH])
        b2r = sb("b2r", [E, C])
        wq1a, wq1b = sb("wq1a", [CA, 2 * C]), sb("wq1b", [CB, 2 * C])
        wk1a, wk1b = sb("wk1a", [CA, 2 * C]), sb("wk1b", [CB, 2 * C])
        wv1a, wv1b = sb("wv1a", [CA, C]), sb("wv1b", [CB, C])
        wo1a, wo1b = sb("wo1a", [CA, C]), sb("wo1b", [CB + 1, C])
        lam_raw = sb("lam_raw", [128, H1])
        lam_exp = sb("lam_exp", [128, H1])
        lam = sb("lam", [128, 2, 3, HQ])
        wg2a, wg2b = sb("wg2a", [CA, E]), sb("wg2b", [CB + 1, E])
        wa2a, wa2b = sb("wa2a", [CA, 128]), sb("wa2b", [CB + 1, 128])
        wqkva, wqkvb = sb("wqkva", [CA, 3 * C]), sb("wqkvb", [104, 3 * C])
        wbm = sb("wbm", [128, 3 * C])
        wp2a, wp2b = sb("wp2a", [CA, C]), sb("wp2b", [CB + 1, C])
        neg_half = sb("neg_half", [128, TT])

        x_tok = sb("x_tok", [128, TT, C])
        h_tok = sb("h_tok", [128, TT, C])
        stats = sb("stats", [128, TT, 6])
        mv = sb("mv", [128, TT, 2])
        veps = sb("veps", [128, TT])
        rstd = sb("rstd", [128, TT])
        xa = sb("xa", [CA, TP])
        xb = sb("xb", [CB + 1, TP])
        xpa = sb("xpa", [CA, 32 * B])
        xpb = sb("xpb", [104, 32 * B])
        gate_w = sb("gate_w", [128, 8, TT, E])
        gate_s = sb("gate_s", [128, 6, TT])
        gates = sb("gates", [128, TT, E])
        gatesT = sb("gatesT", [E, TP])

        early = ExitStack()
        kv0 = sb("kv0", [128, G, 2 * C], scope=early)
        q0 = sb("q0", [128, 2, T], scope=early)
        st0 = sb("st0", [CH, 3, 16], scope=early)
        a0 = sb("a0", [CH, 2, 4, IG, 32], scope=early)
        o0 = sb("o0", [128, 2 * T], scope=early)
        with ExitStack() as first:
            patT = sb("patT", [128, KCH, T], scope=first)
            wconv = sb("wconv", [128, KCH, C], scope=first)
            sel = sb("sel", [N + 1, T], scope=first)
        m0 = sb("m0", [CH, 16, CH], scope=early)
        s0 = sb("s0", [CH, 2, 16, D0], scope=early)
        e0 = sb("e0", [CH, 2, 16, D0], scope=early)
        a0T = sb("a0T", [128, 16, HG0, 32], scope=early)
        early.close()
        late = ExitStack()
        v_bd = sb("v_bd", [128, B, 3, 64], scope=late)
        qT = sb("qT", [128, 3, T + 8], scope=late)
        s1 = sb("s1", [128, 2, 24, N], scope=late)
        e1 = sb("e1", [128, 2, 24, N], scope=late)
        st1 = sb("st1", [128, 2, 4, 24], scope=late)
        p1 = sb("p1", [128, 2, 3, HQ, 32], scope=late)
        p1T = sb("p1T", [128, 2, 3, 128], scope=late)
        oa = sb("oa", [CA, T], scope=late)
        ob = sb("ob", [CB + 1, T], scope=late)
        ce = sb("ce", [128, T], scope=late)
        hwT = sb("hwT", [128, 32 * B], scope=late)
        late.close()
        sb("region_one", [128, 16120])

        ffn = ExitStack()
        w1_raw = sb("w1_raw", [128, 2, HID], scope=ffn)
        w2_raw = sb("w2_raw", [128, HC, C], scope=ffn)
        w1_hi = sb("w1_hi", [128, 2, HID], F32R, scope=ffn)
        w1_lo = sb("w1_lo", [128, 2, HID], F32R, scope=ffn)
        w1_tail = sb("w1_tail", [128, 2, HID], F32R, scope=ffn)
        w2_hi = sb("w2_hi", [128, 2, HC, C], F32R, scope=ffn)
        w2_lo = sb("w2_lo", [128, 2, HC, C], F32R, scope=ffn)
        x_hi = sb("x_hi", [CA, T], F32R, scope=ffn)
        x_lo = sb("x_lo", [CA, T], F32R, scope=ffn)
        xt_hi = sb("xt_hi", [128, T], F32R, scope=ffn)
        xt_lo = sb("xt_lo", [CB, T], F32R, scope=ffn)
        hid = sb("hid", [128, 2, T], scope=ffn)
        hid_hi = sb("hid_hi", [128, HBUF, T], F32R, scope=ffn)
        hid_lo = sb("hid_lo", [128, HBUF, T], F32R, scope=ffn)
        ffn.close()
        k_bd = sb("k_bd", [128, 3, HQ, T])

        patch_in = [sem(f"patch_in{k}") for k in range(KCH)]
        const_in = sem("const_in")
        w0_in = sem("w0_in")
        wlate_in = sem("wlate_in")
        w1_in, w2_in = sem("w1_in"), sem("w2_in")
        out_sent = sem("out_sent")
        pool_set = sem("pool_set")
        vbd_zero = sem("vbd_zero")
        conv_done = sem("conv_done")
        x0_act, x0_dve = sem("x0_act"), sem("x0_dve")
        xT_ready = sem("xT_ready")
        xa_done, xb_done = sem("xa_done"), sem("xb_done")
        kv_ready = sem("kv_ready")
        kv_act, kv_dve = sem("kv_act"), sem("kv_dve")
        q0_ready = sem("q0_ready")
        q0_act, q0_dve = sem("q0_act"), sem("q0_dve")
        s0_ready, s0_masked = sem("s0_ready"), sem("s0_masked")
        s0_shifted, s0_exp, a0_ready = sem("s0_shifted"), sem("s0_exp"), sem("a0_ready")
        a0T_ready, a0T_done = sem("a0T_ready"), sem("a0T_done")
        o0_ready, o0_act, o0_dve = sem("o0_ready"), sem("o0_act"), sem("o0_dve")
        a0T_zero = sem("a0T_zero")
        proj_ready = sem("proj_ready")
        summed = sem("summed")
        veps_ready, rstd_ready = sem("veps_ready"), sem("rstd_ready")
        x_ready = sem("x_ready")
        dve_chain = sem("dve_chain")
        x_split = sem("x_split")
        logits_ready, logits_read = sem("logits_ready"), sem("logits_read")
        shift_ready, gexp_ready, gates_ready = sem("shift_ready"), sem("gexp_ready"), sem("gates_ready")
        gT_ready, gT_done = sem("gT_ready"), sem("gT_done")
        w1_cast, w2_cast = sem("w1_cast"), sem("w2_cast")
        w1_split, w2_split = sem("w1_split"), sem("w2_split")
        z_ready, hid_ready, hid_cast, hid_split = sem("z_ready"), sem("hid_ready"), sem("hid_cast"), sem("hid_split")
        y_done, y_read = sem("y_done"), sem("y_read")
        lam_ready = sem("lam_ready")
        v_ready, v_act, v_dve = sem("v_ready"), sem("v_act"), sem("v_dve")
        qk_ready, qk_act, qk_dve = sem("qk_ready"), sem("qk_act"), sem("qk_dve")
        s1_ready, s1_read, s1_shifted, s1_exp = sem("s1_ready"), sem("s1_read"), sem("s1_shifted"), sem("s1_exp")
        p1_ready, p1T_ready, p1T_done = sem("p1_ready"), sem("p1T_ready"), sem("p1T_done")
        o1_ready, o1_done = sem("o1_ready"), sem("o1_done")
        ce_ready, ce_done, ha_ready, hw_done = sem("ce_ready"), sem("ce_done"), sem("ha_ready"), sem("hw_done")

        def wait(eng, s, value):
            if not isinstance(value, int) or value > 0:
                eng.wait_ge(s, value)

        def tok_bank(first, t):
            return ps[0:rows(t), first + t // 2, (t % 2) * C:(t % 2) * C + C]

        def spread(dst, src, j):
            whole = 512 // N
            cut = 512 - whole * N
            if j == 0:
                return [(view(dst[:, 0:1], [[32, whole], [1, N]]), view(src[:, 0:1], [[N, whole], [1, N]])),
                        (dst[:, 32 * whole:32 * whole + cut], src[:, whole * N:512])]
            rest = N - cut
            return [(dst[:, 32 * whole + cut:32 * whole + N], src[:, 0:rest]),
                    (view(dst[:, 32 * (whole + 1):32 * (whole + 1) + 1], [[32, B - whole - 1], [1, N]]),
                     view(src[:, rest:rest + 1], [[N, B - whole - 1], [1, N]]))]

        def reorder(h):
            pairs = []
            for a in range(2):
                first = (2 * h + a) * N
                for r in range(4):
                    n0 = (r - first) % 4
                    count = len(range(n0, N, 4))
                    src = ps[32 * h:32 * h + 32, 0, a * G * N + n0:a * G * N + n0 + 1]
                    dst = o0[32 * r:32 * r + 32, (first + n0) // 4:(first + n0) // 4 + 1]
                    pairs.append((view(dst, [[2 * N, IG], [2 * GT, G], [1, count]]),
                                  view(src, [[512, IG], [N, G], [4, count]])))
            return pairs

        block = ctx.enter_context(nc.Block())

        @block.sync
        def _(sp):
            def load(dst, src, s):
                sp.dma_start(dst, src).then_inc(s, 16)
                return 16

            for k in range(KCH):
                load(patT[:, k, :], io["patT"][128 * k:128 * k + 128, :], patch_in[k])
                load(wconv[:, k, :], io["wconv"][128 * k:128 * k + 128, :], patch_in[k])
                if k == 0:
                    load(sel[:, :], io["sel"], const_in)
                    pos = io["pos"].rearrange("(y x) c -> y x c", x=SIDE)
                    for y, py in enumerate(POS):
                        for x0, x1, nx in ((0, POS[0], 3), (3, POS[3], 2)):
                            load(posb[NB * y + x0:NB * y + x0 + nx, :],
                                 pos[py, x1:x1 + 6 * (nx - 1) + 1:6, :], const_in)
                    load(posb[N:N + 1, :], io["conv_b"], const_in)
                    load(ident[:, :], io["ident"], const_in)
                    load(head_mask0[:, :], io["mask0"], const_in)
                    load(head_mask1[:, :], io["mask1"], const_in)
                    load(expert_rows[96:104, :], io["expert_rows"], const_in)
                    load(iota8[:, :], io["iota8"], const_in)

            def split_rows(a, b, src, s, cols=None):
                n = src.shape[1]
                return load(a[:, 0:n], src[0:CA, :], s) + load(b[0:CB, 0:n], src[CA:C, :], s)

            split_rows(wkv0a, wkv0b, io["wkv0"], w0_in)
            split_rows(wq0a, wq0b, io["wq0"], w0_in)
            load(wp0[:, :, :].rearrange("p a c -> p (a c)"), io["wp0"], w0_in)
            load(bp0[CB:CB + 1, :], io["bp0"], w0_in)
            split_rows(wg0a, wg0b, io["wg0"], w0_in)
            load(b1c[:, :], io["b1c"], w0_in)
            load(b2r[:, :], io["b2"], w0_in)

            def load_expert(e):
                wait(sp, w1_cast, 2 * e)
                wait(sp, w1_split, 2 * e)
                load(w1_raw[:, 0, :], io["w1"][e, 0:CA, :], w1_in)
                load(w1_raw[0:CB, 1, :], io["w1"][e, CA:C, :], w1_in)
                load(w1_raw[CB:128, 1, :], io["w1"][e, CA:C, :], w1_in)
                wait(sp, w2_cast, e)
                wait(sp, w2_split, e)
                load(w2_raw[:, :, :], io["w2"][e].rearrange("(k p) c -> p k c", p=128), w2_in)

            load_expert(0)
            split_rows(wq1a, wq1b, io["wq1"], wlate_in)
            split_rows(wk1a, wk1b, io["wk1"], wlate_in)
            split_rows(wv1a, wv1b, io["wv1"], wlate_in)
            split_rows(wo1a, wo1b, io["wo1"], wlate_in)
            load(wo1b[CB:CB + 1, :], io["bo1"], wlate_in)
            load(lam_raw[:, :], bass.AP(tensor=io["lam"].tensor, offset=0, ap=[[0, 128], [1, H1]]), wlate_in)
            split_rows(wg2a, wg2b, io["wg2"], wlate_in)
            load(wg2b[CB:CB + 1, :], io["bg2"], wlate_in)
            split_rows(wa2a, wa2b, io["wa2"], wlate_in)
            load(wa2b[CB:CB + 1, :], io["ba2"], wlate_in)
            sp.wait_ge(pool_set, 1)
            split_rows(wqkva, wqkvb, io["wqkv"], wlate_in)
            load(wqkvb[CB:CB + 1, :], io["bqkv"], wlate_in)
            load(wqkvb[96:104, :], io["bb2"], wlate_in)
            load(wbm[:, :], io["bm2"], wlate_in)
            split_rows(wp2a, wp2b, io["wp2"], wlate_in)
            load(wp2b[CB:CB + 1, :], io["bp2"], wlate_in)
            for e in range(1, E):
                load_expert(e)
            for t in range(TT):
                sp.wait_ge(x_ready, 3 * TT + t + 1)
                load(io["out"][128 * t:128 * t + rows(t), :], x_tok[0:rows(t), t, :], out_sent)
            sp.wait_ge(out_sent, 16 * TT)

        @block.gpsimd
        def _(pool):
            count = {}

            def fill(ap, value, s):
                pool.memset(ap, value).then_inc(s, 1)
                count[s] = count.get(s, 0) + 1
                pool.wait_ge(s, count[s])

            fill(wqkvb[CB:104, :], 0.0, pool_set)
            fill(xpa[:, :], 0.0, pool_set)
            fill(xpb[:, :], 0.0, pool_set)
            fill(xa[:, T:TP], 0.0, pool_set)
            fill(xb[0:CB, T:TP], 0.0, pool_set)
            fill(a0[:, :, :, :, D0:32], 0.0, pool_set)
            fill(mv[:, :, :], 1.0, pool_set)
            fill(neg_half[:, :], -0.5, pool_set)
            fill(xb[CB:CB + 1, :], 1.0, pool_set)
            fill(xpb[CB:CB + 1, :], 1.0, pool_set)

            def rsqrt(layer):
                for half in range(2):
                    ts = slice(0, 4) if half == 0 else slice(4, TT)
                    pool.wait_ge(veps_ready, 2 * layer + half + 1)
                    pool.tensor_tensor(rstd[:, ts], veps[:, ts], neg_half[:, ts], ALU.pow).then_inc(rstd_ready, 1)
                    pool.wait_ge(rstd_ready, 2 * layer + half + 1)

            pool.wait_ge(conv_done, TT)
            fill(a0T[:, :, :, :], 0.0, a0T_zero)
            rsqrt(0)
            pool.wait_ge(proj_ready, TT)
            fill(v_bd[:, :, :, :], 0.0, vbd_zero)
            fill(p1[:, :, :, :, N:32], 0.0, vbd_zero)
            fill(qT[:, :, T:T + 8], 0.0, vbd_zero)
            fill(ob[CB:CB + 1, :], 1.0, vbd_zero)
            fill(hwT[:, :], 0.0, vbd_zero)
            fill(lam[:, :, :, :], 1.0, vbd_zero)
            rsqrt(1)
            rsqrt(2)
            rsqrt(3)

        CONSTS = 16 * (1 + 2 * NB + 1 + 5)
        W0S = 16 * (4 + 2 + 2 + 2)
        WLATE = 16 * (8 + 1 + 1 + 3 + 3 + 2 + 2 + 1 + 3)
        PREP = 10

        @block.tensor
        def _(pe):
            def to_channels(layer, first):
                for t in range(TT):
                    n = rows(t)
                    at = 128 * (t % 4)
                    if layer:
                        pe.wait_ge(x_ready, (layer - 1) * TT + t + 1)
                    else:
                        pe.wait_ge([x0_dve, x0_act][(t // 2) % 2], t // 4 + 1)
                    pe.transpose(ps[:, first + t // 4, at:at + n], x_tok[0:n, t, 0:CA], ident[0:n, 0:n])
                    pe.transpose(ps[0:CB, first + 2 + t // 4, at:at + n], x_tok[0:n, t, CA:C], ident[0:n, 0:n]).then_inc(xT_ready, 1)

            def padded(x, g):
                return x[:, 128 * g:128 * g + 128]

            def half_of(x, n):
                return view(x[:, 32 * (B // 2) * n:32 * (B // 2) * n + 1], [[32, B // 2], [1, N]])

            for k in range(KCH):
                pe.wait_ge(patch_in[k], 32)
                for t in range(TT):
                    pe.matmul(tok_bank(0, t), patT[:, k, 128 * t:128 * t + rows(t)], wconv[:, k, :],
                              start=(k == 0 and t % 2 == 0), stop=False, skip_group_check=True)
            pe.wait_ge(const_in, CONSTS)
            for t in range(TT):
                pe.matmul(tok_bank(0, t), sel[:, 128 * t:128 * t + rows(t)], posb[:, :],
                          start=False, stop=True, skip_group_check=True).then_inc(conv_done, 1)
            to_channels(0, 4)

            pe.wait_ge(w0_in, W0S)
            pe.wait_ge(pool_set, PREP)
            for g in range(G):
                half = 1 if GT * (g + 1) <= 512 else 2
                pe.wait_ge(xa_done, half)
                pe.wait_ge(xb_done, half)
                if g >= 4:
                    pe.wait_ge([kv_act, kv_dve][g % 2], (g - 4) // 2 + 1)
                pe.matmul(ps[:, g % 4, 0:2 * C], padded(xpa, g), wkv0a[:, :], start=True, stop=False)
                pe.matmul(ps[:, g % 4, 0:2 * C], padded(xpb[0:CB], g), wkv0b[:, :], start=False, stop=True).then_inc(kv_ready, 1)
            for a in range(2):
                for n in range(2):
                    out = ps[:, 4 + 2 * a + n, 0:HALF]
                    pe.matmul(out, wq0a[:, 128 * a:128 * a + 128], half_of(xpa, n), start=True, stop=False)
                    pe.matmul(out, wq0b[:, 128 * a:128 * a + 128], half_of(xpb[0:CB], n), start=False, stop=True).then_inc(q0_ready, 1)

            def turn_a0(r):
                pe.wait_ge(a0_ready, r + 1)
                for j in range(4):
                    mm = pe.transpose(ps[:, 4 + r % 2, CH * j:CH * j + CH], a0[:, r % 2, j, :, :], ident[0:CH, 0:CH])
                mm.then_inc(a0T_ready, 1)

            pe.wait_ge(kv_act, 4)
            pe.wait_ge(kv_dve, 4)
            for r in range(4):
                wait(pe, s0_masked, r)
                for gg in range(2):
                    for a in range(2):
                        for i in range(IG):
                            kv = kv0[32 * i:32 * i + N, 2 * r + gg, :]
                            mm = pe.matmul(ps[0:CH, i, CH * (2 * gg + a):CH * (2 * gg + a) + CH],
                                           kv[:, CH * a:CH * a + CH], kv[:, C + CH * a:C + CH * a + CH], start=True, stop=True)
                mm.then_inc(s0_ready, 1)
                if r == 0:
                    pe.wait_ge(q0_act, 1)
                    pe.wait_ge(q0_dve, 1)
                if r >= 1:
                    if r >= 3:
                        pe.wait_ge(a0T_done, r - 2)
                    turn_a0(r - 1)
            pe.wait_ge(a0T_done, 2)
            turn_a0(3)
            pe.wait_ge(s0_masked, 4)
            for r in range(4):
                pe.wait_ge(a0T_done, r + 1)
                for gg in range(2):
                    for a in range(2):
                        for i in range(IG):
                            g = 2 * r + gg
                            tok = GT * g + N * i
                            mm = pe.matmul(ps[:, i, (a * G + g) * N:(a * G + g) * N + N],
                                           a0T[32 * i:32 * i + D0, 2 * g + a, :, :],
                                           q0[32 * i:32 * i + D0, a, tok:tok + N], start=True, stop=True)
            mm.then_inc(o0_ready, 1)
            pe.wait_ge(o0_act, 1)
            pe.wait_ge(o0_dve, 1)
            for t in range(TT):
                n = rows(t)
                for s in range(2):
                    pe.matmul(tok_bank(4, t), view(o0[:, 256 * t + s:256 * t + s + 1], [[2, n]]), wp0[:, s, :], start=(s == 0), stop=False)
                pe.matmul(tok_bank(4, t), xb[CB:CB + 1, 0:n], bp0[CB:CB + 1, :], start=False, stop=True).then_inc(proj_ready, 1)

            to_channels(1, 0)

            def logits(layer, wa, wb, kb):
                for t in range(TT):
                    cols = slice(128 * t, 128 * t + 128)
                    pe.matmul(ps[:, 4, E * t:E * t + E], xa[:, cols], wa[:, :], start=True, stop=False)
                    mm = pe.matmul(ps[:, 4, E * t:E * t + E], xb[0:kb, cols], wb[:, :], start=False, stop=True)
                mm.then_inc(logits_ready, 1)

            pe.wait_ge(xa_done, 4)
            pe.wait_ge(xb_done, 4)
            pe.wait_ge(summed, 4)
            logits(1, wg0a, wg0b, CB)

            def expert_in(c):
                e, k = c // HC, c % HC
                if k == 0:
                    pe.wait_ge(w1_split, 2 * (e + 1))
                if c == 0:
                    pe.wait_ge(x_split, 4)
                wait(pe, hid_ready, c - 1)
                cols = slice(128 * k, 128 * k + 128)
                j = e % 2
                for n in range(2):
                    out = ps[:, 2 * (c % 2) + n, 0:HALF]
                    tok = slice(n * HALF, (n + 1) * HALF)
                    pe.matmul(out, w1_hi[:, j, cols], x_hi[:, tok], start=True, stop=False)
                    pe.matmul(out, w1_hi[:, j, cols], x_lo[:, tok], start=False, stop=False)
                    pe.matmul(out, w1_lo[:, j, cols], x_hi[:, tok], start=False, stop=False)
                    pe.matmul(out, w1_tail[:, j, cols], xt_hi[:, tok], start=False, stop=False)
                    mm = pe.matmul(out, w1_tail[0:CB, j, cols], xt_lo[:, tok], start=False, stop=True)
                mm.then_inc(z_ready, 1)

            def expert_out(c):
                e, k = c // HC, c % HC
                j = e % 2
                pe.wait_ge(hid_split, c + 1)
                if k == 0:
                    pe.wait_ge(w2_split, e + 1)
                    wait(pe, y_read, 4 * e)
                if c == 0:
                    pe.wait_ge(logits_read, 1)
                for t in range(TT):
                    cols = slice(128 * t, 128 * t + rows(t))
                    h_hi, h_lo = hid_hi[:, c % HBUF, cols], hid_lo[:, c % HBUF, cols]
                    out = tok_bank(4, t)
                    pe.matmul(out, h_hi, w2_hi[:, j, k, :], start=(k == 0 and t % 2 == 0), stop=False, skip_group_check=True)
                    pe.matmul(out, h_hi, w2_lo[:, j, k, :], start=False, stop=False, skip_group_check=True)
                    mm = pe.matmul(out, h_lo, w2_hi[:, j, k, :], start=False, stop=(k == HC - 1), skip_group_check=True)
                mm.then_inc(y_done, 1)

            for c in range(NCH):
                expert_in(c)
                if c >= 2:
                    expert_out(c - 2)
            expert_out(NCH - 2)
            pe.wait_ge(hid_ready, NCH)
            pe.wait_ge(gates_ready, 1)

            def turn_gates():
                for t in range(TT):
                    n = rows(t)
                    mm = pe.transpose(ps[0:E, t // 4, 128 * (t % 4):128 * (t % 4) + n], gates[0:n, t, :], ident[0:n, 0:n])
                mm.then_inc(gT_ready, 1)

            turn_gates()
            expert_out(NCH - 1)
            pe.wait_ge(gT_done, 1)
            for t in range(TT):
                pe.matmul(tok_bank(0, t), gatesT[:, 128 * t:128 * t + rows(t)], b2r[:, :], start=True, stop=True).then_inc(proj_ready, 1)

            def attention(call, q_jobs, slots, v_terms):
                for g in range(G):
                    pe.wait_ge(v_free[call][0], v_free[call][1])
                    for n, (x, w) in enumerate(v_terms):
                        mm = pe.matmul(ps[:, 4 + g // 2, 256 * (g % 2):256 * (g % 2) + C], padded(x, g), w,
                                       start=(n == 0), stop=(n == len(v_terms) - 1))
                mm.then_inc(v_ready, 1)
                for n_job, (m, terms) in enumerate(q_jobs):
                    job = QK_BASE[call] + n_job
                    if n_job >= 2:
                        pe.wait_ge(qk_act, job - 1)
                        pe.wait_ge(qk_dve, job - 1)
                    for n in range(2):
                        for j, (w, x) in enumerate(terms):
                            mm = pe.matmul(ps[0:m, 2 * (n_job % 2) + n, 0:HALF], w, half_of(x, n), start=(j == 0), stop=(j == len(terms) - 1))
                    mm.then_inc(qk_ready, 1)
                pe.wait_ge(qk_act, QK_BASE[call] + len(q_jobs))
                pe.wait_ge(qk_dve, QK_BASE[call] + len(q_jobs))
                pe.wait_ge(v_act, call + 1)
                pe.wait_ge(v_dve, call + 1)

                def scores(g):
                    n = G * call + g
                    if g >= 2:
                        pe.wait_ge(s1_read, n - 1)
                    for bank, slot, row, stack in slots:
                        for i in range(IG):
                            tok = GT * g + N * i
                            keys = k_bd[row:row + 64, stack, :, tok:tok + N]
                            mm = pe.matmul(ps[32 * i:32 * i + 32, 2 * (g % 2) + bank, 4 * N * slot:4 * N * slot + 4 * N],
                                           qT[row:row + 64, stack, tok:tok + 32], keys, start=True, stop=True)
                    mm.then_inc(s1_ready, 1)

                def turn(g):
                    n = G * call + g
                    pe.wait_ge(p1_ready, n + 1)
                    if g >= 2:
                        pe.wait_ge(p1T_done, n - 1)
                    for b in range(3):
                        mm = pe.transpose(ps[:, 4 + g % 2, 128 * b:128 * b + 128], p1[:, g % 2, b, :, :], ident[:, :])
                    mm.then_inc(p1T_ready, 1)

                def times_v(g):
                    n = G * call + g
                    pe.wait_ge(p1T_done, n + 1)
                    if g >= 2:
                        pe.wait_ge(o1_done, n - 1)
                    for b in range(3):
                        for i in range(IG):
                            rr = 64 * (b % 2)
                            col = (128 if b == 2 else 0) + N * i
                            mm = pe.matmul(ps[rr:rr + 64, 6 + g % 2, col:col + N], v_bd[:, IG * g + i, b, :],
                                           p1T[:, g % 2, b, 32 * i:32 * i + N], start=True, stop=True)
                    mm.then_inc(o1_ready, 1)

                for step in range(G + 2):
                    if step < G:
                        scores(step)
                    if 1 <= step <= G:
                        turn(step - 1)
                    if step >= 2:
                        times_v(step - 2)

            def project(call, wa, wb):
                pe.wait_ge(o1_done, G * (call + 1))
                for t in range(TT):
                    cols = slice(128 * t, 128 * t + rows(t))
                    pe.matmul(tok_bank(0, t), oa[:, cols], wa[:, :], start=True, stop=False)
                    pe.matmul(tok_bank(0, t), ob[:, cols], wb[:, :], start=False, stop=True).then_inc(proj_ready, 1)

            QK_BASE = [0, 6]
            v_free = [(xb_done, 6), (xb_done, 8)]
            pe.wait_ge(y_read, 4 * E)
            to_channels(2, 4)
            pe.wait_ge(xa_done, 6)
            pe.wait_ge(xb_done, 6)
            pe.wait_ge(summed, 8)
            pe.wait_ge(wlate_in, WLATE)
            pe.wait_ge(vbd_zero, 6)
            jobs = []
            for stack in range(3):
                for wa, wb in ((wk1a, wk1b), (wq1a, wq1b)):
                    cols = slice(128 * stack, 128 * stack + 128)
                    jobs.append((128, [(wa[:, cols], xpa), (wb[:, cols], xpb[0:CB])]))
            attention(0, jobs, [(0, 0, 0, 0), (1, 0, 64, 0), (0, 1, 0, 1), (1, 1, 64, 1), (0, 2, 0, 2), (1, 2, 64, 2)],
                      [(xpa, wv1a[:, :]), (xpb[0:CB], wv1b[:, :])])
            project(0, wo1a, wo1b)

            to_channels(3, 4)
            pe.wait_ge(xa_done, 8)
            pe.wait_ge(xb_done, 8)
            pe.wait_ge(summed, 12)
            logits(3, wg2a, wg2b, CB + 1)
            for n in range(2):
                pe.matmul(ps[:, 2 + n, 0:HALF], wa2a[:, :], half_of(xpa, n), start=True, stop=False)
                pe.matmul(ps[:, 2 + n, 0:HALF], wa2b[:, :], half_of(xpb[0:CB + 1], n), start=False, stop=True).then_inc(ha_ready, 1)
            pe.wait_ge(gates_ready, 2)
            turn_gates()
            pe.wait_ge(gT_done, 2)
            for n in range(2):
                pe.matmul(ps[:, 5 + n, 0:HALF], expert_rows[96:104, :], half_of(xpb[96:104], n), start=True, stop=True).then_inc(ce_ready, 1)
            pe.wait_ge(hw_done, 2)

            def terms(c0, m):
                return [(wqkva[:, c0:c0 + m], xpa), (wqkvb[:, c0:c0 + m], xpb), (wbm[:, c0:c0 + m], hwT)]
            jobs = [(128, terms(C, 128)), (128, terms(0, 128)), (64, terms(C + 128, 64)), (64, terms(128, 64))]
            attention(1, jobs, [(0, 0, 0, 0), (1, 0, 64, 0), (0, 1, 0, 1)],
                      [(xpa, wqkva[:, 2 * C:]), (xpb, wqkvb[:, 2 * C:]), (hwT, wbm[:, 2 * C:])])
            project(1, wp2a, wp2b)

        @block.scalar
        def _(act):
            def copy(out, in_):
                return act.activation(out, in_, ACT.Copy)

            def channels_out(layer, first):
                for j in range(2):
                    act.wait_ge(xT_ready, layer * TT + (4 if j == 0 else TT))
                    n = 512 if j == 0 else T - 512
                    outs = spread(xpa, ps[:, first + j, :], j) if layer != 1 else []
                    if layer in (1, 3):
                        outs.append((xa[:, 512 * j:512 * j + n], ps[:, first + j, 0:n]))
                    for out, in_ in outs:
                        ins = copy(out, in_)
                    ins.then_inc(xa_done, 1)

            act.wait_ge(conv_done, 4)
            copy(x_tok[:, 2:4, :], ps[:, 1, 0:2 * C]).then_inc(x0_act, 1)
            act.wait_ge(conv_done, 7)
            copy(x_tok[0:rows(6), 6, :], ps[0:rows(6), 3, 0:C]).then_inc(x0_act, 1)
            act.wait_ge(pool_set, PREP)
            channels_out(0, 4)
            for g in range(0, G, 2):
                act.wait_ge(kv_ready, g + 1)
                copy(kv0[:, g, :], ps[:, g % 4, 0:2 * C]).then_inc(kv_act, 1)
            act.wait_ge(q0_ready, 2)
            copy(q0[:, 0, :], ps[:, 4:6, 0:HALF]).then_inc(q0_act, 1)

            def a0T_out(r):
                act.wait_ge(a0T_ready, r + 1)
                if r == 0:
                    act.wait_ge(a0T_zero, 1)
                blocks = ps[:, 4 + r % 2, 0:4 * CH].rearrange("p (j h d) -> p j h d", j=4, h=HG0)
                copy(a0T[:, 4 * r:4 * r + 4, :, 0:D0], blocks).then_inc(a0T_done, 1)

            for r in range(4):
                act.wait_ge(s0_shifted, r + 1)
                act.activation(e0[:, r % 2], s0[:, r % 2], ACT.Exp, scale=D0 ** -0.5).then_inc(s0_exp, 1)
                if r >= 1:
                    a0T_out(r - 1)
            a0T_out(3)
            act.wait_ge(o0_ready, 1)
            for out, in_ in reorder(2) + reorder(3):
                ins = copy(out, in_)
            ins.then_inc(o0_act, 1)

            def cast_w1(e):
                act.wait_ge(w1_in, 48 * (e + 1))
                wait(act, z_ready, HC * (e - 1))
                copy(w1_hi[:, e % 2, :], w1_raw[:, 0, :]).then_inc(w1_cast, 1)
                copy(w1_tail[:, e % 2, :], w1_raw[:, 1, :]).then_inc(w1_cast, 1)

            def cast_w2(e):
                act.wait_ge(w2_in, 16 * (e + 1))
                wait(act, y_done, HC * (e - 1))
                copy(w2_hi[:, e % 2], w2_raw[:, :, :]).then_inc(w2_cast, 1)

            cast_w1(0)
            cast_w2(0)
            channels_out(1, 0)
            def gate_exp(n):
                act.wait_ge(shift_ready, n + 1)
                act.activation(gate_w[:, 2], gate_w[:, 1], ACT.Exp).then_inc(gexp_ready, 1)
            for c in range(NCH):
                act.wait_ge(z_ready, c + 1)
                wait(act, hid_split, c - 1)
                act.activation(hid[:, c % 2, :], ps[:, 2 * (c % 2):2 * (c % 2) + 2, 0:HALF], ACT.Relu, bias=b1c[:, c:c + 1]).then_inc(hid_ready, 1)
                if c == 0:
                    gate_exp(0)
                e, k = c // HC, c % HC
                if k == 1 and e + 1 < E:
                    cast_w1(e + 1)
                if k == 3 and e + 1 < E:
                    cast_w2(e + 1)

            act.wait_ge(gT_ready, 1)
            copy(gatesT[:, 0:512], ps[0:E, 0, 0:512])
            copy(gatesT[:, 512:T], ps[0:E, 1, 0:T - 512]).then_inc(gT_done, 1)
            act.wait_ge(wlate_in, WLATE)
            act.activation(lam_exp[:, :], lam_raw[:, :], ACT.Exp).then_inc(lam_ready, 1)
            channels_out(2, 4)

            def attention(call, kinds, exps):
                act.wait_ge(v_ready, call + 1)
                for i in (2, 3):
                    for h in range(HQ):
                        src = view(ps[32 * i:32 * i + 32, 4, 16 * h:16 * h + 1], [[256, G], [64, 3], [1, 16]])
                        dst = view(v_bd[32 * h:32 * h + 32, i, 0, 16 * h:16 * h + 1], [[IG * C, G], [64, 3], [1, 16]])
                        mm = copy(dst, src)
                mm.then_inc(v_act, 1)
                for n_job, (kind, stack, m) in enumerate(kinds):
                    act.wait_ge(qk_ready, (6 if call else 0) + n_job + 1)
                    src = ps[0:m, 2 * (n_job % 2) + 1, 0:HALF]
                    if kind == "q":
                        copy(qT[0:m, stack, HALF:T], src).then_inc(qk_act, 1)
                    else:
                        for h in range(HQ):
                            mm = act.activation(k_bd[0:m, stack, h, HALF:T], src, ACT.Copy, scale=head_mask1[0:m, h:h + 1])
                        mm.then_inc(qk_act, 1)

                def p1T_out(g):
                    act.wait_ge(p1T_ready, G * call + g + 1)
                    if g >= 2 or call:
                        act.wait_ge(o1_ready, G * call + g - 1)
                    copy(p1T[:, g % 2, :, :], ps[:, 4 + g % 2, 0:384]).then_inc(p1T_done, 1)

                def o_out(g):
                    act.wait_ge(o1_ready, G * call + g + 1)
                    copy(oa[:, GT * g:GT * g + GT], ps[:, 6 + g % 2, 0:GT])
                    copy(ob[0:CB, GT * g:GT * g + GT], ps[0:CB, 6 + g % 2, 128:128 + GT]).then_inc(o1_done, 1)

                for step in range(G + 2):
                    if step < G:
                        act.wait_ge(s1_shifted, G * call + step + 1)
                        act.activation(e1[:, step % 2, 0:exps], s1[:, step % 2, 0:exps], ACT.Exp, scale=D1 ** -0.5).then_inc(s1_exp, 1)
                    if 1 <= step <= G:
                        p1T_out(step - 1)
                    if step >= 2:
                        o_out(step - 2)

            attention(0, [(x, s, 128) for s in range(3) for x in "kq"], 24)
            channels_out(3, 4)
            gate_exp(1)
            act.wait_ge(gT_ready, 2)
            for j in range(2):
                for out, in_ in spread(xpb[96:104], ps[0:E, j, :], j):
                    ins = copy(out, in_)
            ins.then_inc(gT_done, 1)
            for n in range(2):
                act.wait_ge(ce_ready, n + 1)
                copy(ce[:, n * HALF:(n + 1) * HALF], ps[:, 5 + n, 0:HALF]).then_inc(ce_done, 1)
            attention(1, [("k", 0, 128), ("q", 0, 128), ("k", 1, 64), ("q", 1, 64)], 12)

        @block.vector
        def _(dve):
            links = [0]

            def link(ins):
                links[0] += 1
                ins.then_inc(dve_chain, 1)
                dve.wait_ge(dve_chain, links[0])

            def over(ap, n):
                return bass.AP(tensor=ap.tensor, offset=ap.offset, ap=[list(d) for d in ap.ap] + [[0, n]])

            dve.wait_ge(conv_done, 2)
            dve.tensor_copy(x_tok[:, 0:2, :], ps[:, 0, 0:2 * C]).then_inc(x0_dve, 1)
            dve.wait_ge(conv_done, 6)
            dve.tensor_copy(x_tok[:, 4:6, :], ps[:, 2, 0:2 * C]).then_inc(x0_dve, 1)
            def channels_out(layer, first):
                for j in range(2):
                    dve.wait_ge(xT_ready, layer * TT + (4 if j == 0 else TT))
                    n = 512 if j == 0 else T - 512
                    outs = spread(xpb[0:CB], ps[0:CB, first + 2 + j, :], j)
                    if layer == 3:
                        outs.append((xb[0:CB, 512 * j:512 * j + n], ps[0:CB, first + 2 + j, 0:n]))
                    for out, in_ in outs:
                        ins = dve.tensor_copy(out, in_)
                    ins.then_inc(xb_done, 1)
            dve.wait_ge(pool_set, PREP)
            channels_out(0, 4)
            for g in range(1, G, 2):
                dve.wait_ge(kv_ready, g + 1)
                dve.tensor_copy(kv0[:, g, :], ps[:, g % 4, 0:2 * C]).then_inc(kv_dve, 1)
            dve.wait_ge(q0_ready, 4)
            dve.tensor_copy(q0[:, 1, :], ps[:, 6:8, 0:HALF]).then_inc(q0_dve, 1)

            def shift0(r):
                dve.wait_ge(s0_ready, r + 1)
                src = view(ps[0:CH, 0, 0:1], [[512, IG], [CH, 4], [1, CH]])
                mask = view(head_mask0[:, 0:1], [[0, IG], [0, 4], [1, CH]])
                dve.tensor_tensor(m0[:, :, :].rearrange("p (i j) e -> p i j e", i=IG), src, mask, ALU.mult).then_inc(s0_masked, 1)
                dve.wait_ge(s0_masked, r + 1)
                link(dve.tensor_reduce(s0[:, r % 2], m0[:, :, :].rearrange("p j (h e) -> p j e h", h=HG0), AX.X, ALU.add))
                link(dve.tensor_reduce(st0[:, 0, :], s0[:, r % 2], AX.X, ALU.max))
                dve.tensor_tensor(s0[:, r % 2], s0[:, r % 2], over(st0[:, 0, :], D0), ALU.subtract).then_inc(s0_shifted, 1)

            def norm0(r):
                dve.wait_ge(s0_exp, r + 1)
                link(dve.tensor_reduce(st0[:, 1, :], e0[:, r % 2], AX.X, ALU.add))
                link(dve.reciprocal(st0[:, 2, :], st0[:, 1, :]))
                wait(dve, a0T_ready, r - 1)
                for i in range(IG):
                    part = slice(4 * i, 4 * i + 4)
                    ins = dve.tensor_tensor(a0[:, r % 2, :, i, 0:D0], e0[:, r % 2, part, :], over(st0[:, 2, part], D0), ALU.mult)
                ins.then_inc(a0_ready, 1)

            for r in range(5):
                if r < 4:
                    shift0(r)
                if r >= 1:
                    norm0(r - 1)
            dve.wait_ge(o0_ready, 1)
            for out, in_ in reorder(0) + reorder(1):
                ins = dve.tensor_copy(out, in_)
            ins.then_inc(o0_dve, 1)

            def layernorm(layer, add):
                for half in range(2):
                    ts = range(0, 4) if half == 0 else range(4, TT)
                    for t in ts:
                        n = rows(t)
                        link(add(t))
                        link(dve.bn_stats(stats[0:n, t, :], h_tok[0:n, t, :]))
                        link(dve.bn_aggr(mv[0:n, t, :], stats[0:n, t, :]))
                    cut = slice(ts[0], ts[-1] + 1)
                    dve.tensor_scalar(veps[:, cut], mv[:, cut, 1], EPS, None, ALU.add).then_inc(veps_ready, 1)
                for half in range(2):
                    ts = range(0, 4) if half == 0 else range(4, TT)
                    dve.wait_ge(rstd_ready, 2 * layer + half + 1)
                    for t in ts:
                        n = rows(t)
                        dve.tensor_scalar(x_tok[0:n, t, :], h_tok[0:n, t, :], mv[0:n, t, 0:1], rstd[0:n, t:t + 1],
                                          ALU.subtract, ALU.mult).then_inc(x_ready, 1)

            def from_proj(layer, first, res):
                def add(t):
                    dve.wait_ge(proj_ready, layer * TT + min(t + 2 - t % 2, TT))
                    if t % 2 or t == TT - 1:
                        ins = dve.tensor_tensor(h_tok[0:rows(t), t, :], tok_bank(first, t), res[0:rows(t), t, :], ALU.add)
                        ins.then_inc(summed, 1)
                        dve.wait_ge(summed, 4 * layer + t // 2 + 1)
                        return dve.engine_nop()
                    return dve.tensor_tensor(h_tok[0:rows(t), t, :], tok_bank(first, t), res[0:rows(t), t, :], ALU.add)
                return add

            layernorm(0, from_proj(0, 4, x_tok))

            def split_w1(e):
                dve.wait_ge(w1_cast, 2 * (e + 1))
                j = e % 2
                dve.tensor_tensor(w1_lo[:, j, :], w1_raw[:, 0, :], w1_hi[:, j, :].bitcast(F32), ALU.subtract).then_inc(w1_split, 1)
                low = w1_tail[CB:128, j, :]
                dve.tensor_tensor(low, w1_raw[CB:128, 1, :], low.bitcast(F32), ALU.subtract).then_inc(w1_split, 1)

            def split_w2(e):
                dve.wait_ge(w2_cast, e + 1)
                j = e % 2
                dve.tensor_tensor(w2_lo[:, j], w2_raw[:, :, :], w2_hi[:, j].bitcast(F32), ALU.subtract).then_inc(w2_split, 1)

            split_w1(0)
            split_w2(0)
            for j in range(2):
                n = 512 if j == 0 else T - 512
                cols = slice(512 * j, 512 * j + n)
                dve.wait_ge(xT_ready, TT + (4 if j == 0 else TT))
                tail = ps[0:CB, 2 + j, 0:n]
                dve.tensor_copy(xb[0:CB, cols], tail).then_inc(xb_done, 1)
                dve.tensor_copy(xt_hi[CB:128, cols], tail)
                link(dve.tensor_copy(xt_hi[0:CB, cols], tail))
                dve.tensor_tensor(xt_lo[:, cols], tail, xt_hi[0:CB, cols].bitcast(F32), ALU.subtract).then_inc(x_split, 1)
            for j in range(2):
                n = 512 if j == 0 else T - 512
                cols = slice(512 * j, 512 * j + n)
                dve.wait_ge(xa_done, 3 + j)
                link(dve.tensor_copy(x_hi[:, cols], xa[:, cols]))
                dve.tensor_tensor(x_lo[:, cols], xa[:, cols], x_hi[:, cols].bitcast(F32), ALU.subtract).then_inc(x_split, 1)

            def gating(n, factor):
                W = lambda k: gate_w[:, k]
                S = lambda k: gate_s[:, k]
                grid = view(iota8[:, 0:1], [[0, TT], [1, E]])
                dve.wait_ge(logits_ready, n + 1)
                link(dve.tensor_copy(W(0), ps[:, 4, 0:TT * E].rearrange("p (t e) -> p t e", e=E)))
                dve.engine_nop().then_inc(logits_read, 1)
                link(dve.tensor_reduce(S(0), W(0), AX.X, ALU.max))
                dve.tensor_tensor(W(1), W(0), over(S(0), E), ALU.subtract).then_inc(shift_ready, 1)
                for pick in range(2):
                    src, top, hot = W(0) if pick == 0 else W(5), S(pick), W(3 + pick)
                    if pick:
                        link(dve.scalar_tensor_tensor(W(5), W(3), -3.0e38, W(0), ALU.mult, ALU.add))
                        link(dve.tensor_reduce(S(1), W(5), AX.X, ALU.max))
                    link(dve.tensor_tensor(W(6), src, over(top, E), ALU.is_equal))
                    link(dve.tensor_tensor(W(7), W(6), grid, ALU.mult))
                    link(dve.tensor_reduce(S(2 + pick), W(7), AX.X, ALU.min))
                    link(dve.tensor_tensor(hot, grid, over(S(2 + pick), E), ALU.is_equal))
                link(dve.tensor_tensor(W(6), W(3), W(4), ALU.add))
                dve.wait_ge(gexp_ready, n + 1)
                link(dve.tensor_reduce(S(4), W(2), AX.X, ALU.add))
                link(dve.reciprocal(S(5), S(4)))
                link(dve.tensor_tensor(W(7), W(2), over(S(5), E), ALU.mult))
                dve.scalar_tensor_tensor(gates[:, :, :], W(7), factor, W(6), ALU.mult, ALU.mult).then_inc(gates_ready, 1)

            def mix(e):
                for t in range(TT):
                    n = rows(t)
                    if t == 0:
                        dve.wait_ge(y_done, HC * (e + 1))
                    base = x_tok if e == 0 else h_tok
                    ins = dve.scalar_tensor_tensor(h_tok[0:n, t, :], tok_bank(4, t), gates[0:n, t, e:e + 1], base[0:n, t, :], ALU.mult, ALU.add)
                    if t % 2 or t == TT - 1:
                        ins.then_inc(y_read, 1)

            for c in range(NCH):
                e, k = c // HC, c % HC
                dve.wait_ge(hid_ready, c + 1)
                wait(dve, y_done, c - HBUF + 1)
                dve.tensor_copy(hid_hi[:, c % HBUF, :], hid[:, c % 2, :]).then_inc(hid_cast, 1)
                dve.wait_ge(hid_cast, c + 1)
                dve.tensor_tensor(hid_lo[:, c % HBUF, :], hid[:, c % 2, :], hid_hi[:, c % HBUF, :].bitcast(F32), ALU.subtract).then_inc(hid_split, 1)
                if c == 0:
                    gating(0, 1.0)
                    dve.wait_ge(gates_ready, 1)
                if k == 1 and e >= 1:
                    mix(e - 1)
                if k == 2 and e + 1 < E:
                    split_w1(e + 1)
                if k == 4 and e + 1 < E:
                    split_w2(e + 1)
            mix(E - 1)
            dve.wait_ge(y_read, 4 * E)
            layernorm(1, from_proj(1, 0, h_tok))
            channels_out(2, 4)

            dve.wait_ge(lam_ready, 1)
            dve.wait_ge(vbd_zero, 6)
            for bank, slot, h in ((0, 1, 0), (1, 1, 4), (1, 2, 8)):
                link(dve.tensor_scalar(lam[:, bank, slot, :], lam_exp[:, h:h + HQ], -1.0, None, ALU.mult))

            def attention(call, kinds, two_sets):
                dve.wait_ge(v_ready, call + 1)
                for i in (0, 1):
                    for h in range(HQ):
                        src = view(ps[32 * i:32 * i + 32, 4, 16 * h:16 * h + 1], [[256, G], [64, 3], [1, 16]])
                        dst = view(v_bd[32 * h:32 * h + 32, i, 0, 16 * h:16 * h + 1], [[IG * C, G], [64, 3], [1, 16]])
                        ins = dve.tensor_copy(dst, src)
                ins.then_inc(v_dve, 1)
                for n_job, (kind, stack, m) in enumerate(kinds):
                    dve.wait_ge(qk_ready, (6 if call else 0) + n_job + 1)
                    src = ps[0:m, 2 * (n_job % 2), 0:HALF]
                    if kind == "q":
                        dve.tensor_copy(qT[0:m, stack, 0:HALF], src).then_inc(qk_dve, 1)
                    else:
                        dve.tensor_tensor(k_bd[0:m, stack, :, 0:HALF], view(src, [[0, HQ], [1, HALF]]),
                                          over(head_mask1[0:m, :], HALF), ALU.mult).then_inc(qk_dve, 1)

                def shift(g):
                    n = G * call + g
                    dve.wait_ge(s1_ready, n + 1)
                    first = 2 * (g % 2)
                    if two_sets:
                        parts = [(0, 24, view(ps[:, first, 0:1], [[512, 2], [N, 12], [1, N]]))]
                    else:
                        parts = [(0, 8, view(ps[:, first, 0:1], [[N, 8], [1, N]])), (8, 12, view(ps[:, first + 1, 0:1], [[N, 4], [1, N]]))]
                    for a, b, src in parts:
                        top = st1[:, g % 2, 0, a:b]
                        s = s1[:, g % 2, a:b, :]
                        if two_sets:
                            top2 = top.rearrange("p (a b) -> p a b", a=2)
                            s = s.rearrange("p (a b) m -> p a b m", a=2)
                        else:
                            top2 = top
                        link(dve.tensor_reduce(top2, src, AX.X, ALU.max))
                        ins = dve.tensor_tensor(s, src, over(top2, N), ALU.subtract)
                    ins.then_inc(s1_shifted, 1)
                    dve.engine_nop().then_inc(s1_read, 1)

                def norm(g):
                    n = G * call + g
                    k = 24 if two_sets else 12
                    dve.wait_ge(s1_exp, n + 1)
                    e = e1[:, g % 2, 0:k, :]
                    total, inv, coef = (st1[:, g % 2, j, 0:k] for j in (1, 2, 3))
                    link(dve.tensor_reduce(total, e, AX.X, ALU.add))
                    link(dve.reciprocal(inv, total))
                    if g >= 2 or call:
                        dve.wait_ge(p1T_ready, n - 1)
                    p = p1[:, g % 2]
                    if two_sets:
                        link(dve.tensor_tensor(coef, inv, lam[:, :, :, :].rearrange("p a b c -> p (a b c)"), ALU.mult))
                        link(dve.tensor_tensor(e, e, over(coef, N), ALU.mult))
                        blk = e.rearrange("p (a b c) m -> p a b c m", a=2, b=3)
                        dve.tensor_tensor(p[:, 0:2, :, 0:N], blk[:, :, 0], blk[:, :, 1], ALU.add)
                        dve.tensor_tensor(p[:, 2, :, 0:N], blk[:, 0, 2], blk[:, 1, 2], ALU.add).then_inc(p1_ready, 1)
                    else:
                        dve.tensor_tensor(view(p[:, 0, 0, 0:1], [[256, 2], [32, HQ], [1, N]]),
                                          e[:, 0:8].rearrange("p (a b) m -> p a b m", a=2),
                                          over(inv[:, 0:8].rearrange("p (a b) -> p a b", a=2), N), ALU.mult)
                        dve.tensor_tensor(p[:, 1, :, 0:N], e[:, 8:12], over(inv[:, 8:12], N), ALU.mult).then_inc(p1_ready, 1)

                for step in range(G + 1):
                    if step < G:
                        shift(step)
                    if step >= 1:
                        norm(step - 1)

            attention(0, [(x, s, 128) for s in range(3) for x in "kq"], True)
            layernorm(2, from_proj(2, 0, x_tok))
            channels_out(3, 4)
            gating(1, ADAPT)
            for n in range(2):
                dve.wait_ge(ha_ready, n + 1)
                dve.wait_ge(ce_done, n + 1)
                by_image = lambda x: x.rearrange("p (b n) -> p b n", n=N)
                dve.tensor_tensor(view(hwT[:, 512 * n:512 * n + 1], [[32, B // 2], [1, N]]), by_image(ps[:, 2 + n, 0:HALF]),
                                  by_image(ce[:, n * HALF:(n + 1) * HALF]), ALU.mult).then_inc(hw_done, 1)
            attention(1, [("k", 0, 128), ("q", 0, 128), ("k", 1, 64), ("q", 1, 64)], False)
            layernorm(3, from_proj(3, 0, x_tok))


POS = [j * SIDE // NB for j in range(NB)]


def kernel(**inputs):
    import numpy as np
    import concourse.bacc as bacc
    from concourse.bass_utils import run_bass_kernel_spmd as run

    a = {k: np.asarray(v) for k, v in inputs.items()}
    crop = NB * PATCH
    x = a["x"][:, :, :crop, :crop].reshape(B, CIN, NB, PATCH, NB, PATCH)

    def stacked(w):
        w = w.reshape(C, 2, C)
        return np.concatenate([w[:, 0, :128], w[:, 1, :128], w[:, 0, 128:], w[:, 1, 128:]], axis=1)

    tok = np.arange(T)
    row = np.arange(128)
    arrays = {
        "patT": x.transpose(1, 3, 5, 0, 2, 4).reshape(KP, T),
        "wconv": a["L0_tok_conv_w"].reshape(C, KP).T,
        "pos": a["L0_tok_pos_table"],
        "conv_b": a["L0_tok_conv_b"].reshape(1, C),
        "wq0": np.pad(np.broadcast_to(a["L0_attn_Wq"].reshape(C, 2, 1, D0), (C, 2, 4, D0)), ((0, 0),) * 3 + ((0, 32 - D0),)).reshape(C, 256), "wkv0": a["L0_attn_Wkv"], "wp0": np.pad(a["L0_attn_Wproj"].reshape(2, 4, D0, C), ((0, 0), (0, 0), (0, 32 - D0), (0, 0))).transpose(1, 2, 0, 3).reshape(128, 2 * C),
        "bp0": a["L0_attn_bproj"].reshape(1, C),
        "wg0": a["L0_ffn_Wg"], "w1": a["L0_ffn_W1"], "w2": a["L0_ffn_W2"],
        "b1c": a["L0_ffn_b1"].reshape(NCH, 128).T, "b2": a["L0_ffn_b2"],
        "wq1": stacked(a["L1_attn_Wq"]), "wk1": stacked(a["L1_attn_Wk"]), "wv1": a["L1_attn_Wv"], "wo1": a["L1_attn_Wo"],
        "lam": a["L1_attn_lambda_p"].reshape(1, H1), "bo1": a["L1_attn_bo"].reshape(1, C),
        "wg2": a["L1_ffn_Wg"].T, "bg2": a["L1_ffn_bg"].reshape(1, E),
        "wqkv": a["L1_ffn_Wqkv"].T, "bqkv": a["L1_ffn_bqkv"].reshape(1, 3 * C),
        "wp2": a["L1_ffn_Wproj"].T, "bp2": a["L1_ffn_bproj"].reshape(1, C),
        "wa2": a["L1_ffn_A"].reshape(E * R, C).T, "ba2": a["L1_ffn_ba"].reshape(1, E * R),
        "bm2": a["L1_ffn_Bm"].transpose(0, 2, 1).reshape(E * R, 3 * C), "bb2": a["L1_ffn_bb"],
        "ident": np.eye(128, dtype=np.float32),
        "sel": np.concatenate([np.arange(N)[:, None] == tok[None, :] % N, np.ones((1, T), bool)]).astype(np.float32),
        "mask0": (row[:CH, None] // D0 == row[None, :CH] // D0).astype(np.float32),
        "mask1": (row[:, None] % 64 // D1 == np.arange(HQ)[None, :]).astype(np.float32),
        "expert_rows": (np.arange(E)[:, None] == row[None, :] // R).astype(np.float32),
        "iota8": np.tile(np.arange(E, dtype=np.float32) - E, (128, 1)),
    }
    nc = bacc.Bacc("TRN2", target_bir_lowering=False, num_devices=1)
    io, feed = {}, {}
    for name, v in arrays.items():
        feed[f"in_{name}"] = np.ascontiguousarray(v)
        io[name] = nc.dram_tensor(f"in_{name}", v.shape, F32, kind="ExternalInput").ap()
    io["out"] = nc.dram_tensor("out", (T, C), F32, kind="ExternalOutput").ap()
    build(nc, io)
    r = run(nc, [feed], core_ids=[0])
    return r.results[0]["out"].reshape(B, N, C)
```

```python
from contextlib import ExitStack

import concourse.bass as bass
from concourse import mybir

F32 = mybir.dt.float32
F32R = mybir.dt.float32r
ALU = mybir.AluOpType
ACT = mybir.ActivationFunctionType
AX = mybir.AxisListType

B, CIN, IMG, PATCH = 32, 3, 84, 16
SIDE = 32
NB = IMG // PATCH
N = NB * NB
T = B * N
C = 192
CA, CB = 128, C - 128
KP = CIN * PATCH * PATCH
KCH = KP // 128
TT = (T + 127) // 128
TP = TT * 128
IG = 4
G = B // IG
GT = IG * N
HALF = T // 2
EPS = 1e-5
E, HID = 8, 768
HC = HID // 128
NCH = E * HC
H0, D0 = 8, 24
HG0 = H0 // 2
CH = HG0 * D0
H1, D1 = 12, 16
HQ = 4
R = 16
ADAPT = 2.0
HBUF = 3

CONSTS = [("ident", 128), ("mask0", CH), ("mask1", HQ), ("expert_rows", 128), ("iota8", E), ("expert_sel", E), ("fold", CB)]
W0A = [("wkv0", 2 * C), ("wq0", 128), ("wp0", 2 * C), ("wg0", E), ("b1c", NCH)]
W0B = [("wkv0", 2 * C), ("wq0", 128), ("bp0", C), ("wg0", E), ("b2", C)]
W1A = [("wq1", 2 * C), ("wk1", 2 * C), ("wv1", C), ("wo1", C), ("lam", H1), ("wg2", E), ("wa2", 128),
       ("wqkv", 3 * C), ("wbm", 3 * C), ("wp2", C)]
W1B = [("wq1", 2 * C), ("wk1", 2 * C), ("wv1", C), ("wo1", C), ("wg2", E), ("wa2", 128), ("wqkv", 3 * C), ("wp2", C)]


def rows(t):
    return min(128, T - 128 * t)


def view(ap, dims):
    return bass.AP(tensor=ap.tensor, offset=ap.offset, ap=[list(ap.ap[0])] + [list(d) for d in dims])


def build(nc, io):
    with ExitStack() as ctx:
        def sb(name, shape, dt=F32, scope=ctx):
            return scope.enter_context(nc.sbuf_tensor(name, shape, dt))

        def sem(name):
            return ctx.enter_context(nc.semaphore(name))

        ps = ctx.enter_context(nc.psum_tensor("ps", [128, 8, 512], F32))

        consts = sb("consts", [128, sum(w for _, w in CONSTS)])
        w0a, w0b = (sb(n, [r, sum(w for _, w in cols)]) for n, r, cols in (("w0a", 128, W0A), ("w0b", CB + 1, W0B)))
        w1a, w1b = (sb(n, [r, sum(w for _, w in cols)]) for n, r, cols in (("w1a", 128, W1A), ("w1b", 104, W1B)))

        def col(pack, cols, name, r0=0, r1=None):
            at = 0
            for n, width in cols:
                if n == name:
                    return pack[r0:r1 if r1 else pack.shape[0], at:at + width]
                at += width
            raise KeyError(name)

        ident = col(consts, CONSTS, "ident")
        head_mask0 = col(consts, CONSTS, "mask0", 0, CH)
        head_mask1 = col(consts, CONSTS, "mask1")
        expert_rows = col(consts, CONSTS, "expert_rows", 96, 104)
        iota8 = col(consts, CONSTS, "iota8")
        expert_sel = col(consts, CONSTS, "expert_sel", 0, 2 * E)
        fold = col(consts, CONSTS, "fold")
        wkv0a, wkv0b = col(w0a, W0A, "wkv0"), col(w0b, W0B, "wkv0", 0, CB)
        wq0a, wq0b = col(w0a, W0A, "wq0"), col(w0b, W0B, "wq0", 0, CB)
        wp0 = col(w0a, W0A, "wp0").rearrange("p (s c) -> p s c", s=2)
        bp0 = col(w0b, W0B, "bp0", CB, CB + 1)
        wg0a, wg0b = col(w0a, W0A, "wg0"), col(w0b, W0B, "wg0", 0, CB)
        b1c = col(w0a, W0A, "b1c")
        b2r = col(w0b, W0B, "b2", 0, 2 * E)
        wq1a, wq1b = col(w1a, W1A, "wq1"), col(w1b, W1B, "wq1", 0, CB)
        wk1a, wk1b = col(w1a, W1A, "wk1"), col(w1b, W1B, "wk1", 0, CB)
        wv1a, wv1b = col(w1a, W1A, "wv1"), col(w1b, W1B, "wv1", 0, CB)
        wo1a, wo1b = col(w1a, W1A, "wo1"), col(w1b, W1B, "wo1", 0, CB + 1)
        lam_raw = col(w1a, W1A, "lam")
        wg2a, wg2b = col(w1a, W1A, "wg2"), col(w1b, W1B, "wg2", 0, CB + 1)
        wa2a, wa2b = col(w1a, W1A, "wa2"), col(w1b, W1B, "wa2", 0, CB + 1)
        wqkva, wqkvb = col(w1a, W1A, "wqkv"), col(w1b, W1B, "wqkv")
        wbm = col(w1a, W1A, "wbm")
        wp2a, wp2b = col(w1a, W1A, "wp2"), col(w1b, W1B, "wp2", 0, CB + 1)
        lam_exp = sb("lam_exp", [128, H1])
        lam = sb("lam", [128, 2, 3, HQ])
        neg_half = sb("neg_half", [128, TT])

        x_tok = sb("x_tok", [128, TT, C])
        h_tok = sb("h_tok", [128, TT, C])
        stats = sb("stats", [128, TT, 6])
        mv = sb("mv", [128, TT, 2])
        veps = sb("veps", [128, TT])
        rstd = sb("rstd", [128, TT])
        xa = sb("xa", [CA, TP])
        xb = sb("xb", [CB + 1, TP])
        xpa = sb("xpa", [CA, 32 * B])
        xpb = sb("xpb", [104, 32 * B])
        gate_w = sb("gate_w", [128, 8, TT, E])
        gate_s = sb("gate_s", [128, 6, TT])
        gates = sb("gates", [128, TT, E])
        gate_hl = sb("gate_hl", [128, TT, 2 * E])
        gatesT = sb("gatesT", [2 * E, T], F32R)

        early = ExitStack()
        kv0 = sb("kv0", [128, G, 2 * C], scope=early)
        q0 = sb("q0", [128, 2, T], scope=early)
        st0 = sb("st0", [CH, 3, 16], scope=early)
        a0 = sb("a0", [CH, 2, 2, IG, 2, 32], scope=early)
        o0 = sb("o0", [128, 2 * T], scope=early)
        with ExitStack() as first:
            pat = sb("pat", [128, KCH, T + C], scope=first)
            pos_sel = sb("pos_sel", [N + 1, C + T], scope=first)
            posb, sel = pos_sel[:, 0:C], pos_sel[:, C:]
        m0 = sb("m0", [CH, 16, CH], scope=early)
        s0 = sb("s0", [CH, 2, 16, D0], scope=early)
        e0 = sb("e0", [CH, 2, 16, D0], scope=early)
        a0T = sb("a0T", [128, 16, HG0, 32], scope=early)
        early.close()
        late = ExitStack()
        v_bd = sb("v_bd", [128, B, 3, 64], scope=late)
        p1 = sb("p1", [128, 2, 3, HQ, 32], scope=late)
        ob = sb("ob", [CB + 1, T], scope=late)
        hwT = sb("hwT", [128, 32 * B], scope=late)
        with ExitStack() as moe:
            gate_bc = sb("gate_bc", [128, E, T], scope=moe)
        s1 = sb("s1", [128, 2, 24, N], scope=late)
        e1 = sb("e1", [128, 2, 24, N], scope=late)
        st1 = sb("st1", [128, 2, 4, 24], scope=late)
        p1T = sb("p1T", [128, 2, 3, 128], scope=late)
        oa = sb("oa", [CA, T], scope=late)
        ce = sb("ce", [128, T], scope=late)
        qT = sb("qT", [128, 3, T + 8], scope=late)
        late.close()
        sb("region_one", [128, 16120])

        ffn = ExitStack()
        w1_raw = sb("w1_raw", [128, 2, HID], scope=ffn)
        w2_raw = sb("w2_raw", [128, HC, C], scope=ffn)
        w1_hi = sb("w1_hi", [128, 2, HID], F32R, scope=ffn)
        w1_lo = sb("w1_lo", [128, 2, HID], F32R, scope=ffn)
        w1_tail = sb("w1_tail", [128, 2, HID], F32R, scope=ffn)
        w2_hi = sb("w2_hi", [128, 2, HC, CA], F32R, scope=ffn)
        w2_lo = sb("w2_lo", [128, 2, HC, CA], F32R, scope=ffn)
        w2_tail = sb("w2_tail", [128, 2, HC, 2 * CB], F32R, scope=ffn)
        x_hi = sb("x_hi", [CA, T], F32R, scope=ffn)
        x_lo = sb("x_lo", [CA, T], F32R, scope=ffn)
        xt_hi = sb("xt_hi", [128, T], F32R, scope=ffn)
        xt_lo = sb("xt_lo", [CB, T], F32R, scope=ffn)
        with ExitStack() as before:
            bc_sel = sb("bc_sel", [2 * E, E, 128], F32R, scope=before)
        hid = sb("hid", [128, 2, T], scope=ffn)
        hid_hi = sb("hid_hi", [128, HBUF, T], F32R, scope=ffn)
        hid_lo = sb("hid_lo", [128, HBUF, T], F32R, scope=ffn)
        ffn.close()
        yT = hid
        k_bd = sb("k_bd", [128, 3, HQ, T])

        patch_in = [sem(f"patch_in{k}") for k in range(KCH)]
        const_in = sem("const_in")
        w0_in = sem("w0_in")
        wlate_in = sem("wlate_in")
        w1_in, w2_in = sem("w1_in"), sem("w2_in")
        out_sent = sem("out_sent")
        pool_set = sem("pool_set")
        vbd_zero = sem("vbd_zero")
        conv_done = sem("conv_done")
        x0_act, x0_dve = sem("x0_act"), sem("x0_dve")
        xT_ready = sem("xT_ready")
        xa_done, xb_done = sem("xa_done"), sem("xb_done")
        kv_ready = sem("kv_ready")
        kv_act, kv_dve = sem("kv_act"), sem("kv_dve")
        q0_ready = sem("q0_ready")
        q0_act, q0_dve = sem("q0_act"), sem("q0_dve")
        s0_ready, s0_masked = sem("s0_ready"), sem("s0_masked")
        s0_shifted, s0_exp, a0_ready = sem("s0_shifted"), sem("s0_exp"), sem("a0_ready")
        a0T_ready, a0T_done = sem("a0T_ready"), sem("a0T_done")
        o0_ready, o0_act, o0_dve = sem("o0_ready"), sem("o0_act"), sem("o0_dve")
        a0T_zero = sem("a0T_zero")
        proj_ready = sem("proj_ready")
        summed = sem("summed")
        veps_ready, rstd_ready = sem("veps_ready"), sem("rstd_ready")
        x_ready = sem("x_ready")
        dve_chain = sem("dve_chain")
        x_split = sem("x_split")
        logits_ready, logits_read = sem("logits_ready"), sem("logits_read")
        shift_ready, gexp_ready, gates_ready = sem("shift_ready"), sem("gexp_ready"), sem("gates_ready")
        gT_ready, gT_done = sem("gT_ready"), sem("gT_done")
        w1_cast, w2_cast = sem("w1_cast"), sem("w2_cast")
        w1_split, w2_split = sem("w1_split"), sem("w2_split")
        z_ready, hid_ready, hid_cast, hid_split = sem("z_ready"), sem("hid_ready"), sem("hid_cast"), sem("hid_split")
        gate_parts = sem("gate_parts")
        bc_ready, bc_act, bc_dve = sem("bc_ready"), sem("bc_act"), sem("bc_dve")
        sel_ready = sem("sel_ready")
        y_done, yT_act, yT_dve = sem("y_done"), sem("yT_act"), sem("yT_dve")
        lam_ready = sem("lam_ready")
        v_ready, v_act, v_dve = sem("v_ready"), sem("v_act"), sem("v_dve")
        qk_ready, qk_act, qk_dve = sem("qk_ready"), sem("qk_act"), sem("qk_dve")
        s1_ready, s1_shifted, s1_exp = sem("s1_ready"), sem("s1_shifted"), sem("s1_exp")
        p1_ready, p1T_ready, p1T_done = sem("p1_ready"), sem("p1T_ready"), sem("p1T_done")
        o1_ready, o1_done = sem("o1_ready"), sem("o1_done")
        ce_ready, ce_done, ha_ready, hw_done = sem("ce_ready"), sem("ce_done"), sem("ha_ready"), sem("hw_done")

        def wait(eng, s, value):
            if not isinstance(value, int) or value > 0:
                eng.wait_ge(s, value)

        def tok_bank(first, t):
            return ps[0:rows(t), first + t // 2, (t % 2) * C:(t % 2) * C + C]

        def spread(dst, src, j):
            whole = 512 // N
            cut = 512 - whole * N
            if j == 0:
                return [(view(dst[:, 0:1], [[32, whole], [1, N]]), view(src[:, 0:1], [[N, whole], [1, N]])),
                        (dst[:, 32 * whole:32 * whole + cut], src[:, whole * N:512])]
            rest = N - cut
            return [(dst[:, 32 * whole + cut:32 * whole + N], src[:, 0:rest]),
                    (view(dst[:, 32 * (whole + 1):32 * (whole + 1) + 1], [[32, B - whole - 1], [1, N]]),
                     view(src[:, rest:rest + 1], [[N, B - whole - 1], [1, N]]))]

        def reorder(h):
            pairs = []
            for a in range(2):
                first = (2 * h + a) * N
                for r in range(4):
                    n0 = (r - first) % 4
                    count = len(range(n0, N, 4))
                    src = ps[32 * h:32 * h + 32, 0, a * N + n0:a * N + n0 + 1]
                    dst = o0[32 * r:32 * r + 32, (first + n0) // 4:(first + n0) // 4 + 1]
                    pairs.append((view(dst, [[2 * N, IG], [2 * GT, G], [1, count]]),
                                  view(src, [[512, IG], [2 * N, G], [4, count]])))
            return pairs

        block = ctx.enter_context(nc.Block())

        @block.sync
        def _(sp):
            def load(dst, src, s):
                sp.dma_start(dst, src).then_inc(s, 16)
                return 16

            for k in range(KCH):
                load(pat[:, k, :], io["pat"][128 * k:128 * k + 128, :], patch_in[k])
            load(pos_sel[:, :], io["pos_sel"], const_in)
            load(consts[:, :], io["consts"], const_in)
            load(w0a[:, :], io["w0a"], w0_in)
            load(w0b[:, :], io["w0b"], w0_in)

            def load_expert(e):
                wait(sp, w1_cast, 2 * e)
                wait(sp, w1_split, 2 * e)
                load(w1_raw[:, 0, :], io["w1"][e, 0:CA, :], w1_in)
                load(w1_raw[0:CB, 1, :], io["w1"][e, CA:C, :], w1_in)
                load(w1_raw[CB:128, 1, :], io["w1"][e, CA:C, :], w1_in)
                wait(sp, w2_cast, 2 * e)
                wait(sp, w2_split, 2 * e)
                load(w2_raw[:, :, :], io["w2"][e].rearrange("(k p) c -> p k c", p=128), w2_in)

            load_expert(0)
            load(w1a[:, :], io["w1a"], wlate_in)
            load(w1b[:, :], io["w1b"], wlate_in)
            for e in range(1, E):
                load_expert(e)
            for t in range(TT):
                sp.wait_ge(x_ready, 3 * TT + t + 1)
                load(io["out"][128 * t:128 * t + rows(t), :], x_tok[0:rows(t), t, :], out_sent)
            sp.wait_ge(out_sent, 16 * TT)

        @block.gpsimd
        def _(pool):
            count = {}

            def fill(ap, value, s):
                pool.memset(ap, value).then_inc(s, 1)
                count[s] = count.get(s, 0) + 1
                pool.wait_ge(s, count[s])

            fill(xpa[:, :], 0.0, pool_set)
            fill(xpb[:, :], 0.0, pool_set)
            fill(xa[:, T:TP], 0.0, pool_set)
            fill(xb[0:CB, T:TP], 0.0, pool_set)
            fill(a0[:, :, :, :, :, D0:32], 0.0, pool_set)
            fill(q0[:, :, :], 0.0, pool_set)
            fill(mv[:, :, :], 1.0, pool_set)
            fill(neg_half[:, :], -0.5, pool_set)
            fill(xb[CB:CB + 1, :], 1.0, pool_set)
            fill(xpb[CB:CB + 1, :], 1.0, pool_set)

            def rsqrt(layer):
                for half in range(2):
                    ts = slice(0, 4) if half == 0 else slice(4, TT)
                    pool.wait_ge(veps_ready, 2 * layer + half + 1)
                    pool.tensor_tensor(rstd[:, ts], veps[:, ts], neg_half[:, ts], ALU.pow).then_inc(rstd_ready, 1)
                    pool.wait_ge(rstd_ready, 2 * layer + half + 1)

            pool.wait_ge(conv_done, TT)
            fill(a0T[:, :, :, :], 0.0, a0T_zero)
            rsqrt(0)
            pool.wait_ge(proj_ready, TT)
            fill(v_bd[:, :, :, :], 0.0, vbd_zero)
            fill(p1[:, :, :, :, N:32], 0.0, vbd_zero)
            fill(ob[CB:CB + 1, :], 1.0, vbd_zero)
            fill(hwT[:, :], 0.0, vbd_zero)
            fill(lam[:, :, :, :], 1.0, vbd_zero)
            pool.wait_ge(hid_ready, NCH)
            fill(qT[:, :, T:T + 8], 0.0, vbd_zero)
            rsqrt(1)
            rsqrt(2)
            rsqrt(3)

        PREP = 10

        @block.tensor
        def _(pe):
            def to_channels(layer, first):
                for t in range(TT):
                    n = rows(t)
                    at = 128 * (t % 4)
                    if layer:
                        pe.wait_ge(x_ready, (layer - 1) * TT + t + 1)
                    else:
                        pe.wait_ge([x0_dve, x0_act][(t // 2) % 2], t // 4 + 1)
                    pe.transpose(ps[:, first + t // 4, at:at + n], x_tok[0:n, t, 0:CA], ident[0:n, 0:n])
                    pe.transpose(ps[0:CB, first + 2 + t // 4, at:at + n], x_tok[0:n, t, CA:C], ident[0:n, 0:n]).then_inc(xT_ready, 1)

            def padded(x, g):
                return x[:, 128 * g:128 * g + 128]

            def half_of(x, n):
                return view(x[:, 32 * (B // 2) * n:32 * (B // 2) * n + 1], [[32, B // 2], [1, N]])

            for k in range(KCH):
                pe.wait_ge(patch_in[k], 16)
                for t in range(TT):
                    pe.matmul(tok_bank(0, t), pat[:, k, 128 * t:128 * t + rows(t)], pat[:, k, T:],
                              start=(k == 0 and t % 2 == 0), stop=False, skip_group_check=True)
            pe.wait_ge(const_in, 32)
            for t in range(TT):
                pe.matmul(tok_bank(0, t), sel[:, 128 * t:128 * t + rows(t)], posb,
                          start=False, stop=True, skip_group_check=True).then_inc(conv_done, 1)
            to_channels(0, 4)

            pe.wait_ge(w0_in, 32)
            pe.wait_ge(pool_set, PREP)
            for g in range(G):
                half = 1 if GT * (g + 1) <= 512 else 2
                pe.wait_ge(xa_done, half)
                pe.wait_ge(xb_done, half)
                if g >= 4:
                    pe.wait_ge([kv_act, kv_dve][g % 2], (g - 4) // 2 + 1)
                pe.matmul(ps[:, g % 4, 0:2 * C], padded(xpa, g), wkv0a[:, :], start=True, stop=False)
                pe.matmul(ps[:, g % 4, 0:2 * C], padded(xpb[0:CB], g), wkv0b[:, :], start=False, stop=True).then_inc(kv_ready, 1)
            for n in range(2):
                out = ps[:, 4 + n, 0:HALF]
                pe.matmul(out, wq0a, half_of(xpa, n), start=True, stop=False)
                pe.matmul(out, wq0b, half_of(xpb[0:CB], n), start=False, stop=True).then_inc(q0_ready, 1)

            def turn_a0(r):
                pe.wait_ge(a0_ready, r + 1)
                for j in range(4):
                    mm = pe.transpose(ps[:, 4 + r % 2, CH * j:CH * j + CH],
                                      a0[:, r % 2, j // 2, 2 * (j % 2):2 * (j % 2) + 2, :, :], ident[0:CH, 0:CH])
                mm.then_inc(a0T_ready, 1)

            pe.wait_ge(kv_act, 4)
            pe.wait_ge(kv_dve, 4)
            for r in range(6):
                if r < 4:
                    wait(pe, s0_masked, r)
                    for gg in range(2):
                        for a in range(2):
                            for i in range(IG):
                                kv = kv0[32 * i:32 * i + N, 2 * r + gg, :]
                                mm = pe.matmul(ps[0:CH, i, CH * (2 * gg + a):CH * (2 * gg + a) + CH],
                                               kv[:, CH * a:CH * a + CH], kv[:, C + CH * a:C + CH * a + CH], start=True, stop=True)
                    mm.then_inc(s0_ready, 1)
                if r == 1:
                    pe.wait_ge(q0_act, 1)
                    pe.wait_ge(q0_dve, 1)
                if r >= 2:
                    wait(pe, a0T_done, r - 3)
                    turn_a0(r - 2)
            pe.wait_ge(s0_masked, 4)
            for r in range(4):
                pe.wait_ge(a0T_done, r + 1)
                for gg in range(2):
                    g = 2 * r + gg
                    for i in range(IG):
                        row = 64 * (i % 2)
                        tok = GT * g + N * i
                        mm = pe.matmul(ps[:, i, 2 * N * g:2 * N * g + 2 * N],
                                       a0T[row:row + 64, 4 * r + 2 * gg + i // 2, :, :],
                                       q0[row:row + 64, :, tok:tok + N], start=True, stop=True)
            mm.then_inc(o0_ready, 1)
            pe.wait_ge(o0_act, 1)
            pe.wait_ge(o0_dve, 1)
            for t in range(TT):
                n = rows(t)
                for s in range(2):
                    pe.matmul(tok_bank(4, t), view(o0[:, 256 * t + s:256 * t + s + 1], [[2, n]]), wp0[:, s, :], start=(s == 0), stop=False)
                pe.matmul(tok_bank(4, t), xb[CB:CB + 1, 0:n], bp0, start=False, stop=True).then_inc(proj_ready, 1)

            to_channels(1, 0)

            def logits(layer, wa, wb, kb):
                for t in range(TT):
                    cols = slice(128 * t, 128 * t + 128)
                    pe.matmul(ps[:, 4, E * t:E * t + E], xa[:, cols], wa[:, :], start=True, stop=False)
                    mm = pe.matmul(ps[:, 4, E * t:E * t + E], xb[0:kb, cols], wb[:, :], start=False, stop=True)
                mm.then_inc(logits_ready, 1)

            pe.wait_ge(xa_done, 4)
            pe.wait_ge(xb_done, 4)
            pe.wait_ge(summed, 4)
            logits(1, wg0a, wg0b, CB)

            def expert_in(c):
                e, k = c // HC, c % HC
                if k == 0:
                    pe.wait_ge(w1_split, 2 * (e + 1))
                if c == 0:
                    pe.wait_ge(x_split, 4)
                wait(pe, hid_ready, c - 1)
                cols = slice(128 * k, 128 * k + 128)
                j = e % 2
                for n in range(2):
                    out = ps[:, 2 * (c % 2) + n, 0:HALF]
                    tok = slice(n * HALF, (n + 1) * HALF)
                    pe.matmul(out, w1_hi[:, j, cols], x_hi[:, tok], start=True, stop=False)
                    pe.matmul(out, w1_hi[:, j, cols], x_lo[:, tok], start=False, stop=False)
                    pe.matmul(out, w1_lo[:, j, cols], x_hi[:, tok], start=False, stop=False)
                    pe.matmul(out, w1_tail[:, j, cols], xt_hi[:, tok], start=False, stop=False)
                    mm = pe.matmul(out, w1_tail[0:CB, j, cols], xt_lo[:, tok], start=False, stop=True)
                mm.then_inc(z_ready, 1)

            def expert_out(c):
                e, k = c // HC, c % HC
                j = e % 2
                pe.wait_ge(hid_split, c + 1)
                if k == 0:
                    pe.wait_ge(w2_split, 2 * (e + 1))
                if c == 0:
                    pe.wait_ge(bc_act, E)
                    pe.wait_ge(bc_dve, E)
                first, last = c == 0, c == NCH - 1
                for n in range(2):
                    tok = slice(n * HALF, (n + 1) * HALF)
                    h_hi, h_lo = hid_hi[:, c % HBUF, tok], hid_lo[:, c % HBUF, tok]
                    top, tail = ps[:, 4 + n, 0:HALF], ps[:, 6 + n, 0:HALF]
                    pe.matmul(top, w2_hi[:, j, k, :], h_hi, start=first, stop=False, skip_group_check=True)
                    pe.matmul(top, w2_lo[:, j, k, :], h_hi, start=False, stop=False, skip_group_check=True)
                    pe.matmul(top, w2_hi[:, j, k, :], h_lo, start=False, stop=last, skip_group_check=True)
                    pe.matmul(tail, w2_tail[:, j, k, :], h_hi, start=first, stop=False, skip_group_check=True)
                    mm = pe.matmul(tail[0:CB], w2_tail[:, j, k, 0:CB], h_lo, start=False, stop=last, skip_group_check=True)
                mm.then_inc(y_done, 1)

            def turn_gates(gates, e, first):
                for t in range(TT):
                    n = rows(t)
                    mm = pe.transpose(ps[0:e, first + t // 4, 128 * (t % 4):128 * (t % 4) + n], gates[0:n, t, :], ident[0:n, 0:n])
                mm.then_inc(gT_ready, 1)

            expert_in(0)
            expert_in(1)
            pe.wait_ge(gate_parts, 2)
            turn_gates(gate_hl, 2 * E, 4)
            pe.wait_ge(gT_done, 1)
            pe.wait_ge(sel_ready, 1)
            for e in range(E):
                for n in range(2):
                    if e >= 2:
                        pe.wait_ge([bc_act, bc_dve][n], e - 1)
                    pe.matmul(ps[:, 4 + 2 * (e % 2) + n, 0:HALF], bc_sel[:, e, :], gatesT[:, n * HALF:(n + 1) * HALF], start=True, stop=True).then_inc(bc_ready, 1)
            for c in range(2, NCH):
                expert_in(c)
                expert_out(c - 2)
            expert_out(NCH - 2)
            expert_out(NCH - 1)
            pe.wait_ge(yT_act, 2)
            pe.wait_ge(yT_dve, 2)
            for t in range(TT):
                cols = slice(128 * t, 128 * t + rows(t))
                out = tok_bank(0, t)
                pe.matmul(out, gatesT[:, cols].bitcast(F32), b2r, start=True, stop=False, skip_group_check=True)
                pe.matmul(out[:, 0:CA], yT[:, 0, cols], ident, start=False, stop=True, skip_group_check=True)
                pe.matmul(out[:, CA:C], yT[:, 1, cols], fold, start=False, stop=True, skip_group_check=True).then_inc(proj_ready, 1)

            def attention(call, q_jobs, slots, v_terms):
                for g in range(G):
                    pe.wait_ge(v_free[call][0], v_free[call][1])
                    for n, (x, w) in enumerate(v_terms):
                        mm = pe.matmul(ps[:, 4 + g // 2, 256 * (g % 2):256 * (g % 2) + C], padded(x, g), w,
                                       start=(n == 0), stop=(n == len(v_terms) - 1))
                mm.then_inc(v_ready, 1)
                for n_job, (m, terms) in enumerate(q_jobs):
                    job = QK_BASE[call] + n_job
                    if n_job >= 2:
                        pe.wait_ge(qk_act, job - 1)
                        pe.wait_ge(qk_dve, job - 1)
                    for n in range(2):
                        for j, (w, x) in enumerate(terms):
                            mm = pe.matmul(ps[0:m, 2 * (n_job % 2) + n, 0:HALF], w, half_of(x, n), start=(j == 0), stop=(j == len(terms) - 1))
                    mm.then_inc(qk_ready, 1)
                pe.wait_ge(qk_act, QK_BASE[call] + len(q_jobs))
                pe.wait_ge(qk_dve, QK_BASE[call] + len(q_jobs))
                pe.wait_ge(v_act, call + 1)
                pe.wait_ge(v_dve, call + 1)

                def scores(g):
                    n = G * call + g
                    if g >= 2:
                        pe.wait_ge(s1_shifted, n - 1)
                    for bank, slot, row, stack in slots:
                        for i in range(IG):
                            tok = GT * g + N * i
                            keys = k_bd[row:row + 64, stack, :, tok:tok + N]
                            mm = pe.matmul(ps[32 * i:32 * i + 32, 2 * (g % 2) + bank, 4 * N * slot:4 * N * slot + 4 * N],
                                           qT[row:row + 64, stack, tok:tok + 32], keys, start=True, stop=True)
                    mm.then_inc(s1_ready, 1)

                def turn(g):
                    n = G * call + g
                    pe.wait_ge(p1_ready, n + 1)
                    if g >= 2:
                        pe.wait_ge(p1T_done, n - 1)
                    for b in range(3):
                        mm = pe.transpose(ps[:, 4 + g % 2, 128 * b:128 * b + 128], p1[:, g % 2, b, :, :], ident[:, :])
                    mm.then_inc(p1T_ready, 1)

                def times_v(g):
                    n = G * call + g
                    pe.wait_ge(p1T_done, n + 1)
                    if g >= 2:
                        pe.wait_ge(o1_done, n - 1)
                    for b in range(3):
                        for i in range(IG):
                            rr = 64 * (b % 2)
                            col = (128 if b == 2 else 0) + N * i
                            mm = pe.matmul(ps[rr:rr + 64, 6 + g % 2, col:col + N], v_bd[:, IG * g + i, b, :],
                                           p1T[:, g % 2, b, 32 * i:32 * i + N], start=True, stop=True)
                    mm.then_inc(o1_ready, 1)

                for step in range(G + 3):
                    if step < G:
                        scores(step)
                    if 2 <= step <= G + 1:
                        turn(step - 2)
                    if step >= 3:
                        times_v(step - 3)

            def project(call, wa, wb):
                pe.wait_ge(o1_done, G * (call + 1))
                for t in range(TT):
                    cols = slice(128 * t, 128 * t + rows(t))
                    pe.matmul(tok_bank(0, t), oa[:, cols], wa[:, :], start=True, stop=False)
                    pe.matmul(tok_bank(0, t), ob[:, cols], wb[:, :], start=False, stop=True).then_inc(proj_ready, 1)

            QK_BASE = [0, 6]
            v_free = [(xb_done, 6), (xb_done, 8)]
            to_channels(2, 4)
            pe.wait_ge(xa_done, 6)
            pe.wait_ge(xb_done, 6)
            pe.wait_ge(summed, 8)
            pe.wait_ge(wlate_in, 32)
            pe.wait_ge(vbd_zero, 6)
            jobs = []
            for stack in range(3):
                for wa, wb in ((wk1a, wk1b), (wq1a, wq1b)):
                    cols = slice(128 * stack, 128 * stack + 128)
                    jobs.append((128, [(wa[:, cols], xpa), (wb[:, cols], xpb[0:CB])]))
            attention(0, jobs, [(0, 0, 0, 0), (1, 0, 64, 0), (0, 1, 0, 1), (1, 1, 64, 1), (0, 2, 0, 2), (1, 2, 64, 2)],
                      [(xpa, wv1a[:, :]), (xpb[0:CB], wv1b[:, :])])
            project(0, wo1a, wo1b)

            to_channels(3, 4)
            pe.wait_ge(xa_done, 8)
            pe.wait_ge(xb_done, 8)
            pe.wait_ge(summed, 12)
            logits(3, wg2a, wg2b, CB + 1)
            for n in range(2):
                pe.matmul(ps[:, 2 + n, 0:HALF], wa2a[:, :], half_of(xpa, n), start=True, stop=False)
                pe.matmul(ps[:, 2 + n, 0:HALF], wa2b[:, :], half_of(xpb[0:CB + 1], n), start=False, stop=True).then_inc(ha_ready, 1)
            pe.wait_ge(gates_ready, 2)
            turn_gates(gates, E, 0)
            pe.wait_ge(gT_done, 2)
            for n in range(2):
                pe.matmul(ps[:, 5 + n, 0:HALF], expert_rows, half_of(xpb[96:104], n), start=True, stop=True).then_inc(ce_ready, 1)
            pe.wait_ge(hw_done, 2)

            def terms(c0, m):
                return [(wqkva[:, c0:c0 + m], xpa), (wqkvb[:, c0:c0 + m], xpb), (wbm[:, c0:c0 + m], hwT)]
            jobs = [(128, terms(C, 128)), (128, terms(0, 128)), (64, terms(C + 128, 64)), (64, terms(128, 64))]
            attention(1, jobs, [(0, 0, 0, 0), (1, 0, 64, 0), (0, 1, 0, 1)],
                      [(xpa, wqkva[:, 2 * C:]), (xpb, wqkvb[:, 2 * C:]), (hwT, wbm[:, 2 * C:])])
            project(1, wp2a, wp2b)

        @block.scalar
        def _(act):
            def copy(out, in_):
                return act.activation(out, in_, ACT.Copy)

            def channels_out(layer, first):
                for j in range(2):
                    act.wait_ge(xT_ready, layer * TT + (4 if j == 0 else TT))
                    n = 512 if j == 0 else T - 512
                    outs = spread(xpa, ps[:, first + j, :], j) if layer != 1 else []
                    if layer in (1, 3):
                        outs.append((xa[:, 512 * j:512 * j + n], ps[:, first + j, 0:n]))
                    for out, in_ in outs:
                        ins = copy(out, in_)
                    ins.then_inc(xa_done, 1)

            act.wait_ge(conv_done, 4)
            copy(x_tok[:, 2:4, :], ps[:, 1, 0:2 * C]).then_inc(x0_act, 1)
            act.wait_ge(conv_done, 7)
            copy(x_tok[0:rows(6), 6, :], ps[0:rows(6), 3, 0:C]).then_inc(x0_act, 1)
            act.wait_ge(pool_set, PREP)
            channels_out(0, 4)
            for g in range(0, G, 2):
                act.wait_ge(kv_ready, g + 1)
                copy(kv0[:, g, :], ps[:, g % 4, 0:2 * C]).then_inc(kv_act, 1)
            act.wait_ge(q0_ready, 2)
            for row in (0, 64):
                ins = copy(q0[row:row + 32, 0, :], ps[row:row + 32, 4:6, 0:HALF])
            ins.then_inc(q0_act, 1)

            def cast_w1(e):
                act.wait_ge(w1_in, 48 * (e + 1))
                wait(act, z_ready, HC * (e - 1))
                copy(w1_hi[:, e % 2, :], w1_raw[:, 0, :]).then_inc(w1_cast, 1)
                copy(w1_tail[:, e % 2, :], w1_raw[:, 1, :]).then_inc(w1_cast, 1)

            def cast_w2(e):
                act.wait_ge(w2_in, 16 * (e + 1))
                wait(act, y_done, HC * (e - 1))
                copy(w2_hi[:, e % 2], w2_raw[:, :, 0:CA]).then_inc(w2_cast, 1)
                copy(w2_tail[:, e % 2, :, 0:CB], w2_raw[:, :, CA:C]).then_inc(w2_cast, 1)

            def a0T_out(r):
                act.wait_ge(a0T_ready, r + 1)
                if r == 0:
                    act.wait_ge(a0T_zero, 1)
                blocks = ps[:, 4 + r % 2, 0:4 * CH].rearrange("p (j h d) -> p j h d", j=4, h=HG0)
                copy(a0T[:, 4 * r:4 * r + 4, :, 0:D0], blocks).then_inc(a0T_done, 1)

            for r in range(4):
                act.wait_ge(s0_shifted, r + 1)
                act.activation(e0[:, r % 2], s0[:, r % 2], ACT.Exp, scale=D0 ** -0.5).then_inc(s0_exp, 1)
                if r >= 1:
                    a0T_out(r - 1)
            a0T_out(3)
            cast_w1(0)
            cast_w2(0)
            act.wait_ge(o0_ready, 1)
            for out, in_ in reorder(2) + reorder(3):
                ins = copy(out, in_)
            ins.then_inc(o0_act, 1)

            channels_out(1, 0)
            def gate_exp(n):
                act.wait_ge(shift_ready, n + 1)
                act.activation(gate_w[:, 2], gate_w[:, 1], ACT.Exp).then_inc(gexp_ready, 1)
            gate_exp(0)
            act.wait_ge(gT_ready, 1)
            copy(gatesT[:, 0:512], ps[0:2 * E, 4, 0:512])
            copy(gatesT[:, 512:T], ps[0:2 * E, 5, 0:T - 512]).then_inc(gT_done, 1)
            for e in range(E):
                act.wait_ge(bc_ready, 2 * e + 1)
                copy(gate_bc[:, e, 0:HALF], ps[:, 4 + 2 * (e % 2), 0:HALF]).then_inc(bc_act, 1)
            for c in range(NCH):
                act.wait_ge(hid_ready, c + 1)
                wait(act, y_done, c - HBUF + 1)
                act.activation(hid_hi[:, c % HBUF, :], hid[:, c % 2, :], ACT.Relu).then_inc(hid_cast, 1)
                e, k = c // HC, c % HC
                if k == 1 and e + 1 < E:
                    cast_w1(e + 1)
                if k == 3 and e + 1 < E:
                    cast_w2(e + 1)
            act.wait_ge(y_done, NCH)
            for n in range(2):
                copy(yT[:, 0, n * HALF:(n + 1) * HALF], ps[:, 4 + n, 0:HALF]).then_inc(yT_act, 1)

            act.wait_ge(wlate_in, 32)
            act.activation(lam_exp[:, :], lam_raw[:, :], ACT.Exp).then_inc(lam_ready, 1)
            channels_out(2, 4)

            def attention(call, kinds, exps):
                act.wait_ge(v_ready, call + 1)
                for i in (2, 3):
                    for h in range(HQ):
                        src = view(ps[32 * i:32 * i + 32, 4, 16 * h:16 * h + 1], [[256, G], [64, 3], [1, 16]])
                        dst = view(v_bd[32 * h:32 * h + 32, i, 0, 16 * h:16 * h + 1], [[IG * C, G], [64, 3], [1, 16]])
                        mm = copy(dst, src)
                mm.then_inc(v_act, 1)
                for n_job, (kind, stack, m) in enumerate(kinds):
                    act.wait_ge(qk_ready, (6 if call else 0) + n_job + 1)
                    src = ps[0:m, 2 * (n_job % 2) + 1, 0:HALF]
                    if kind == "q":
                        copy(qT[0:m, stack, HALF:T], src).then_inc(qk_act, 1)
                    else:
                        for h in range(HQ):
                            mm = act.activation(k_bd[0:m, stack, h, HALF:T], src, ACT.Copy, scale=head_mask1[0:m, h:h + 1])
                        mm.then_inc(qk_act, 1)

                def p1T_out(g):
                    act.wait_ge(p1T_ready, G * call + g + 1)
                    if g >= 2 or call:
                        act.wait_ge(o1_ready, G * call + g - 1)
                    copy(p1T[:, g % 2, :, :], ps[:, 4 + g % 2, 0:384]).then_inc(p1T_done, 1)

                def o_out(g):
                    act.wait_ge(o1_ready, G * call + g + 1)
                    copy(oa[:, GT * g:GT * g + GT], ps[:, 6 + g % 2, 0:GT])
                    copy(ob[0:CB, GT * g:GT * g + GT], ps[0:CB, 6 + g % 2, 128:128 + GT]).then_inc(o1_done, 1)

                for step in range(G + 3):
                    if step < G:
                        act.wait_ge(s1_shifted, G * call + step + 1)
                        act.activation(e1[:, step % 2, 0:exps], s1[:, step % 2, 0:exps], ACT.Exp, scale=D1 ** -0.5).then_inc(s1_exp, 1)
                    if 2 <= step <= G + 1:
                        p1T_out(step - 2)
                    if step >= 3:
                        o_out(step - 3)

            attention(0, [(x, s, 128) for s in range(3) for x in "kq"], 24)
            channels_out(3, 4)
            gate_exp(1)
            act.wait_ge(gT_ready, 2)
            for j in range(2):
                for out, in_ in spread(xpb[96:104], ps[0:E, j, :], j):
                    ins = copy(out, in_)
            ins.then_inc(gT_done, 1)
            for n in range(2):
                act.wait_ge(ce_ready, n + 1)
                copy(ce[:, n * HALF:(n + 1) * HALF], ps[:, 5 + n, 0:HALF]).then_inc(ce_done, 1)
            attention(1, [("k", 0, 128), ("q", 0, 128), ("k", 1, 64), ("q", 1, 64)], 12)

        @block.vector
        def _(dve):
            links = [0]

            def link(ins):
                links[0] += 1
                ins.then_inc(dve_chain, 1)
                dve.wait_ge(dve_chain, links[0])

            def over(ap, n):
                return bass.AP(tensor=ap.tensor, offset=ap.offset, ap=[list(d) for d in ap.ap] + [[0, n]])

            dve.wait_ge(conv_done, 2)
            dve.tensor_copy(x_tok[:, 0:2, :], ps[:, 0, 0:2 * C]).then_inc(x0_dve, 1)
            dve.wait_ge(conv_done, 6)
            dve.tensor_copy(x_tok[:, 4:6, :], ps[:, 2, 0:2 * C]).then_inc(x0_dve, 1)
            def channels_out(layer, first):
                for j in range(2):
                    dve.wait_ge(xT_ready, layer * TT + (4 if j == 0 else TT))
                    n = 512 if j == 0 else T - 512
                    outs = spread(xpb[0:CB], ps[0:CB, first + 2 + j, :], j)
                    if layer == 3:
                        outs.append((xb[0:CB, 512 * j:512 * j + n], ps[0:CB, first + 2 + j, 0:n]))
                    for out, in_ in outs:
                        ins = dve.tensor_copy(out, in_)
                    ins.then_inc(xb_done, 1)
            dve.wait_ge(pool_set, PREP)
            channels_out(0, 4)
            for g in range(1, G, 2):
                dve.wait_ge(kv_ready, g + 1)
                dve.tensor_copy(kv0[:, g, :], ps[:, g % 4, 0:2 * C]).then_inc(kv_dve, 1)
            dve.wait_ge(q0_ready, 2)
            for row in (32, 96):
                ins = dve.tensor_copy(q0[row:row + 32, 1, :], ps[row:row + 32, 4:6, 0:HALF])
            ins.then_inc(q0_dve, 1)

            def shift0(r):
                dve.wait_ge(s0_ready, r + 1)
                src = view(ps[0:CH, 0, 0:1], [[512, IG], [CH, 4], [1, CH]])
                mask = view(head_mask0[:, 0:1], [[0, IG], [0, 4], [1, CH]])
                dve.tensor_tensor(m0[:, :, :].rearrange("p (i j) e -> p i j e", i=IG), src, mask, ALU.mult).then_inc(s0_masked, 1)
                dve.wait_ge(s0_masked, r + 1)
                link(dve.tensor_reduce(s0[:, r % 2], m0[:, :, :].rearrange("p j (h e) -> p j e h", h=HG0), AX.X, ALU.add))
                link(dve.tensor_reduce(st0[:, 0, :], s0[:, r % 2], AX.X, ALU.max))
                dve.tensor_tensor(s0[:, r % 2], s0[:, r % 2], over(st0[:, 0, :], D0), ALU.subtract).then_inc(s0_shifted, 1)

            def norm0(r):
                dve.wait_ge(s0_exp, r + 1)
                link(dve.tensor_reduce(st0[:, 1, :], e0[:, r % 2], AX.X, ALU.add))
                link(dve.reciprocal(st0[:, 2, :], st0[:, 1, :]))
                wait(dve, a0T_ready, r - 1)
                for gg in range(2):
                    part = e0[:, r % 2].rearrange("p (i g a) e -> p i g a e", i=IG, g=2)[:, :, gg]
                    inv = st0[:, 2, :].rearrange("p (i g a) -> p i g a", i=IG, g=2)[:, :, gg]
                    ins = dve.tensor_tensor(a0[:, r % 2, gg, :, :, 0:D0], part, over(inv, D0), ALU.mult)
                ins.then_inc(a0_ready, 1)

            for r in range(5):
                if r < 4:
                    shift0(r)
                if r >= 1:
                    norm0(r - 1)
            def split_w1(e):
                dve.wait_ge(w1_cast, 2 * (e + 1))
                j = e % 2
                dve.tensor_tensor(w1_lo[:, j, :], w1_raw[:, 0, :], w1_hi[:, j, :].bitcast(F32), ALU.subtract).then_inc(w1_split, 1)
                low = w1_tail[CB:128, j, :]
                dve.tensor_tensor(low, w1_raw[CB:128, 1, :], low.bitcast(F32), ALU.subtract).then_inc(w1_split, 1)

            def split_w2(e):
                dve.wait_ge(w2_cast, 2 * (e + 1))
                j = e % 2
                dve.tensor_tensor(w2_lo[:, j], w2_raw[:, :, 0:CA], w2_hi[:, j].bitcast(F32), ALU.subtract).then_inc(w2_split, 1)
                dve.tensor_tensor(w2_tail[:, j, :, CB:2 * CB], w2_raw[:, :, CA:C], w2_tail[:, j, :, 0:CB].bitcast(F32), ALU.subtract).then_inc(w2_split, 1)

            split_w1(0)
            split_w2(0)
            dve.wait_ge(o0_ready, 1)
            for out, in_ in reorder(0) + reorder(1):
                ins = dve.tensor_copy(out, in_)
            ins.then_inc(o0_dve, 1)

            def layernorm(layer, add):
                for half in range(2):
                    ts = range(0, 4) if half == 0 else range(4, TT)
                    for t in ts:
                        n = rows(t)
                        add(t)
                        link(dve.bn_stats(stats[0:n, t, :], h_tok[0:n, t, :]))
                        link(dve.bn_aggr(mv[0:n, t, :], stats[0:n, t, :]))
                    cut = slice(ts[0], ts[-1] + 1)
                    dve.tensor_scalar(veps[:, cut], mv[:, cut, 1], EPS, None, ALU.add).then_inc(veps_ready, 1)
                for half in range(2):
                    ts = range(0, 4) if half == 0 else range(4, TT)
                    dve.wait_ge(rstd_ready, 2 * layer + half + 1)
                    for t in ts:
                        n = rows(t)
                        dve.tensor_scalar(x_tok[0:n, t, :], h_tok[0:n, t, :], mv[0:n, t, 0:1], rstd[0:n, t:t + 1],
                                          ALU.subtract, ALU.mult).then_inc(x_ready, 1)

            def from_proj(layer, first, res):
                def add(t):
                    dve.wait_ge(proj_ready, layer * TT + min(t + 2 - t % 2, TT))
                    ins = dve.tensor_tensor(h_tok[0:rows(t), t, :], tok_bank(first, t), res[0:rows(t), t, :], ALU.add)
                    if t % 2 or t == TT - 1:
                        ins.then_inc(summed, 1)
                        dve.wait_ge(summed, 4 * layer + t // 2 + 1)
                    else:
                        link(ins)
                return add

            layernorm(0, from_proj(0, 4, x_tok))

            for j in range(2):
                n = 512 if j == 0 else T - 512
                cols = slice(512 * j, 512 * j + n)
                dve.wait_ge(xT_ready, TT + (4 if j == 0 else TT))
                tail = ps[0:CB, 2 + j, 0:n]
                dve.tensor_copy(xb[0:CB, cols], tail).then_inc(xb_done, 1)
                dve.tensor_copy(xt_hi[CB:128, cols], tail)
                link(dve.tensor_copy(xt_hi[0:CB, cols], tail))
                dve.tensor_tensor(xt_lo[:, cols], tail, xt_hi[0:CB, cols].bitcast(F32), ALU.subtract).then_inc(x_split, 1)
            for j in range(2):
                n = 512 if j == 0 else T - 512
                cols = slice(512 * j, 512 * j + n)
                dve.wait_ge(xa_done, 3 + j)
                link(dve.tensor_copy(x_hi[:, cols], xa[:, cols]))
                dve.tensor_tensor(x_lo[:, cols], xa[:, cols], x_hi[:, cols].bitcast(F32), ALU.subtract).then_inc(x_split, 1)

            def gating(n, factor):
                W = lambda k: gate_w[:, k]
                S = lambda k: gate_s[:, k]
                grid = view(iota8[:, 0:1], [[0, TT], [1, E]])
                dve.wait_ge(logits_ready, n + 1)
                dve.tensor_copy(W(0), ps[:, 4, 0:TT * E].rearrange("p (t e) -> p t e", e=E)).then_inc(logits_read, 1)
                dve.wait_ge(logits_read, n + 1)
                link(dve.tensor_reduce(S(0), W(0), AX.X, ALU.max))
                dve.tensor_tensor(W(1), W(0), over(S(0), E), ALU.subtract).then_inc(shift_ready, 1)
                for pick in range(2):
                    src, top, hot = W(0) if pick == 0 else W(5), S(pick), W(3 + pick)
                    if pick:
                        link(dve.scalar_tensor_tensor(W(5), W(3), -3.0e38, W(0), ALU.mult, ALU.add))
                        link(dve.tensor_reduce(S(1), W(5), AX.X, ALU.max))
                    link(dve.tensor_tensor(W(6), src, over(top, E), ALU.is_equal))
                    link(dve.tensor_tensor(W(7), W(6), grid, ALU.mult))
                    link(dve.tensor_reduce(S(2 + pick), W(7), AX.X, ALU.min))
                    link(dve.tensor_tensor(hot, grid, over(S(2 + pick), E), ALU.is_equal))
                link(dve.tensor_tensor(W(6), W(3), W(4), ALU.add))
                dve.wait_ge(gexp_ready, n + 1)
                link(dve.tensor_reduce(S(4), W(2), AX.X, ALU.add))
                link(dve.reciprocal(S(5), S(4)))
                link(dve.tensor_tensor(W(7), W(2), over(S(5), E), ALU.mult))
                dve.scalar_tensor_tensor(gates[:, :, :], W(7), factor, W(6), ALU.mult, ALU.mult).then_inc(gates_ready, 1)

            gating(0, 1.0)
            dve.wait_ge(gates_ready, 1)
            parts = gate_hl[:, :, :].bitcast(F32R)
            dve.tensor_copy(parts[:, :, 0:E], gates[:, :, :]).then_inc(gate_parts, 1)
            dve.wait_ge(gate_parts, 1)
            dve.tensor_tensor(parts[:, :, E:2 * E], gates[:, :, :], gate_hl[:, :, 0:E], ALU.subtract).then_inc(gate_parts, 1)
            dve.tensor_copy(bc_sel[:, :, :], over(expert_sel, 128)).then_inc(sel_ready, 1)
            for e in range(E):
                dve.wait_ge(bc_ready, 2 * e + 2)
                dve.tensor_copy(gate_bc[:, e, HALF:T], ps[:, 5 + 2 * (e % 2), 0:HALF]).then_inc(bc_dve, 1)

            def weigh(c):
                dve.wait_ge(z_ready, c + 1)
                if c == 0:
                    dve.wait_ge(bc_act, E)
                    dve.wait_ge(bc_dve, E)
                wait(dve, hid_cast, c - 1)
                wait(dve, hid_split, c - 1)
                gate = gate_bc[:, c // HC, :].rearrange("p (n t) -> p n t", n=2)
                dve.scalar_tensor_tensor(hid[:, c % 2, :].rearrange("p (n t) -> p n t", n=2), ps[:, 2 * (c % 2):2 * (c % 2) + 2, 0:HALF],
                                         b1c[:, c:c + 1], gate, ALU.add, ALU.mult).then_inc(hid_ready, 1)

            def split_hid(c):
                dve.wait_ge(hid_cast, c + 1)
                dve.scalar_tensor_tensor(hid_lo[:, c % HBUF, :], hid[:, c % 2, :], 0.0, hid_hi[:, c % HBUF, :].bitcast(F32),
                                         ALU.max, ALU.subtract).then_inc(hid_split, 1)

            weigh(0)
            for c in range(NCH):
                e, k = c // HC, c % HC
                if c + 1 < NCH:
                    weigh(c + 1)
                split_hid(c)
                if k == 2 and e + 1 < E:
                    split_w1(e + 1)
                if k == 4 and e + 1 < E:
                    split_w2(e + 1)
            dve.wait_ge(y_done, NCH)
            for n in range(2):
                dve.tensor_copy(yT[:, 1, n * HALF:(n + 1) * HALF], ps[:, 6 + n, 0:HALF]).then_inc(yT_dve, 1)
            layernorm(1, from_proj(1, 0, x_tok))
            channels_out(2, 4)

            dve.wait_ge(lam_ready, 1)
            dve.wait_ge(vbd_zero, 6)
            for bank, slot, h in ((0, 1, 0), (1, 1, 4), (1, 2, 8)):
                link(dve.tensor_scalar(lam[:, bank, slot, :], lam_exp[:, h:h + HQ], -1.0, None, ALU.mult))

            def attention(call, kinds, two_sets):
                dve.wait_ge(v_ready, call + 1)
                for i in (0, 1):
                    for h in range(HQ):
                        src = view(ps[32 * i:32 * i + 32, 4, 16 * h:16 * h + 1], [[256, G], [64, 3], [1, 16]])
                        dst = view(v_bd[32 * h:32 * h + 32, i, 0, 16 * h:16 * h + 1], [[IG * C, G], [64, 3], [1, 16]])
                        ins = dve.tensor_copy(dst, src)
                ins.then_inc(v_dve, 1)
                for n_job, (kind, stack, m) in enumerate(kinds):
                    dve.wait_ge(qk_ready, (6 if call else 0) + n_job + 1)
                    src = ps[0:m, 2 * (n_job % 2), 0:HALF]
                    if kind == "q":
                        dve.tensor_copy(qT[0:m, stack, 0:HALF], src).then_inc(qk_dve, 1)
                    else:
                        dve.tensor_tensor(k_bd[0:m, stack, :, 0:HALF], view(src, [[0, HQ], [1, HALF]]),
                                          over(head_mask1[0:m, :], HALF), ALU.mult).then_inc(qk_dve, 1)

                def shift(g):
                    n = G * call + g
                    dve.wait_ge(s1_ready, n + 1)
                    first = 2 * (g % 2)
                    if two_sets:
                        parts = [(0, 24, view(ps[:, first, 0:1], [[512, 2], [N, 12], [1, N]]))]
                    else:
                        parts = [(0, 8, view(ps[:, first, 0:1], [[N, 8], [1, N]])), (8, 12, view(ps[:, first + 1, 0:1], [[N, 4], [1, N]]))]
                    for a, b, src in parts:
                        top = st1[:, g % 2, 0, a:b]
                        s = s1[:, g % 2, a:b, :]
                        if two_sets:
                            top2 = top.rearrange("p (a b) -> p a b", a=2)
                            s = s.rearrange("p (a b) m -> p a b m", a=2)
                        else:
                            top2 = top
                        link(dve.tensor_reduce(top2, src, AX.X, ALU.max))
                        ins = dve.tensor_tensor(s, src, over(top2, N), ALU.subtract)
                    ins.then_inc(s1_shifted, 1)

                def norm(g):
                    n = G * call + g
                    k = 24 if two_sets else 12
                    dve.wait_ge(s1_exp, n + 1)
                    e = e1[:, g % 2, 0:k, :]
                    total, inv, coef = (st1[:, g % 2, j, 0:k] for j in (1, 2, 3))
                    link(dve.tensor_reduce(total, e, AX.X, ALU.add))
                    link(dve.reciprocal(inv, total))
                    if g >= 2 or call:
                        dve.wait_ge(p1T_ready, n - 1)
                    p = p1[:, g % 2]
                    if two_sets:
                        link(dve.tensor_tensor(coef, inv, lam[:, :, :, :].rearrange("p a b c -> p (a b c)"), ALU.mult))
                        link(dve.tensor_tensor(e, e, over(coef, N), ALU.mult))
                        blk = e.rearrange("p (a b c) m -> p a b c m", a=2, b=3)
                        dve.tensor_tensor(p[:, 0:2, :, 0:N], blk[:, :, 0], blk[:, :, 1], ALU.add)
                        dve.tensor_tensor(p[:, 2, :, 0:N], blk[:, 0, 2], blk[:, 1, 2], ALU.add).then_inc(p1_ready, 1)
                    else:
                        dve.tensor_tensor(view(p[:, 0, 0, 0:1], [[256, 2], [32, HQ], [1, N]]),
                                          e[:, 0:8].rearrange("p (a b) m -> p a b m", a=2),
                                          over(inv[:, 0:8].rearrange("p (a b) -> p a b", a=2), N), ALU.mult)
                        dve.tensor_tensor(p[:, 1, :, 0:N], e[:, 8:12], over(inv[:, 8:12], N), ALU.mult).then_inc(p1_ready, 1)

                for step in range(G + 1):
                    if step < G:
                        shift(step)
                    if step >= 1:
                        norm(step - 1)

            attention(0, [(x, s, 128) for s in range(3) for x in "kq"], True)
            layernorm(2, from_proj(2, 0, x_tok))
            channels_out(3, 4)
            gating(1, ADAPT)
            for n in range(2):
                dve.wait_ge(ha_ready, n + 1)
                dve.wait_ge(ce_done, n + 1)
                by_image = lambda x: x.rearrange("p (b n) -> p b n", n=N)
                dve.tensor_tensor(view(hwT[:, 512 * n:512 * n + 1], [[32, B // 2], [1, N]]), by_image(ps[:, 2 + n, 0:HALF]),
                                  by_image(ce[:, n * HALF:(n + 1) * HALF]), ALU.mult).then_inc(hw_done, 1)
            attention(1, [("k", 0, 128), ("q", 0, 128), ("k", 1, 64), ("q", 1, 64)], False)
            layernorm(3, from_proj(3, 0, x_tok))


def kernel(**inputs):
    import numpy as np
    import concourse.bacc as bacc
    from concourse.bass_utils import run_bass_kernel_spmd as run

    a = {k: np.asarray(v) for k, v in inputs.items()}
    crop = NB * PATCH
    x = a["x"][:, :, :crop, :crop].reshape(B, CIN, NB, PATCH, NB, PATCH)
    tok = np.arange(T)
    row = np.arange(128)
    at = np.arange(NB) * SIDE // NB
    pos = a["L0_tok_pos_table"].reshape(SIDE, SIDE, C)[at][:, at].reshape(N, C)

    def stacked(w):
        w = w.reshape(C, 2, C)
        return np.concatenate([w[:, 0, :128], w[:, 1, :128], w[:, 0, 128:], w[:, 1, 128:]], axis=1)

    def pack(rows, cols, parts):
        out = np.zeros((rows, sum(w for _, w in cols)), np.float32)
        c = 0
        for name, width in cols:
            for r, v in parts[name]:
                out[r:r + v.shape[0], c:c + width] = v
            c += width
        return out

    wq0 = np.zeros((C, 2, 2, 32), np.float32)
    wq0[:, :, :, :D0] = a["L0_attn_Wq"].reshape(C, 1, 2, D0)
    wp0 = np.zeros((4, 32, 2, C), np.float32)
    wp0[:, :D0] = a["L0_attn_Wproj"].reshape(2, 4, D0, C).transpose(1, 2, 0, 3)
    full = {
        "wkv0": a["L0_attn_Wkv"], "wq0": wq0.reshape(C, 128), "wg0": a["L0_ffn_Wg"],
        "wq1": stacked(a["L1_attn_Wq"]), "wk1": stacked(a["L1_attn_Wk"]), "wv1": a["L1_attn_Wv"],
        "wo1": a["L1_attn_Wo"], "wg2": a["L1_ffn_Wg"].T, "wa2": a["L1_ffn_A"].reshape(E * R, C).T,
        "wqkv": a["L1_ffn_Wqkv"].T, "wp2": a["L1_ffn_Wproj"].T,
    }
    bias = {"wo1": a["L1_attn_bo"], "wg2": a["L1_ffn_bg"], "wa2": a["L1_ffn_ba"].reshape(-1),
            "wqkv": a["L1_ffn_bqkv"], "wp2": a["L1_ffn_bproj"]}
    top = {k: [(0, v[:CA])] for k, v in full.items()}
    low = {k: [(0, v[CA:])] + ([(CB, bias[k][None])] if k in bias else []) for k, v in full.items()}
    top["wp0"] = [(0, wp0.reshape(128, 2 * C))]
    top["b1c"] = [(0, a["L0_ffn_b1"].reshape(NCH, 128).T)]
    top["lam"] = [(0, np.broadcast_to(a["L1_attn_lambda_p"].reshape(1, H1), (128, H1)))]
    top["wbm"] = [(0, a["L1_ffn_Bm"].transpose(0, 2, 1).reshape(E * R, 3 * C))]
    low["bp0"] = [(CB, a["L0_attn_bproj"][None])]
    low["b2"] = [(0, a["L0_ffn_b2"]), (E, a["L0_ffn_b2"])]
    low["wqkv"].append((96, a["L1_ffn_bb"]))
    consts = {
        "ident": [(0, np.eye(128))],
        "mask0": [(0, row[:CH, None] // D0 == row[None, :CH] // D0)],
        "mask1": [(0, row[:, None] % 64 // D1 == np.arange(HQ)[None, :])],
        "expert_rows": [(96, np.arange(E)[:, None] == row[None, :] // R)],
        "expert_sel": [(0, np.arange(2 * E)[:, None] % E == np.arange(E)[None, :])],
        "fold": [(0, row[:, None] % CB == np.arange(CB)[None, :])],
        "iota8": [(0, np.tile(np.arange(E) - E, (128, 1)))],
    }
    sel = np.concatenate([np.arange(N)[:, None] == tok[None, :] % N, np.ones((1, T), bool)]).astype(np.float32)
    arrays = {
        "pat": np.concatenate([x.transpose(1, 3, 5, 0, 2, 4).reshape(KP, T),
                               a["L0_tok_conv_w"].reshape(C, KP).T], axis=1),
        "pos_sel": np.concatenate([np.concatenate([pos, a["L0_tok_conv_b"][None]]), sel], axis=1),
        "consts": pack(128, CONSTS, consts),
        "w0a": pack(128, W0A, top), "w0b": pack(CB + 1, W0B, low),
        "w1a": pack(128, W1A, top), "w1b": pack(104, W1B, low),
        "w1": a["L0_ffn_W1"], "w2": a["L0_ffn_W2"],
    }
    nc = bacc.Bacc("TRN2", target_bir_lowering=False, num_devices=1)
    io, feed = {}, {}
    for name, v in arrays.items():
        feed[f"in_{name}"] = np.ascontiguousarray(v)
        io[name] = nc.dram_tensor(f"in_{name}", v.shape, F32, kind="ExternalInput").ap()
    io["out"] = nc.dram_tensor("out", (T, C), F32, kind="ExternalOutput").ap()
    build(nc, io)
    r = run(nc, [feed], core_ids=[0])
    return r.results[0]["out"].reshape(B, N, C)
```

```python
from contextlib import ExitStack

import concourse.bass as bass
from concourse import mybir

F32 = mybir.dt.float32
F32R = mybir.dt.float32r
ALU = mybir.AluOpType
ACT = mybir.ActivationFunctionType
AX = mybir.AxisListType

B, CIN, IMG, PATCH = 32, 3, 84, 16
SIDE = 32
NB = IMG // PATCH
N = NB * NB
T = B * N
C = 192
CA, CB = 128, C - 128
KP = CIN * PATCH * PATCH
KCH = KP // 128
TT = (T + 127) // 128
TP = TT * 128
PAIRS = (TT + 1) // 2
IG = 4
G = B // IG
GT = IG * N
HALF = T // 2
EPS = 1e-5
E, HID = 8, 768
HC = HID // 128
NCH = E * HC
H0, D0 = 8, 24
HG0 = H0 // 2
CH = HG0 * D0
KV = 2 * 128 + C
H1, D1 = 12, 16
HQ = 4
R = 16
ADAPT = 2.0
HBUF = 3

CONSTS = [("ident", 128), ("mask1", HQ), ("expert_rows", 128), ("iota8", E), ("expert_sel", E), ("fold", CB)]
W0A = [("wkv0", KV), ("wq0", 128), ("wp0", 2 * C), ("wg0", E), ("b1c", NCH)]
W0B = [("wkv0", KV), ("wq0", 128), ("bp0", C), ("wg0", E), ("b2", C)]
W1A = [("wq1", 2 * C), ("wk1", 2 * C), ("wv1", C), ("wo1", C), ("lam", H1), ("wa2", 128),
       ("wqkv", 3 * C), ("wg2", E), ("wbm", 3 * C), ("wp2", C)]
W1B = [("wq1", 2 * C), ("wk1", 2 * C), ("wv1", C), ("wo1", C), ("wg2", E), ("wa2", 128), ("wqkv", 3 * C), ("wp2", C)]


def rows(t):
    return min(128, T - 128 * t)


def view(ap, dims):
    return bass.AP(tensor=ap.tensor, offset=ap.offset, ap=[list(ap.ap[0])] + [list(d) for d in dims])


def build(nc, io):
    with ExitStack() as ctx:
        def sb(name, shape, dt=F32, scope=ctx):
            return scope.enter_context(nc.sbuf_tensor(name, shape, dt))

        def sem(name):
            return ctx.enter_context(nc.semaphore(name))

        ps = ctx.enter_context(nc.psum_tensor("ps", [128, 8, 512], F32))

        consts = sb("consts", [128, sum(w for _, w in CONSTS)])
        w0a, w0b = (sb(n, [r, sum(w for _, w in cols)]) for n, r, cols in (("w0a", 128, W0A), ("w0b", CB + 1, W0B)))
        w1a, w1b = (sb(n, [r, sum(w for _, w in cols)]) for n, r, cols in (("w1a", 128, W1A), ("w1b", 104, W1B)))

        def col(pack, cols, name, r0=0, r1=None):
            at = 0
            for n, width in cols:
                if n == name:
                    return pack[r0:r1 if r1 else pack.shape[0], at:at + width]
                at += width
            raise KeyError(name)

        ident = col(consts, CONSTS, "ident")
        head_mask1 = col(consts, CONSTS, "mask1")
        expert_rows = col(consts, CONSTS, "expert_rows", 96, 104)
        iota8 = col(consts, CONSTS, "iota8")
        expert_sel = col(consts, CONSTS, "expert_sel", 0, 2 * E)
        fold = col(consts, CONSTS, "fold")
        wkv0a, wkv0b = col(w0a, W0A, "wkv0"), col(w0b, W0B, "wkv0", 0, CB)
        wq0a, wq0b = col(w0a, W0A, "wq0"), col(w0b, W0B, "wq0", 0, CB)
        wp0 = col(w0a, W0A, "wp0").rearrange("p (s c) -> p s c", s=2)
        bp0 = col(w0b, W0B, "bp0", CB, CB + 1)
        wg0a, wg0b = col(w0a, W0A, "wg0"), col(w0b, W0B, "wg0", 0, CB)
        b1c = col(w0a, W0A, "b1c")
        b2r = col(w0b, W0B, "b2", 0, 2 * E)
        wqk1a, wqk1b = w1a[:, 0:4 * C], w1b[0:CB, 0:4 * C]
        wv1a, wv1b = col(w1a, W1A, "wv1"), col(w1b, W1B, "wv1", 0, CB)
        wo1a, wo1b = col(w1a, W1A, "wo1"), col(w1b, W1B, "wo1", 0, CB + 1)
        lam_raw = col(w1a, W1A, "lam")
        wg2b = col(w1b, W1B, "wg2", 0, CB + 1)
        wa2a, wa2b = col(w1a, W1A, "wa2"), col(w1b, W1B, "wa2", 0, CB + 1)
        wqkva, wqkvb = col(w1a, W1A, "wqkv"), col(w1b, W1B, "wqkv")
        wbm = col(w1a, W1A, "wbm")
        at_v = sum(w for _, w in W1A[:6]) + 2 * C
        wvg2a = w1a[:, at_v:at_v + C + E]
        wp2a, wp2b = col(w1a, W1A, "wp2"), col(w1b, W1B, "wp2", 0, CB + 1)
        lam_exp = sb("lam_exp", [128, H1])
        lam = sb("lam", [128, 2, 3, HQ])
        neg_half = sb("neg_half", [128, TT])

        x_tok = sb("x_tok", [128, TT, C])
        h_tok = sb("h_tok", [128, TT, C])
        stats = sb("stats", [128, TT, 6])
        mv = sb("mv", [128, TT, 2])
        veps = sb("veps", [128, TT])
        rstd = sb("rstd", [128, TT])
        xa = sb("xa", [CA, TP])
        xb = sb("xb", [CB + 1, TP])
        xpa = sb("xpa", [CA, 32 * B])
        xpb = sb("xpb", [104, 32 * B])
        gate_w = sb("gate_w", [128, 8, G, E])
        gate_s = sb("gate_s", [128, 6, G])
        gates = sb("gates", [128, G, E])
        gate_hl = sb("gate_hl", [128, TT, 2 * E])
        gatesT = sb("gatesT", [2 * E, T], F32R)

        early = ExitStack()
        k0 = sb("k0", [128, G, 256], scope=early)
        v0 = sb("v0", [128, G, IG, C], scope=early)
        q0 = sb("q0", [128, 2, 2, B // 2, N], scope=early)
        st0 = sb("st0", [128, 3, 16], scope=early)
        a0 = sb("a0", [128, 2, 2, IG, 2, 32], scope=early)
        o0 = sb("o0", [128, 2 * T], scope=early)
        s0 = sb("s0", [128, 2, 16, D0], scope=early)
        e0 = sb("e0", [128, 2, 16, D0], scope=early)
        a0T = sb("a0T", [128, 16, 128], scope=early)
        early.close()
        late = ExitStack()
        v_bd = sb("v_bd", [128, B, 3, 64], scope=late)
        p1 = sb("p1", [128, 2, 3, HQ, 32], scope=late)
        ob = sb("ob", [CB + 1, T], scope=late)
        hwT = sb("hwT", [128, 32 * B], scope=late)
        with ExitStack() as moe:
            gate_bc = sb("gate_bc", [128, 2, T], scope=moe)
            bc_sel = sb("bc_sel", [2 * E, E, 128], F32R, scope=moe)
            wqk_hi = sb("wqk_hi", [128, 4 * C], F32R, scope=moe)
            wqk_lo = sb("wqk_lo", [128, 4 * C], F32R, scope=moe)
            wqk_tail = sb("wqk_tail", [128, 4 * C], F32R, scope=moe)
        s1 = sb("s1", [128, 2, 24, N], scope=late)
        e1 = sb("e1", [128, 2, 24, N], scope=late)
        st1 = sb("st1", [128, 2, 4, 24], scope=late)
        p1T = sb("p1T", [128, 2, 3, 128], scope=late)
        oa = sb("oa", [CA, T], scope=late)
        sb("beside_wqk", [128, 4 * C], scope=late)
        qT = sb("qT", [128, 3, T + 8], scope=late)
        late.close()
        sb("region_one", [128, 16120])

        ffn = ExitStack()
        w1_raw = sb("w1_raw", [128, 2, HID], scope=ffn)
        w2_raw = sb("w2_raw", [128, HC, C], scope=ffn)
        w1_hi = sb("w1_hi", [128, 2, HID], F32R, scope=ffn)
        w1_lo = sb("w1_lo", [128, 2, HID], F32R, scope=ffn)
        w1_tail = sb("w1_tail", [128, 2, HID], F32R, scope=ffn)
        w2_hi = sb("w2_hi", [128, 2, HC, CA], F32R, scope=ffn)
        w2_lo = sb("w2_lo", [128, 2, HC, CA], F32R, scope=ffn)
        w2_tail = sb("w2_tail", [128, 2, HC, 2 * CB], F32R, scope=ffn)
        with ExitStack() as first:
            pat = sb("pat", [128, KCH, T + C], scope=first)
            pos_sel = sb("pos_sel", [N + 1, C + T], scope=first)
            posb, sel = pos_sel[:, 0:C], pos_sel[:, C:]
        x_hi = sb("x_hi", [CA, T], F32R, scope=ffn)
        x_lo = sb("x_lo", [CA, T], F32R, scope=ffn)
        xt_hi = sb("xt_hi", [128, T], F32R, scope=ffn)
        xt_lo = sb("xt_lo", [CB, T], F32R, scope=ffn)
        hid = sb("hid", [128, 2, T], scope=ffn)
        hid_hi = sb("hid_hi", [128, HBUF, T], F32R, scope=ffn)
        hid_lo = sb("hid_lo", [128, HBUF, T], F32R, scope=ffn)
        ffn.close()
        yT = hid
        k_bd = sb("k_bd", [128, 3, HQ, T])

        patch_in = [sem(f"patch_in{k}") for k in range(KCH)]
        const_in = sem("const_in")
        w0_in = sem("w0_in")
        wlate_in = sem("wlate_in")
        w1_in, w2_in = sem("w1_in"), sem("w2_in")
        out_sent = sem("out_sent")
        pool_set = sem("pool_set")
        vbd_zero = sem("vbd_zero")
        conv_done = sem("conv_done")
        x0_act, x0_dve = sem("x0_act"), sem("x0_dve")
        xT_ready = sem("xT_ready")
        xa_done, xb_done = sem("xa_done"), sem("xb_done")
        kv_ready = sem("kv_ready")
        kv_act, kv_dve = sem("kv_act"), sem("kv_dve")
        q0_ready = sem("q0_ready")
        q0_act, q0_dve = sem("q0_act"), sem("q0_dve")
        s0_ready, s0_act, s0_dve = sem("s0_ready"), sem("s0_act"), sem("s0_dve")
        s0_shifted, s0_exp, a0_ready = sem("s0_shifted"), sem("s0_exp"), sem("a0_ready")
        a0T_ready, a0T_done = sem("a0T_ready"), sem("a0T_done")
        o0_ready, o0_act, o0_dve = sem("o0_ready"), sem("o0_act"), sem("o0_dve")
        first_split = sem("first_split")
        proj_ready = sem("proj_ready")
        summed = sem("summed")
        veps_ready, rstd_ready = sem("veps_ready"), sem("rstd_ready")
        x_ready = sem("x_ready")
        dve_chain = sem("dve_chain")
        x_cast, x_split, x_twice = sem("x_cast"), sem("x_split"), sem("x_twice")
        logits_ready, logits_read = sem("logits_ready"), sem("logits_read")
        shift_ready, gexp_ready, gates_ready = sem("shift_ready"), sem("gexp_ready"), sem("gates_ready")
        gT_ready, gT_done = sem("gT_ready"), sem("gT_done")
        gT_dve = sem("gT_dve")
        w1_cast, w2_cast = sem("w1_cast"), sem("w2_cast")
        w1_split, w2_split = sem("w1_split"), sem("w2_split")
        z_ready, hid_ready, hid_cast, hid_split = sem("z_ready"), sem("hid_ready"), sem("hid_cast"), sem("hid_split")
        gate_parts = sem("gate_parts")
        wqk_cast, wqk_split = sem("wqk_cast"), sem("wqk_split")
        bc_ready, bc_act, bc_dve = sem("bc_ready"), sem("bc_act"), sem("bc_dve")
        sel_ready = sem("sel_ready")
        y_done, yT_act, yT_dve = sem("y_done"), sem("yT_act"), sem("yT_dve")
        lam_ready = sem("lam_ready")
        v_ready, v_act, v_dve = sem("v_ready"), sem("v_act"), sem("v_dve")
        qk_ready, qk_act, qk_dve = sem("qk_ready"), sem("qk_act"), sem("qk_dve")
        s1_ready, s1_shifted, s1_exp = sem("s1_ready"), sem("s1_shifted"), sem("s1_exp")
        p1_ready, p1T_ready, p1T_done = sem("p1_ready"), sem("p1T_ready"), sem("p1T_done")
        o1_ready, o1_done = sem("o1_ready"), sem("o1_done")
        ce_ready, ha_ready, ha_done, hw_done = sem("ce_ready"), sem("ha_ready"), sem("ha_done"), sem("hw_done")

        def wait(eng, s, value):
            if not isinstance(value, int) or value > 0:
                eng.wait_ge(s, value)

        def tok_bank(first, t):
            return ps[0:rows(t), first + t // 2, (t % 2) * C:(t % 2) * C + C]

        def spread(dst, src, j):
            whole = 512 // N
            cut = 512 - whole * N
            if j == 0:
                return [(view(dst[:, 0:1], [[32, whole], [1, N]]), view(src[:, 0:1], [[N, whole], [1, N]])),
                        (dst[:, 32 * whole:32 * whole + cut], src[:, whole * N:512])]
            rest = N - cut
            return [(dst[:, 32 * whole + cut:32 * whole + N], src[:, 0:rest]),
                    (view(dst[:, 32 * (whole + 1):32 * (whole + 1) + 1], [[32, B - whole - 1], [1, N]]),
                     view(src[:, rest:rest + 1], [[N, B - whole - 1], [1, N]]))]

        def dense(x):
            return x.rearrange("p (b n) -> p b n", n=N)

        def unpadded(x):
            return view(x[:, 0:1], [[32, B], [1, N]])

        QK_ORDER = [("q", 0), ("k", 0), ("q", 1), ("k", 1), ("k", 2), ("q", 2)]

        def adapted(n):
            return view(hwT[:, 512 * n:512 * n + 1], [[32, B // 2], [1, N]])

        def z_bank(c):
            return 2 * ((c + min((c + 1) // HC, E - 1)) % 2)

        def bc_bank(e):
            return 2 * ((HC * e - 1 + e - 1) % 2)

        def queries_out(quad):
            par, a = quad // 2, quad % 2
            r = slice(32 * quad, 32 * quad + 32)
            return (q0[r, par, a, :, :].rearrange("p (n b) t -> p n b t", n=2),
                    view(ps[r, 4, N * par:N * par + 1], [[512, 2], [2 * N, B // 4], [1, N]]))

        def heads_out(h, r):
            return (s0[32 * h:32 * h + 32, r % 2].rearrange("p (j i) e -> p j i e", i=IG),
                    view(ps[32 * h:32 * h + 32, 0, D0 * h:D0 * h + 1], [[512, 4], [CH, IG], [1, D0]]))

        def reorder(h, half):
            pairs = []
            for a in range(2):
                first = (2 * h + a) * N
                for r in range(4):
                    n0 = (r - first) % 4
                    count = len(range(n0, N, 4))
                    src = ps[32 * h:32 * h + 32, O0_BANK[half], a * N + n0:a * N + n0 + 1]
                    at = 2 * HALF * half + (first + n0) // 4
                    dst = o0[32 * r:32 * r + 32, at:at + 1]
                    pairs.append((view(dst, [[16 * N, 2], [2 * N, B // 4], [1, count]]),
                                  view(src, [[512, 2], [2 * N, B // 4], [4, count]])))
            return pairs

        O0_BANK = [6, 0]

        block = ctx.enter_context(nc.Block())

        @block.sync
        def _(sp):
            def load(dst, src, s):
                sp.dma_start(dst, src).then_inc(s, 16)
                return 16

            for k in range(KCH):
                load(pat[:, k, :], io["pat"][128 * k:128 * k + 128, :], patch_in[k])
            load(pos_sel[:, :], io["pos_sel"], const_in)
            load(consts[:, :], io["consts"], const_in)
            load(w0a[:, :], io["w0a"], w0_in)
            load(w0b[:, :], io["w0b"], w0_in)

            def load_expert(e):
                wait(sp, w1_cast, 2 * e)
                if e == 1:
                    sp.wait_ge(first_split, 4)
                wait(sp, w1_split, 2 * e - 2)
                load(w1_raw[:, 0, :], io["w1"][e, 0:CA, :], w1_in)
                load(w1_raw[0:CB, 1, :], io["w1"][e, CA:C, :], w1_in)
                load(w1_raw[CB:128, 1, :], io["w1"][e, CA:C, :], w1_in)
                wait(sp, w2_cast, 2 * e)
                wait(sp, w2_split, 2 * e - 2)
                load(w2_raw[:, :, :], io["w2"][e].rearrange("(k p) c -> p k c", p=128), w2_in)

            load_expert(0)
            load(w1a[:, :], io["w1a"], wlate_in)
            load(w1b[:, :], io["w1b"], wlate_in)
            for e in range(1, E):
                load_expert(e)
            for t in range(TT):
                sp.wait_ge(x_ready, 3 * TT + t + 1)
                load(io["out"][128 * t:128 * t + rows(t), :], x_tok[0:rows(t), t, :], out_sent)
            sp.wait_ge(out_sent, 16 * TT)

        @block.gpsimd
        def _(pool):
            count = {}

            def fill(ap, value, s):
                pool.memset(ap, value).then_inc(s, 1)
                count[s] = count.get(s, 0) + 1
                pool.wait_ge(s, count[s])

            fill(xpa[:, :], 0.0, pool_set)
            fill(xpb[:, :], 0.0, pool_set)
            fill(xa[:, T:TP], 0.0, pool_set)
            fill(xb[0:CB, T:TP], 0.0, pool_set)
            fill(a0[:, :, :, :, :, D0:32], 0.0, pool_set)
            fill(q0[:, :, :, :, :], 0.0, pool_set)
            fill(v0[:, :, :, :], 0.0, pool_set)
            fill(mv[:, :, :], 1.0, pool_set)
            fill(neg_half[:, :], -0.5, pool_set)
            fill(xb[CB:CB + 1, :], 1.0, pool_set)
            fill(xpb[CB:CB + 1, :], 1.0, pool_set)

            def rsqrt(layer):
                for pair in range(PAIRS):
                    ts = slice(2 * pair, min(2 * pair + 2, TT))
                    pool.wait_ge(veps_ready, PAIRS * layer + pair + 1)
                    pool.tensor_tensor(rstd[:, ts], veps[:, ts], neg_half[:, ts], ALU.pow).then_inc(rstd_ready, 1)
                    pool.wait_ge(rstd_ready, PAIRS * layer + pair + 1)

            pool.wait_ge(w1_cast, 2)
            pool.tensor_tensor(w1_lo[:, 0, :], w1_raw[:, 0, :], w1_hi[:, 0, :].bitcast(F32), ALU.subtract).then_inc(first_split, 1)
            pool.wait_ge(first_split, 1)
            low = w1_tail[CB:128, 0, :]
            pool.tensor_tensor(low, w1_raw[CB:128, 1, :], low.bitcast(F32), ALU.subtract).then_inc(first_split, 1)
            pool.wait_ge(first_split, 2)
            pool.wait_ge(w2_cast, 2)
            pool.tensor_tensor(w2_lo[:, 0], w2_raw[:, :, 0:CA], w2_hi[:, 0].bitcast(F32), ALU.subtract).then_inc(first_split, 1)
            pool.wait_ge(first_split, 3)
            pool.tensor_tensor(w2_tail[:, 0, :, CB:2 * CB], w2_raw[:, :, CA:C], w2_tail[:, 0, :, 0:CB].bitcast(F32), ALU.subtract).then_inc(first_split, 1)
            pool.wait_ge(first_split, 4)
            rsqrt(0)
            for j, cols in enumerate((slice(0, 512), slice(512, T))):
                pool.wait_ge(xb_done, 3 + j)
                pool.tensor_copy(xt_hi[CB:128, cols], xb[0:CB, cols]).then_inc(x_twice, 1)
                pool.wait_ge(x_twice, j + 1)
            pool.wait_ge(proj_ready, TT)
            fill(v_bd[:, :, :, :], 0.0, vbd_zero)
            fill(p1[:, :, :, :, N:32], 0.0, vbd_zero)
            fill(ob[CB:CB + 1, :], 1.0, vbd_zero)
            fill(hwT[:, :], 0.0, vbd_zero)
            fill(lam[:, :, :, :], 1.0, vbd_zero)
            pool.wait_ge(wqk_cast, 2)
            pool.tensor_tensor(wqk_lo[:, :], wqk1a, wqk_hi[:, :].bitcast(F32), ALU.subtract).then_inc(wqk_split, 1)
            pool.wait_ge(wqk_split, 1)
            pool.tensor_tensor(wqk_tail[CB:128, :], wqk1b, wqk_tail[0:CB, :].bitcast(F32), ALU.subtract).then_inc(wqk_split, 1)
            pool.wait_ge(wqk_split, 2)
            pool.wait_ge(hid_ready, NCH)
            fill(qT[:, :, T:T + 8], 0.0, vbd_zero)
            rsqrt(1)
            pool.wait_ge(xb_done, 6)
            pool.tensor_copy(dense(xt_hi[CB:128, :]), unpadded(xpb[0:CB, :])).then_inc(x_twice, 1)
            pool.wait_ge(x_twice, 3)
            rsqrt(2)
            rsqrt(3)

        PREP = 11

        PROJ_BANKS = [6, 7, 6, 7]

        def last_group(t):
            return (128 * t + rows(t) - 1) // GT

        @block.tensor
        def _(pe):
            def keep_busy(bank, n, width=128):
                for _ in range(n):
                    pe.matmul(ps[:, bank, 0:width], ident, w1a[:, 0:width] if width > 128 else ident, start=True, stop=True)

            def to_channels(layer, first):
                spare = {0: None, 1: [7] * 4, 2: [7, 7, 7, 0], 3: [4] * 4}[layer]
                for t in range(TT):
                    n = rows(t)
                    at = 128 * (t % 4)
                    if layer and t % 2 == 0:
                        keep_busy(spare[t // 2], 2)
                    if layer:
                        pe.wait_ge(x_ready, (layer - 1) * TT + t + 1)
                    else:
                        pe.wait_ge([x0_dve, x0_act][(t // 2) % 2], t // 4 + 1)
                    pe.transpose(ps[:, first + t // 4, at:at + n], x_tok[0:n, t, 0:CA], ident[0:n, 0:n])
                    pe.transpose(ps[0:CB, first + 2 + t // 4, at:at + n], x_tok[0:n, t, CA:C], ident[0:n, 0:n]).then_inc(xT_ready, 1)

            def padded(x, g):
                return x[:, 128 * g:128 * g + 128]

            def half_of(x, n):
                return view(x[:, 32 * (B // 2) * n:32 * (B // 2) * n + 1], [[32, B // 2], [1, N]])

            for k in range(KCH):
                pe.wait_ge(patch_in[k], 16)
                for t in range(TT):
                    pe.matmul(tok_bank(0, t), pat[:, k, 128 * t:128 * t + rows(t)], pat[:, k, T:],
                              start=(k == 0 and t % 2 == 0), stop=False, skip_group_check=True)
            pe.wait_ge(const_in, 32)
            for t in range(TT):
                pe.matmul(tok_bank(0, t), sel[:, 128 * t:128 * t + rows(t)], posb,
                          start=False, stop=True, skip_group_check=True).then_inc(conv_done, 1)
            to_channels(0, 4)

            pe.wait_ge(w0_in, 32)
            pe.wait_ge(pool_set, PREP)
            for g in range(G):
                half = 1 if GT * (g + 1) <= 512 else 2
                pe.wait_ge(xa_done, half)
                pe.wait_ge(xb_done, half)
                if g >= 4:
                    pe.wait_ge([kv_act, kv_dve][g % 2], (g - 4) // 2 + 1)
                pe.matmul(ps[:, g % 4, 0:KV], padded(xpa, g), wkv0a[:, :], start=True, stop=False)
                pe.matmul(ps[:, g % 4, 0:KV], padded(xpb[0:CB], g), wkv0b[:, :], start=False, stop=True).then_inc(kv_ready, 1)
            for n in range(2):
                out = ps[:, 4 + n, 0:HALF]
                pe.matmul(out, wq0a, half_of(xpa, n), start=True, stop=False)
                pe.matmul(out, wq0b, half_of(xpb[0:CB], n), start=False, stop=True).then_inc(q0_ready, 1)

            def turn_a0(r):
                pe.wait_ge(a0_ready, r + 1)
                wait(pe, a0T_done, r - 1)
                for j in range(4):
                    mm = pe.transpose(ps[:, 4 + r % 2, 128 * j:128 * j + 128],
                                      a0[:, r % 2, j // 2, 2 * (j % 2):2 * (j % 2) + 2, :, :], ident)
                mm.then_inc(a0T_ready, 1)

            def keys_by_values(r):
                wait(pe, s0_act, r)
                wait(pe, s0_dve, r)
                for gg in range(2):
                    g = 2 * r + gg
                    for a in range(2):
                        mm = pe.matmul(ps[:, 2 * gg + a, 0:IG * CH], k0[:, g, 128 * a:128 * a + 128],
                                       v0[:, g, :, CH * a:CH * a + CH], start=True, stop=True)
                mm.then_inc(s0_ready, 1)

            def by_queries(r):
                pe.wait_ge(a0T_done, r + 1)
                if r == 0:
                    pe.wait_ge(q0_act, 1)
                    pe.wait_ge(q0_dve, 1)
                if r == 2:
                    pe.wait_ge(s0_act, 4)
                    pe.wait_ge(s0_dve, 4)
                for j in range(4):
                    mm = pe.matmul(ps[:, O0_BANK[r // 2] + r % 2, 4 * N * j:4 * N * j + 4 * N], a0T[:, 4 * r + j, :],
                                   q0[:, :, :, 4 * r + j, :].rearrange("p a b t -> p (a b) t"), start=True, stop=True)
                if r % 2:
                    mm.then_inc(o0_ready, 1)

            pe.wait_ge(kv_act, 4)
            pe.wait_ge(kv_dve, 4)
            for step in range(6):
                if step < 4:
                    keys_by_values(step)
                if step >= 3:
                    by_queries(step - 3)
                if 2 <= step:
                    turn_a0(step - 2)
            keep_busy(2, 6)
            by_queries(3)
            keep_busy(2, 6)
            for t in range(TT):
                if 128 * t + rows(t) <= HALF:
                    pe.wait_ge(o0_act, 1)
                    pe.wait_ge(o0_dve, 1)
                else:
                    pe.wait_ge(o0_act, 2)
                    pe.wait_ge(o0_dve, 2)
                n = rows(t)
                for s in range(2):
                    pe.matmul(tok_bank(2, t), view(o0[:, 256 * t + s:256 * t + s + 1], [[2, n]]), wp0[:, s, :], start=(s == 0), stop=False)
                pe.matmul(tok_bank(2, t), xb[CB:CB + 1, 0:n], bp0, start=False, stop=True).then_inc(proj_ready, 1)

            to_channels(1, 0)

            pe.wait_ge(summed, 4)
            for t in range(TT):
                if t in (0, 4):
                    pe.wait_ge(xa_done, 3 if t == 0 else 4)
                    pe.wait_ge(xb_done, 3 if t == 0 else 4)
                cols = slice(128 * t, 128 * t + 128)
                pe.matmul(ps[:, 4, E * t:E * t + E], xa[:, cols], wg0a, start=True, stop=False)
                mm = pe.matmul(ps[:, 4, E * t:E * t + E], xb[0:CB, cols], wg0b, start=False, stop=True)
            mm.then_inc(logits_ready, 1)

            def split_product(banks, w_hi, w_lo, w_tail):
                halves = [(ps[:, banks + n, 0:HALF], slice(n * HALF, (n + 1) * HALF)) for n in range(2)]
                for out, tok in halves:
                    pe.matmul(out, w_hi, x_hi[:, tok], start=True, stop=False)
                    pe.matmul(out, w_hi, x_lo[:, tok], start=False, stop=False)
                    pe.matmul(out, w_lo, x_hi[:, tok], start=False, stop=False)
                    pe.matmul(out, w_tail, xt_hi[:, tok], start=False, stop=False)
                for out, tok in halves:
                    mm = pe.matmul(out, w_tail[0:CB], xt_lo[:, tok], start=False, stop=True)
                return mm

            def expert_in(c):
                e, k = c // HC, c % HC
                if k == 0:
                    pe.wait_ge(w1_split if e else first_split, 2 * e if e else 4)
                if c == 0:
                    pe.wait_ge(x_split, 4)
                    pe.wait_ge(x_twice, 2)
                if k == 0 and e:
                    pe.wait_ge(bc_act, e + 1)
                else:
                    wait(pe, hid_ready, c if k == HC - 1 and e < E - 1 else c - 1)
                cols = slice(128 * k, 128 * k + 128)
                j = e % 2
                split_product(z_bank(c), w1_hi[:, j, cols], w1_lo[:, j, cols], w1_tail[:, j, cols]).then_inc(z_ready, 1)

            def expert_out(c):
                e, k = c // HC, c % HC
                j = e % 2
                pe.wait_ge(hid_split, c + 1)
                if k == 0:
                    wait(pe, w2_split, 2 * e)
                if c == 0:
                    pe.wait_ge(bc_act, 1)
                    pe.wait_ge(bc_dve, 1)
                first, last = c == 0, c == NCH - 1
                toks = [slice(n * HALF, (n + 1) * HALF) for n in range(2)]
                for n, tok in enumerate(toks):
                    h_hi, h_lo = hid_hi[:, c % HBUF, tok], hid_lo[:, c % HBUF, tok]
                    top = ps[:, 4 + n, 0:HALF]
                    pe.matmul(top, w2_hi[:, j, k, :], h_hi, start=first, stop=False, skip_group_check=True)
                    pe.matmul(top, w2_lo[:, j, k, :], h_hi, start=False, stop=False, skip_group_check=True)
                    pe.matmul(top, w2_hi[:, j, k, :], h_lo, start=False, stop=last, skip_group_check=True)
                    pe.matmul(ps[:, 6 + n, 0:HALF], w2_tail[:, j, k, :], h_hi, start=first, stop=False, skip_group_check=True)
                for n, tok in enumerate(toks):
                    mm = pe.matmul(ps[0:CB, 6 + n, 0:HALF], w2_tail[:, j, k, 0:CB], hid_lo[:, c % HBUF, tok],
                                   start=False, stop=last, skip_group_check=True)
                mm.then_inc(y_done, 1)

            expert_in(0)
            pe.wait_ge(gate_parts, 2)
            for t in range(TT):
                n = rows(t)
                mm = pe.transpose(ps[0:2 * E, 4 + t // 4, 128 * (t % 4):128 * (t % 4) + n], gate_hl[0:n, t, :], ident[0:n, 0:n])
            mm.then_inc(gT_ready, 1)
            expert_in(1)
            pe.wait_ge(gT_done, 1)
            pe.wait_ge(sel_ready, 1)

            def spread_gates(e, first):
                for n in range(2):
                    mm = pe.matmul(ps[:, first + n, 0:HALF], bc_sel[:, e, :], gatesT[:, n * HALF:(n + 1) * HALF], start=True, stop=True)
                mm.then_inc(bc_ready, 1)

            spread_gates(0, 4)
            for c in range(2, NCH):
                e, k = c // HC, c % HC
                if k == HC - 1 and e + 1 < E:
                    pe.wait_ge(hid_ready, c - 1)
                    spread_gates(e + 1, bc_bank(e + 1))
                expert_in(c)
                expert_out(c - 2)
            expert_out(NCH - 2)
            expert_out(NCH - 1)
            pe.wait_ge(yT_act, 2)
            pe.wait_ge(yT_dve, 2)
            for t in range(TT):
                cols = slice(128 * t, 128 * t + rows(t))
                out = tok_bank(0, t)
                pe.matmul(out, gatesT[:, cols].bitcast(F32), b2r, start=True, stop=False, skip_group_check=True)
                pe.matmul(out[:, 0:CA], yT[:, 0, cols], ident, start=False, stop=True, skip_group_check=True)
                pe.matmul(out[:, CA:C], yT[:, 1, cols], fold, start=False, stop=True, skip_group_check=True).then_inc(proj_ready, 1)

            def values(gs, terms, start, stop):
                for g in gs:
                    for n, (x, w) in enumerate(terms):
                        mm = pe.matmul(ps[:, 4 + g // 2, 256 * (g % 2):256 * (g % 2) + C], padded(x, g), w,
                                       start=(start and n == 0 and g % 2 == 0), stop=(stop and n == len(terms) - 1), skip_group_check=True)
                return mm

            def query_or_key(n_job, m, terms, start, stop):
                for n in range(2):
                    for j, (w, x) in enumerate(terms):
                        mm = pe.matmul(ps[0:m, 2 * (n_job % 2) + n, 0:HALF], w, half_of(x, n),
                                       start=(start and j == 0), stop=(stop and j == len(terms) - 1))
                return mm

            def attention(call, slots, wa, wb):
                pe.wait_ge(qk_act, QK_JOBS[call])
                pe.wait_ge(qk_dve, QK_JOBS[call])
                pe.wait_ge(v_act, call + 1)
                pe.wait_ge(v_dve, call + 1)

                def scores(g):
                    for bank, slot, row, stack in slots:
                        for i in range(IG):
                            tok = GT * g + N * i
                            keys = k_bd[row:row + 64, stack, :, tok:tok + N]
                            mm = pe.matmul(ps[32 * i:32 * i + 32, 2 * (g % 2) + bank, 4 * N * slot:4 * N * slot + 4 * N],
                                           qT[row:row + 64, stack, tok:tok + 32], keys, start=True, stop=True)
                    mm.then_inc(s1_ready, 1)

                def turn(g):
                    n = G * call + g
                    pe.wait_ge(p1_ready, n + 1)
                    if g >= 1:
                        pe.wait_ge(p1T_done, n)
                    for b in range(3):
                        mm = pe.transpose(ps[:, 4, 128 * b:128 * b + 128], p1[:, g % 2, b, :, :], ident[:, :])
                    mm.then_inc(p1T_ready, 1)

                def times_v(g):
                    n = G * call + g
                    pe.wait_ge(p1T_done, n + 1)
                    if g >= 1:
                        pe.wait_ge(o1_done, n)
                    for b in range(3):
                        for i in range(IG):
                            rr = 64 * (b % 2)
                            col = (128 if b == 2 else 0) + N * i
                            mm = pe.matmul(ps[rr:rr + 64, 5, col:col + N], v_bd[:, IG * g + i, b, :],
                                           p1T[:, g % 2, b, 32 * i:32 * i + N], start=True, stop=True)
                    mm.then_inc(o1_ready, 1)

                def project(t):
                    pe.wait_ge(o1_done, G * call + last_group(t) + 1)
                    if t >= 4 and t % 2 == 0:
                        pe.wait_ge(summed, PAIRS * (2 + call) + t // 2 - 1)
                    cols = slice(128 * t, 128 * t + rows(t))
                    out = ps[0:rows(t), PROJ_BANKS[t // 2], (t % 2) * C:(t % 2) * C + C]
                    pe.matmul(out, oa[:, cols], wa, start=True, stop=False)
                    pe.matmul(out, ob[:, cols], wb, start=False, stop=True).then_inc(proj_ready, 1)

                for step in range(G + 3):
                    if 2 <= step < G + 2:
                        pe.wait_ge(s1_shifted, G * call + step - 1)
                    if 0 < step < G + 2:
                        keep_busy(2 * (step % 2), 2, 384)
                    if step < G:
                        scores(step)
                    if 2 <= step <= G + 1:
                        turn(step - 2)
                    if step >= 3:
                        times_v(step - 3)
                    for t in range(TT):
                        if last_group(t) + 4 == step:
                            project(t)
                for t in range(TT):
                    if last_group(t) + 4 > G + 2:
                        project(t)

            QK_JOBS = [6, 9]
            to_channels(2, 4)
            pe.wait_ge(xa_done, 6)
            pe.wait_ge(xb_done, 6)
            pe.wait_ge(summed, 8)
            pe.wait_ge(wlate_in, 32)
            pe.wait_ge(vbd_zero, 6)
            values(range(G), [(xpa, wv1a), (xpb[0:CB], wv1b)], True, True).then_inc(v_ready, 1)
            pe.wait_ge(wqk_split, 2)
            pe.wait_ge(x_split, 6)
            pe.wait_ge(x_twice, 3)
            for n_job, (kind, stack) in enumerate(QK_ORDER):
                at = (2 * C if kind == "k" else 0) + 128 * stack
                cols = slice(at, at + 128)
                if n_job >= 2:
                    pe.wait_ge(qk_act, n_job - 1)
                    pe.wait_ge(qk_dve, n_job - 1)
                split_product(2 * (n_job % 2), wqk_hi[:, cols], wqk_lo[:, cols], wqk_tail[:, cols]).then_inc(qk_ready, 1)
            attention(0, [(0, 0, 0, 0), (1, 0, 64, 0), (0, 1, 0, 1), (1, 1, 64, 1), (0, 2, 0, 2), (1, 2, 64, 2)], wo1a, wo1b)

            to_channels(3, 0)
            pe.wait_ge(xa_done, 8)
            pe.wait_ge(xb_done, 8)
            pe.wait_ge(summed, 12)

            def at_group(g, c0, c1):
                return ps[:, 4 + g // 2, 256 * (g % 2) + c0:256 * (g % 2) + c1]

            for g in range(G):
                pe.matmul(at_group(g, 0, C + E), padded(xpa, g), wvg2a, start=(g % 2 == 0), stop=False, skip_group_check=True)
                mm = pe.matmul(at_group(g, C, C + E), padded(xpb[0:CB + 1], g), wg2b, start=False, stop=True, skip_group_check=True)
            mm.then_inc(logits_ready, 1)
            for n in range(2):
                pe.matmul(ps[:, 2 + n, 0:HALF], wa2a[:, :], half_of(xpa, n), start=True, stop=False)
                pe.matmul(ps[:, 2 + n, 0:HALF], wa2b[:, :], half_of(xpb[0:CB + 1], n), start=False, stop=True).then_inc(ha_ready, 1)
            jobs = [(0, 128), (CA, 128), (2 * CA, 128)]

            def first_term(n_job):
                c0, m = jobs[n_job]
                query_or_key(n_job, m, [(wqkva[:, c0:c0 + m], xpa)], True, False)

            def second_term(n_job):
                c0, m = jobs[n_job]
                query_or_key(n_job, m, [(wqkvb[:, c0:c0 + m], xpb)], False, False)

            def last_term(n_job):
                c0, m = jobs[n_job]
                query_or_key(n_job, m, [(wbm[:, c0:c0 + m], hwT)], False, True).then_inc(qk_ready, 1)


            first_term(0)
            pe.wait_ge(gates_ready, 2)
            pe.wait_ge(ha_done, 2)
            for g in range(G):
                mm = pe.transpose(ps[0:E, 2 + g // 4, 128 * (g % 4):128 * (g % 4) + 128], gates[:, g, :], ident)
            mm.then_inc(gT_ready, 1)
            pe.wait_ge(gT_done, 2)
            pe.wait_ge(gT_dve, 1)
            for n in range(2):
                pe.matmul(ps[:, 2 + n, 0:HALF], expert_rows, half_of(xpb[96:104], n), start=True, stop=True).then_inc(ce_ready, 1)
            wvb, wvm = wqkvb[:, 2 * C:], wbm[:, 2 * C:]
            second_term(0)
            values(range(G), [(xpb, wvb)], False, False)
            pe.wait_ge(hw_done, 2)
            last_term(0)
            values(range(G), [(hwT, wvm)], False, True).then_inc(v_ready, 1)
            for n_job in range(1, 3):
                if n_job >= 2:
                    pe.wait_ge(qk_act, 6 + n_job - 1)
                    pe.wait_ge(qk_dve, 6 + n_job - 1)
                first_term(n_job)
                second_term(n_job)
                last_term(n_job)
            attention(1, [(0, 0, 0, 0), (1, 0, 64, 0), (0, 1, 0, 1)], wp2a, wp2b)

        @block.scalar
        def _(act):
            def copy(out, in_):
                return act.activation(out, in_, ACT.Copy)

            def channels_out(layer, first):
                for j in range(2):
                    act.wait_ge(xT_ready, layer * TT + (4 if j == 0 else TT))
                    n = 512 if j == 0 else T - 512
                    outs = spread(xpa, ps[:, first + j, :], j) if layer != 1 else []
                    if layer == 1:
                        outs.append((xa[:, 512 * j:512 * j + n], ps[:, first + j, 0:n]))
                    for out, in_ in outs:
                        ins = copy(out, in_)
                    ins.then_inc(xa_done, 1)
                    if layer == 1:
                        copy(x_hi[:, 512 * j:512 * j + n], ps[:, first + j, 0:n]).then_inc(x_cast, 1)

            act.wait_ge(conv_done, 4)
            copy(x_tok[:, 2:4, :], ps[:, 1, 0:2 * C]).then_inc(x0_act, 1)
            act.wait_ge(conv_done, 7)
            copy(x_tok[0:rows(6), 6, :], ps[0:rows(6), 3, 0:C]).then_inc(x0_act, 1)
            act.wait_ge(pool_set, PREP)
            channels_out(0, 4)
            for g in range(0, G, 2):
                act.wait_ge(kv_ready, g + 1)
                copy(k0[:, g, :], ps[:, g % 4, 0:256])
                for i in range(IG):
                    quad = slice(32 * i, 32 * i + 32)
                    ins = copy(v0[quad, g, i, :], ps[quad, g % 4, 256:KV])
                ins.then_inc(kv_act, 1)
            act.wait_ge(q0_ready, 2)
            for quad in (0, 2):
                ins = copy(*queries_out(quad))
            ins.then_inc(q0_act, 1)

            def cast_w1(e):
                act.wait_ge(w1_in, 48 * (e + 1))
                wait(act, z_ready, HC * (e - 1))
                copy(w1_hi[:, e % 2, :], w1_raw[:, 0, :]).then_inc(w1_cast, 1)
                copy(w1_tail[:, e % 2, :], w1_raw[:, 1, :]).then_inc(w1_cast, 1)

            def cast_w2(e):
                act.wait_ge(w2_in, 16 * (e + 1))
                wait(act, y_done, HC * (e - 1))
                copy(w2_hi[:, e % 2], w2_raw[:, :, 0:CA]).then_inc(w2_cast, 1)
                copy(w2_tail[:, e % 2, :, 0:CB], w2_raw[:, :, CA:C]).then_inc(w2_cast, 1)

            cast_w1(0)
            cast_w2(0)

            def a0T_out(r):
                act.wait_ge(a0T_ready, r + 1)
                copy(a0T[:, 4 * r:4 * r + 4, :], ps[:, 4 + r % 2, :]).then_inc(a0T_done, 1)

            for r in range(4):
                act.wait_ge(s0_ready, r + 1)
                for h in (2, 3):
                    ins = copy(*heads_out(h, r))
                ins.then_inc(s0_act, 1)
                if r >= 2:
                    a0T_out(r - 2)
                act.wait_ge(s0_shifted, r + 1)
                act.activation(e0[:, r % 2], s0[:, r % 2], ACT.Exp, scale=D0 ** -0.5).then_inc(s0_exp, 1)
            for half in range(2):
                act.wait_ge(o0_ready, half + 1)
                for out, in_ in reorder(2, half) + reorder(3, half):
                    ins = copy(out, in_)
                ins.then_inc(o0_act, 1)
                if half == 0:
                    a0T_out(2)
                    a0T_out(3)

            channels_out(1, 0)
            def gate_exp(n, tiles):
                act.wait_ge(shift_ready, n + 1)
                act.activation(gate_w[:, 2, 0:tiles], gate_w[:, 1, 0:tiles], ACT.Exp).then_inc(gexp_ready, 1)
            gate_exp(0, TT)
            act.wait_ge(gT_ready, 1)
            copy(gatesT[:, 0:512], ps[0:2 * E, 4, 0:512])
            copy(gatesT[:, 512:T], ps[0:2 * E, 5, 0:T - 512]).then_inc(gT_done, 1)
            act.wait_ge(bc_ready, 1)
            copy(gate_bc[:, 0, 0:HALF], ps[:, 4, 0:HALF]).then_inc(bc_act, 1)
            act.wait_ge(wlate_in, 32)
            for c in range(NCH):
                if c == HC:
                    copy(wqk_hi[:, :], wqk1a).then_inc(wqk_cast, 1)
                    copy(wqk_tail[0:CB, :], wqk1b).then_inc(wqk_cast, 1)
                act.wait_ge(hid_ready, c + 1)
                wait(act, y_done, c - HBUF + 1)
                act.activation(hid_hi[:, c % HBUF, :], hid[:, c % 2, :], ACT.Relu).then_inc(hid_cast, 1)
                e, k = c // HC, c % HC
                if k == 1 and e + 1 < E:
                    cast_w1(e + 1)
                if k == 3 and e + 1 < E:
                    cast_w2(e + 1)
                if k == HC - 2 and e + 1 < E:
                    act.wait_ge(bc_ready, e + 2)
                    first = bc_bank(e + 1)
                    copy(gate_bc[:, (e + 1) % 2, :].rearrange("p (n t) -> p n t", n=2), ps[:, first:first + 2, 0:HALF]).then_inc(bc_act, 1)
            act.wait_ge(y_done, NCH)
            for n in range(2):
                copy(yT[:, 0, n * HALF:(n + 1) * HALF], ps[:, 4 + n, 0:HALF]).then_inc(yT_act, 1)

            act.wait_ge(wlate_in, 32)
            act.activation(lam_exp[:, :], lam_raw[:, :], ACT.Exp).then_inc(lam_ready, 1)
            channels_out(2, 4)
            act.wait_ge(xa_done, 6)
            copy(dense(x_hi[:, :]), unpadded(xpa)).then_inc(x_cast, 1)

            def attention(call, kinds, exps):
                def values_out():
                    act.wait_ge(v_ready, call + 1)
                    for i in (2, 3):
                        for h in range(HQ):
                            src = view(ps[32 * i:32 * i + 32, 4, 16 * h:16 * h + 1], [[256, G], [64, 3], [1, 16]])
                            dst = view(v_bd[32 * h:32 * h + 32, i, 0, 16 * h:16 * h + 1], [[IG * C, G], [64, 3], [1, 16]])
                            mm = copy(dst, src)
                    mm.then_inc(v_act, 1)

                for n_job, (kind, stack, m) in enumerate(kinds):
                    if n_job == call:
                        values_out()
                    act.wait_ge(qk_ready, (6 if call else 0) + n_job + 1)
                    src = ps[0:m, 2 * (n_job % 2) + 1, 0:HALF]
                    if kind == "kq":
                        copy(qT[0:m, stack, HALF:T], ps[m:2 * m, 2 * (n_job % 2) + 1, 0:HALF])
                    if kind == "q":
                        copy(qT[0:m, stack, HALF:T], src).then_inc(qk_act, 1)
                    else:
                        for h in range(HQ):
                            mm = act.activation(k_bd[0:m, stack, h, HALF:T], src, ACT.Copy, scale=head_mask1[0:m, h:h + 1])
                        mm.then_inc(qk_act, 1)

                def p1T_out(g):
                    act.wait_ge(p1T_ready, G * call + g + 1)
                    if g >= 2 or call:
                        act.wait_ge(o1_ready, G * call + g - 1)
                    copy(p1T[:, g % 2, :, :], ps[:, 4, 0:384]).then_inc(p1T_done, 1)

                def o_out(g):
                    act.wait_ge(o1_ready, G * call + g + 1)
                    copy(oa[:, GT * g:GT * g + GT], ps[:, 5, 0:GT])
                    copy(ob[0:CB, GT * g:GT * g + GT], ps[0:CB, 5, 128:128 + GT]).then_inc(o1_done, 1)

                for step in range(G + 3):
                    if step < G:
                        act.wait_ge(s1_shifted, G * call + step + 1)
                        act.activation(e1[:, step % 2, 0:exps], s1[:, step % 2, 0:exps], ACT.Exp, scale=D1 ** -0.5).then_inc(s1_exp, 1)
                    if 2 <= step <= G + 1:
                        p1T_out(step - 2)
                    if step >= 3:
                        o_out(step - 3)

            attention(0, [(x, s, 128) for x, s in QK_ORDER], 24)
            channels_out(3, 0)
            gate_exp(1, G)
            for n in range(2):
                act.wait_ge(ha_ready, n + 1)
                copy(adapted(n), ps[:, 2 + n, 0:HALF].rearrange("p (b n) -> p b n", n=N)).then_inc(ha_done, 1)
            act.wait_ge(gT_ready, 2)
            copy(xpb[96:104, 0:512], ps[0:E, 2, :]).then_inc(gT_done, 1)
            attention(1, [("q", 0, 128), ("k", 0, 128), ("kq", 1, 64)], 12)

        @block.vector
        def _(dve):
            links = [0]

            def link(ins):
                links[0] += 1
                ins.then_inc(dve_chain, 1)
                dve.wait_ge(dve_chain, links[0])

            def over(ap, n):
                return bass.AP(tensor=ap.tensor, offset=ap.offset, ap=[list(d) for d in ap.ap] + [[0, n]])

            dve.wait_ge(conv_done, 2)
            dve.tensor_copy(x_tok[:, 0:2, :], ps[:, 0, 0:2 * C]).then_inc(x0_dve, 1)
            dve.wait_ge(conv_done, 6)
            dve.tensor_copy(x_tok[:, 4:6, :], ps[:, 2, 0:2 * C]).then_inc(x0_dve, 1)
            def channels_out(layer, first):
                for j in range(2):
                    dve.wait_ge(xT_ready, layer * TT + (4 if j == 0 else TT))
                    n = 512 if j == 0 else T - 512
                    outs = spread(xpb[0:CB], ps[0:CB, first + 2 + j, :], j)
                    for out, in_ in outs:
                        ins = dve.tensor_copy(out, in_)
                    ins.then_inc(xb_done, 1)
            dve.wait_ge(pool_set, PREP)
            channels_out(0, 4)
            for g in range(1, G, 2):
                dve.wait_ge(kv_ready, g + 1)
                dve.tensor_copy(k0[:, g, :], ps[:, g % 4, 0:256])
                for i in range(IG):
                    quad = slice(32 * i, 32 * i + 32)
                    ins = dve.tensor_copy(v0[quad, g, i, :], ps[quad, g % 4, 256:KV])
                ins.then_inc(kv_dve, 1)
            dve.wait_ge(q0_ready, 2)
            for quad in (1, 3):
                ins = dve.tensor_copy(*queries_out(quad))
            ins.then_inc(q0_dve, 1)

            def shift0(r):
                dve.wait_ge(s0_ready, r + 1)
                for h in (0, 1):
                    ins = dve.tensor_copy(*heads_out(h, r))
                ins.then_inc(s0_dve, 1)
                dve.wait_ge(s0_dve, r + 1)
                dve.wait_ge(s0_act, r + 1)
                link(dve.tensor_reduce(st0[:, 0, :], s0[:, r % 2], AX.X, ALU.max))
                dve.tensor_tensor(s0[:, r % 2], s0[:, r % 2], over(st0[:, 0, :], D0), ALU.subtract).then_inc(s0_shifted, 1)

            def norm0(r):
                dve.wait_ge(s0_exp, r + 1)
                link(dve.tensor_reduce(st0[:, 1, :], e0[:, r % 2], AX.X, ALU.add))
                link(dve.reciprocal(st0[:, 2, :], st0[:, 1, :]))
                wait(dve, a0T_ready, r - 1)
                for gg in range(2):
                    part = e0[:, r % 2].rearrange("p (g a i) e -> p g i a e", i=IG, g=2)[:, gg]
                    inv = st0[:, 2, :].rearrange("p (g a i) -> p g i a", i=IG, g=2)[:, gg]
                    ins = dve.tensor_tensor(a0[:, r % 2, gg, :, :, 0:D0], part, over(inv, D0), ALU.mult)
                ins.then_inc(a0_ready, 1)

            for r in range(5):
                if r < 4:
                    shift0(r)
                if r >= 1:
                    norm0(r - 1)
            def split_w1(e):
                dve.wait_ge(w1_cast, 2 * (e + 1))
                j = e % 2
                dve.tensor_tensor(w1_lo[:, j, :], w1_raw[:, 0, :], w1_hi[:, j, :].bitcast(F32), ALU.subtract).then_inc(w1_split, 1)
                low = w1_tail[CB:128, j, :]
                dve.tensor_tensor(low, w1_raw[CB:128, 1, :], low.bitcast(F32), ALU.subtract).then_inc(w1_split, 1)

            def split_w2(e):
                dve.wait_ge(w2_cast, 2 * (e + 1))
                j = e % 2
                dve.tensor_tensor(w2_lo[:, j], w2_raw[:, :, 0:CA], w2_hi[:, j].bitcast(F32), ALU.subtract).then_inc(w2_split, 1)
                dve.tensor_tensor(w2_tail[:, j, :, CB:2 * CB], w2_raw[:, :, CA:C], w2_tail[:, j, :, 0:CB].bitcast(F32), ALU.subtract).then_inc(w2_split, 1)

            for half in range(2):
                dve.wait_ge(o0_ready, half + 1)
                for out, in_ in reorder(0, half) + reorder(1, half):
                    ins = dve.tensor_copy(out, in_)
                ins.then_inc(o0_dve, 1)

            def stats_of(layer, pair, first, res):
                t0, t1 = 2 * pair, min(2 * pair + 2, TT)
                n = rows(t0)
                dve.wait_ge(proj_ready, layer * TT + t1)
                dve.tensor_tensor(h_tok[0:n, t0:t1, :], ps[0:n, first, 0:(t1 - t0) * C].rearrange("p (t c) -> p t c", c=C),
                                  res[0:n, t0:t1, :], ALU.add).then_inc(summed, 1)
                dve.wait_ge(summed, PAIRS * layer + pair + 1)
                for t in range(t0, t1):
                    ins = dve.bn_stats(stats[0:n, t, :], h_tok[0:n, t, :])
                link(ins)
                for t in range(t0, t1):
                    ins = dve.bn_aggr(mv[0:n, t, :], stats[0:n, t, :])
                link(ins)
                dve.tensor_scalar(veps[:, t0:t1], mv[:, t0:t1, 1], EPS, None, ALU.add).then_inc(veps_ready, 1)

            def normalized(layer, pair):
                dve.wait_ge(rstd_ready, PAIRS * layer + pair + 1)
                for t in range(2 * pair, min(2 * pair + 2, TT)):
                    n = rows(t)
                    dve.tensor_scalar(x_tok[0:n, t, :], h_tok[0:n, t, :], mv[0:n, t, 0:1], rstd[0:n, t:t + 1],
                                      ALU.subtract, ALU.mult).then_inc(x_ready, 1)

            def layernorm(layer, banks, res):
                for pair in range(PAIRS):
                    stats_of(layer, pair, banks[pair], res)
                    if pair >= 1:
                        normalized(layer, pair - 1)
                normalized(layer, PAIRS - 1)

            layernorm(0, [2, 3, 4, 5], x_tok)

            halves = [slice(0, 512), slice(512, T)]
            for j, cols in enumerate(halves):
                dve.wait_ge(xT_ready, TT + (4 if j == 0 else TT))
                dve.tensor_copy(xb[0:CB, cols], ps[0:CB, 2 + j, 0:cols.stop - cols.start]).then_inc(xb_done, 1)
            for j, cols in enumerate(halves):
                tail = ps[0:CB, 2 + j, 0:cols.stop - cols.start]
                link(dve.tensor_copy(xt_hi[0:CB, cols], tail))
                dve.tensor_tensor(xt_lo[:, cols], tail, xt_hi[0:CB, cols].bitcast(F32), ALU.subtract).then_inc(x_split, 1)
            for j, cols in enumerate(halves):
                dve.wait_ge(x_cast, 1 + j)
                dve.tensor_tensor(x_lo[:, cols], ps[:, j, 0:cols.stop - cols.start], x_hi[:, cols].bitcast(F32), ALU.subtract).then_inc(x_split, 1)

            def gating(n, factor, src):
                tiles = src.ap[-2][1] if len(src.ap) == 3 else src.ap[1][1] * src.ap[2][1]
                W = lambda k: gate_w[:, k, 0:tiles, :]
                S = lambda k: gate_s[:, k, 0:tiles]
                grid = view(iota8[:, 0:1], [[0, tiles], [1, E]])
                dve.wait_ge(logits_ready, n + 1)
                dve.tensor_copy(W(0), src).then_inc(logits_read, 1)
                dve.wait_ge(logits_read, n + 1)
                link(dve.tensor_reduce(S(0), W(0), AX.X, ALU.max))
                dve.tensor_tensor(W(1), W(0), over(S(0), E), ALU.subtract).then_inc(shift_ready, 1)
                for pick in range(2):
                    src, top, hot = W(0) if pick == 0 else W(5), S(pick), W(3 + pick)
                    if pick:
                        link(dve.scalar_tensor_tensor(W(5), W(3), -3.0e38, W(0), ALU.mult, ALU.add))
                        link(dve.tensor_reduce(S(1), W(5), AX.X, ALU.max))
                    link(dve.tensor_tensor(W(6), src, over(top, E), ALU.is_equal))
                    link(dve.tensor_tensor(W(7), W(6), grid, ALU.mult))
                    link(dve.tensor_reduce(S(2 + pick), W(7), AX.X, ALU.min))
                    link(dve.tensor_tensor(hot, grid, over(S(2 + pick), E), ALU.is_equal))
                link(dve.tensor_tensor(W(6), W(3), W(4), ALU.add))
                dve.wait_ge(gexp_ready, n + 1)
                link(dve.tensor_reduce(S(4), W(2), AX.X, ALU.add))
                link(dve.reciprocal(S(5), S(4)))
                link(dve.tensor_tensor(W(7), W(2), over(S(5), E), ALU.mult))
                dve.scalar_tensor_tensor(gates[:, 0:tiles, :], W(7), factor, W(6), ALU.mult, ALU.mult).then_inc(gates_ready, 1)

            dve.tensor_copy(bc_sel[:, :, :], over(expert_sel, 128)).then_inc(sel_ready, 1)
            gating(0, 1.0, ps[:, 4, 0:TT * E].rearrange("p (t e) -> p t e", e=E))
            dve.wait_ge(gates_ready, 1)
            parts = gate_hl[:, :, :].bitcast(F32R)
            dve.tensor_copy(parts[:, :, 0:E], gates[:, 0:TT, :]).then_inc(gate_parts, 1)
            dve.wait_ge(gate_parts, 1)
            dve.tensor_tensor(parts[:, :, E:2 * E], gates[:, 0:TT, :], gate_hl[:, :, 0:E], ALU.subtract).then_inc(gate_parts, 1)
            def weigh(c):
                dve.wait_ge(z_ready, c + 1)
                if c % HC == 0:
                    dve.wait_ge(bc_act, c // HC + 1)
                wait(dve, hid_cast, c - 1)
                wait(dve, hid_split, c - 1)
                gate = gate_bc[:, c // HC % 2, :].rearrange("p (n t) -> p n t", n=2)
                dve.scalar_tensor_tensor(hid[:, c % 2, :].rearrange("p (n t) -> p n t", n=2), ps[:, z_bank(c):z_bank(c) + 2, 0:HALF],
                                         b1c[:, c:c + 1], gate, ALU.add, ALU.mult).then_inc(hid_ready, 1)

            def split_hid(c):
                dve.wait_ge(hid_cast, c + 1)
                dve.scalar_tensor_tensor(hid_lo[:, c % HBUF, :], hid[:, c % 2, :], 0.0, hid_hi[:, c % HBUF, :].bitcast(F32),
                                         ALU.max, ALU.subtract).then_inc(hid_split, 1)

            dve.wait_ge(bc_ready, 1)
            dve.tensor_copy(gate_bc[:, 0, HALF:T], ps[:, 5, 0:HALF]).then_inc(bc_dve, 1)
            dve.wait_ge(bc_dve, 1)
            weigh(0)
            for c in range(NCH):
                e, k = c // HC, c % HC
                if c + 1 < NCH:
                    weigh(c + 1)
                split_hid(c)
                if k == 2 and e + 1 < E:
                    split_w1(e + 1)
                if k == 4 and e + 1 < E:
                    split_w2(e + 1)
            dve.wait_ge(y_done, NCH)
            for n in range(2):
                dve.tensor_copy(yT[:, 1, n * HALF:(n + 1) * HALF], ps[:, 6 + n, 0:HALF]).then_inc(yT_dve, 1)
            layernorm(1, [0, 1, 2, 3], x_tok)
            channels_out(2, 4)
            dve.wait_ge(xb_done, 6)
            link(dve.tensor_copy(dense(xt_hi[0:CB, :]), unpadded(xpb[0:CB, :])))
            dve.tensor_tensor(dense(xt_lo[:, :]), unpadded(xpb[0:CB, :]), dense(xt_hi[0:CB, :].bitcast(F32)), ALU.subtract).then_inc(x_split, 1)
            dve.wait_ge(x_cast, 3)
            dve.tensor_tensor(dense(x_lo[:, :]), unpadded(xpa), dense(x_hi[:, :].bitcast(F32)), ALU.subtract).then_inc(x_split, 1)

            dve.wait_ge(lam_ready, 1)
            dve.wait_ge(vbd_zero, 6)
            for bank, slot, h in ((0, 1, 0), (1, 1, 4), (1, 2, 8)):
                link(dve.tensor_scalar(lam[:, bank, slot, :], lam_exp[:, h:h + HQ], -1.0, None, ALU.mult))

            def attention(call, kinds, two_sets):
                def values_out():
                    dve.wait_ge(v_ready, call + 1)
                    for i in (0, 1):
                        for h in range(HQ):
                            src = view(ps[32 * i:32 * i + 32, 4, 16 * h:16 * h + 1], [[256, G], [64, 3], [1, 16]])
                            dst = view(v_bd[32 * h:32 * h + 32, i, 0, 16 * h:16 * h + 1], [[IG * C, G], [64, 3], [1, 16]])
                            ins = dve.tensor_copy(dst, src)
                    ins.then_inc(v_dve, 1)

                for n_job, (kind, stack, m) in enumerate(kinds):
                    if n_job == call:
                        values_out()
                    dve.wait_ge(qk_ready, (6 if call else 0) + n_job + 1)
                    src = ps[0:m, 2 * (n_job % 2), 0:HALF]
                    if kind == "kq":
                        dve.tensor_copy(qT[0:m, stack, 0:HALF], ps[m:2 * m, 2 * (n_job % 2), 0:HALF])
                    if kind == "q":
                        dve.tensor_copy(qT[0:m, stack, 0:HALF], src).then_inc(qk_dve, 1)
                    else:
                        dve.tensor_tensor(k_bd[0:m, stack, :, 0:HALF], view(src, [[0, HQ], [1, HALF]]),
                                          over(head_mask1[0:m, :], HALF), ALU.mult).then_inc(qk_dve, 1)

                def shift(g):
                    n = G * call + g
                    dve.wait_ge(s1_ready, n + 1)
                    first = 2 * (g % 2)
                    if two_sets:
                        parts = [(0, 24, view(ps[:, first, 0:1], [[512, 2], [N, 12], [1, N]]))]
                    else:
                        parts = [(0, 8, view(ps[:, first, 0:1], [[N, 8], [1, N]])), (8, 12, view(ps[:, first + 1, 0:1], [[N, 4], [1, N]]))]
                    for a, b, src in parts:
                        top = st1[:, g % 2, 0, a:b]
                        s = s1[:, g % 2, a:b, :]
                        if two_sets:
                            top2 = top.rearrange("p (a b) -> p a b", a=2)
                            s = s.rearrange("p (a b) m -> p a b m", a=2)
                        else:
                            top2 = top
                        link(dve.tensor_reduce(top2, src, AX.X, ALU.max))
                        ins = dve.tensor_tensor(s, src, over(top2, N), ALU.subtract)
                    ins.then_inc(s1_shifted, 1)

                def norm(g):
                    n = G * call + g
                    k = 24 if two_sets else 12
                    dve.wait_ge(s1_exp, n + 1)
                    e = e1[:, g % 2, 0:k, :]
                    total, inv, coef = (st1[:, g % 2, j, 0:k] for j in (1, 2, 3))
                    link(dve.tensor_reduce(total, e, AX.X, ALU.add))
                    link(dve.reciprocal(inv, total))
                    if g >= 2 or call:
                        dve.wait_ge(p1T_ready, n - 1)
                    p = p1[:, g % 2]
                    if two_sets:
                        link(dve.tensor_tensor(coef, inv, lam[:, :, :, :].rearrange("p a b c -> p (a b c)"), ALU.mult))
                        link(dve.tensor_tensor(e, e, over(coef, N), ALU.mult))
                        blk = e.rearrange("p (a b c) m -> p a b c m", a=2, b=3)
                        dve.tensor_tensor(p[:, 0:2, :, 0:N], blk[:, :, 0], blk[:, :, 1], ALU.add)
                        dve.tensor_tensor(p[:, 2, :, 0:N], blk[:, 0, 2], blk[:, 1, 2], ALU.add).then_inc(p1_ready, 1)
                    else:
                        dve.tensor_tensor(view(p[:, 0, 0, 0:1], [[256, 2], [32, HQ], [1, N]]),
                                          e[:, 0:8].rearrange("p (a b) m -> p a b m", a=2),
                                          over(inv[:, 0:8].rearrange("p (a b) -> p a b", a=2), N), ALU.mult)
                        dve.tensor_tensor(p[:, 1, :, 0:N], e[:, 8:12], over(inv[:, 8:12], N), ALU.mult).then_inc(p1_ready, 1)

                for step in range(G + 1):
                    if step < G:
                        shift(step)
                    if step >= 1:
                        norm(step - 1)

            attention(0, [(x, s, 128) for x, s in QK_ORDER], True)
            layernorm(2, PROJ_BANKS, x_tok)
            channels_out(3, 0)
            gating(1, ADAPT, view(ps[:, 4, C:C + 1], [[256, G], [1, E]]))
            dve.wait_ge(gT_ready, 2)
            dve.tensor_copy(xpb[96:104, 512:1024], ps[0:E, 3, :]).then_inc(gT_dve, 1)
            for n in range(2):
                dve.wait_ge(ha_done, n + 1)
                dve.wait_ge(ce_ready, n + 1)
                dve.tensor_tensor(adapted(n), adapted(n), ps[:, 2 + n, 0:HALF].rearrange("p (b n) -> p b n", n=N), ALU.mult).then_inc(hw_done, 1)
            attention(1, [("q", 0, 128), ("k", 0, 128), ("kq", 1, 64)], False)
            layernorm(3, PROJ_BANKS, x_tok)


def kernel(**inputs):
    import numpy as np
    import concourse.bacc as bacc
    from concourse.bass_utils import run_bass_kernel_spmd as run

    a = {k: np.asarray(v) for k, v in inputs.items()}
    crop = NB * PATCH
    x = a["x"][:, :, :crop, :crop].reshape(B, CIN, NB, PATCH, NB, PATCH)
    tok = np.arange(T)
    row = np.arange(128)
    at = np.arange(NB) * SIDE // NB
    pos = a["L0_tok_pos_table"].reshape(SIDE, SIDE, C)[at][:, at].reshape(N, C)

    def stacked(w):
        w = w.reshape(C, 2, C)
        return np.concatenate([w[:, 0, :128], w[:, 1, :128], w[:, 0, 128:], w[:, 1, 128:]], axis=1)

    def cut(w):
        return np.concatenate([w[..., :CA], w[..., C:C + CA], w[..., C + CA:2 * C], w[..., CA:C], w[..., 2 * C:]], axis=-1)

    def pack(rows, cols, parts):
        out = np.zeros((rows, sum(w for _, w in cols)), np.float32)
        c = 0
        for name, width in cols:
            for r, v in parts[name]:
                out[r:r + v.shape[0], c:c + width] = v
            c += width
        return out

    wq0 = np.zeros((C, 2, 2, 32), np.float32)
    wq0[:, :, :, :D0] = a["L0_attn_Wq"].reshape(C, 1, 2, D0)
    wk0 = np.zeros((C, H0, 32), np.float32)
    wk0[:, :, :D0] = a["L0_attn_Wkv"][:, :C].reshape(C, H0, D0)
    wp0 = np.zeros((4, 32, 2, C), np.float32)
    wp0[:, :D0] = a["L0_attn_Wproj"].reshape(2, 4, D0, C).transpose(1, 2, 0, 3)
    full = {
        "wkv0": np.concatenate([wk0.reshape(C, 256), a["L0_attn_Wkv"][:, C:]], axis=1), "wq0": wq0.reshape(C, 128), "wg0": a["L0_ffn_Wg"],
        "wq1": stacked(a["L1_attn_Wq"]), "wk1": stacked(a["L1_attn_Wk"]), "wv1": a["L1_attn_Wv"],
        "wo1": a["L1_attn_Wo"], "wg2": a["L1_ffn_Wg"].T, "wa2": a["L1_ffn_A"].reshape(E * R, C).T,
        "wqkv": cut(a["L1_ffn_Wqkv"].T), "wp2": a["L1_ffn_Wproj"].T,
    }
    bias = {"wo1": a["L1_attn_bo"], "wg2": a["L1_ffn_bg"], "wa2": a["L1_ffn_ba"].reshape(-1),
            "wqkv": cut(a["L1_ffn_bqkv"]), "wp2": a["L1_ffn_bproj"]}
    top = {k: [(0, v[:CA])] for k, v in full.items()}
    low = {k: [(0, v[CA:])] + ([(CB, bias[k][None])] if k in bias else []) for k, v in full.items()}
    top["wp0"] = [(0, wp0.reshape(128, 2 * C))]
    top["b1c"] = [(0, a["L0_ffn_b1"].reshape(NCH, 128).T)]
    top["lam"] = [(0, np.broadcast_to(a["L1_attn_lambda_p"].reshape(1, H1), (128, H1)))]
    top["wbm"] = [(0, cut(a["L1_ffn_Bm"].transpose(0, 2, 1).reshape(E * R, 3 * C)))]
    low["bp0"] = [(CB, a["L0_attn_bproj"][None])]
    low["b2"] = [(0, a["L0_ffn_b2"]), (E, a["L0_ffn_b2"])]
    low["wqkv"].append((96, cut(a["L1_ffn_bb"])))
    consts = {
        "ident": [(0, np.eye(128))],
        "mask1": [(0, row[:, None] % 64 // D1 == np.arange(HQ)[None, :])],
        "expert_rows": [(96, np.arange(E)[:, None] == row[None, :] // R)],
        "expert_sel": [(0, np.arange(2 * E)[:, None] % E == np.arange(E)[None, :])],
        "fold": [(0, row[:, None] % CB == np.arange(CB)[None, :])],
        "iota8": [(0, np.tile(np.arange(E) - E, (128, 1)))],
    }
    sel = np.concatenate([np.arange(N)[:, None] == tok[None, :] % N, np.ones((1, T), bool)]).astype(np.float32)
    arrays = {
        "pat": np.concatenate([x.transpose(1, 3, 5, 0, 2, 4).reshape(KP, T),
                               a["L0_tok_conv_w"].reshape(C, KP).T], axis=1),
        "pos_sel": np.concatenate([np.concatenate([pos, a["L0_tok_conv_b"][None]]), sel], axis=1),
        "consts": pack(128, CONSTS, consts),
        "w0a": pack(128, W0A, top), "w0b": pack(CB + 1, W0B, low),
        "w1a": pack(128, W1A, top), "w1b": pack(104, W1B, low),
        "w1": a["L0_ffn_W1"], "w2": a["L0_ffn_W2"],
    }
    nc = bacc.Bacc("TRN2", target_bir_lowering=False, num_devices=1)
    io, feed = {}, {}
    for name, v in arrays.items():
        feed[f"in_{name}"] = np.ascontiguousarray(v)
        io[name] = nc.dram_tensor(f"in_{name}", v.shape, F32, kind="ExternalInput").ap()
    io["out"] = nc.dram_tensor("out", (T, C), F32, kind="ExternalOutput").ap()
    build(nc, io)
    r = run(nc, [feed], core_ids=[0])
    return r.results[0]["out"].reshape(B, N, C)
```
